# Optimizing a Trainium2 kernel written in Bass

```python
import numpy as np
import jax
import jax.numpy as jnp

def _softmax(x, axis=-1):
    return jax.nn.softmax(x, axis=axis)

def _gelu(x):
    return jax.nn.gelu(x, approximate=True)

def _silu(x):
    return jax.nn.silu(x)

def _sigmoid(x):
    return jax.nn.sigmoid(x)

def _layernorm(x, axis=-1, eps=1e-05):
    m = jnp.mean(x, axis=axis, keepdims=True)
    v = jnp.var(x, axis=axis, keepdims=True)
    return (x - m) / jnp.sqrt(v + eps)

def _scatter_add(tgt, idx, src, axis=0):
    return tgt.at[idx].add(src)

def _segment_sum(src, seg, n):
    return jax.ops.segment_sum(src, seg, n)
kernel_name = 'mk_gps_d1_gnn_r8_4dfa1a'

def setup_inputs(seed: int=0):
    np.random.seed(seed)
    _w = jnp.asarray

    def _rec_inputs():
        import jax
        import jax.numpy as jnp
        _gk = jax.random.key(seed)
        x = -0.000125 + 0.9999 * jax.random.normal(jax.random.fold_in(_gk, 1), (8192, 512), jnp.float32)
        src = jax.random.randint(jax.random.fold_in(_gk, 2), (131072,), 0, 8192, jnp.int32)
        dst = jax.random.randint(jax.random.fold_in(_gk, 3), (131072,), 0, 8192, jnp.int32)
        _o = jnp.argsort(dst, stable=True)
        src = src[_o]
        dst = dst[_o]
        edge_weight = jax.random.uniform(jax.random.fold_in(_gk, 12), (131072,), jnp.float32, 0.0, 0.999998)
        return (x, src, dst, edge_weight)
    x, src, dst, edge_weight = _rec_inputs()

    def _L0_gnn_setup():
        import jax, jax.numpy as jnp
        import numpy as np
        N_NODES = 8192
        N_EDGES = 65536
        FEAT_DIM = 512
        EMBED_DIM = 512
        key = jax.random.key(seed)
        k1, k2, k3, k4, k5 = jax.random.split(key, 5)
        x = jax.random.normal(k1, (N_NODES, FEAT_DIM), dtype=jnp.float32)
        limit = float(np.sqrt(6.0 / (EMBED_DIM + FEAT_DIM)))
        weight = jax.random.uniform(k2, (EMBED_DIM, FEAT_DIM), dtype=jnp.float32, minval=-limit, maxval=limit)
        row = jax.random.randint(k3, (N_EDGES,), 0, N_NODES, dtype=jnp.int64)
        col = jax.random.randint(k4, (N_EDGES,), 0, N_NODES, dtype=jnp.int64)
        vals = jax.random.uniform(k5, (N_EDGES,), dtype=jnp.float32)
        return {'x': x, 'weight': weight, 'row': row, 'col': col, 'vals': vals}
    _L0_gnn_all = _L0_gnn_setup()
    _L0_gnn_in = {k: v for k, v in _L0_gnn_all.items() if k in ('weight',)}
    del _L0_gnn_all

    def _L0_mix_setup():
        import jax, jax.numpy as jnp
        import numpy as np
        DIM = 512
        DIM_HEAD = 64
        HEADS = 8
        SCALE = 8.0
        DIM_INNER = DIM_HEAD * HEADS

        def _l2norm(t, axis=-1, eps=1e-12):
            return t / jnp.maximum(jnp.linalg.norm(t, axis=axis, keepdims=True), eps)
        key = jax.random.key(seed)
        k1, k2, k3, k4 = jax.random.split(key, 4)
        b, n = (8, 512)
        x = jax.random.normal(k1, (b, n, DIM), dtype=jnp.float32)
        gamma = jnp.ones((DIM,), dtype=jnp.float32)
        w_qkv = jax.random.normal(k2, (DIM, 3 * DIM_INNER), dtype=jnp.float32) * DIM ** (-0.5)
        temperature = jnp.ones((HEADS, 1, 1), dtype=jnp.float32)
        w_out = jax.random.normal(k3, (DIM_INNER, DIM), dtype=jnp.float32) * DIM_INNER ** (-0.5)
        return {'x': x, 'gamma': gamma, 'w_qkv': w_qkv, 'temperature': temperature, 'w_out': w_out}
    _L0_mix_all = _L0_mix_setup()
    _L0_mix_in = {k: v for k, v in _L0_mix_all.items() if k in ('gamma', 'w_qkv', 'temperature', 'w_out')}
    del _L0_mix_all

    def _L0_ffn_setup():
        import jax, jax.numpy as jnp
        import numpy as np
        CAPACITY_FACTOR = 1.25
        TOP_K = 2

        def _moe(x, Wg, W1, b1, W2, b2):
            B, T, D = x.shape
            N = Wg.shape[1]
            K = TOP_K
            BT = B * T
            BTK = BT * K
            C = int(np.ceil(CAPACITY_FACTOR * BTK / N))
            x_flat = x.reshape(BT, D)
            probs = jax.nn.softmax(x_flat @ Wg, axis=-1)
            vals, idx = jax.lax.top_k(probs, K)
            vals = vals / jnp.clip(vals.sum(-1, keepdims=True), 1e-09)
            a = idx.reshape(BTK)
            oh = jax.nn.one_hot(a, N, dtype=jnp.int32)
            rank = jnp.cumsum(oh, axis=0) - oh
            pos = jnp.take_along_axis(rank, a[:, None], axis=1)[:, 0]
            keep = pos < C
            dest = jnp.where(keep, a * C + pos, N * C)
            token = jnp.arange(BTK) // K
            buf = jnp.zeros((N * C, D), x.dtype).at[dest].set(x_flat[token], mode='drop')
            buf = buf.reshape(N, C, D)
            h = jax.nn.relu(jnp.einsum('ncd,ndh->nch', buf, W1) + b1[:, None, :])
            o = (jnp.einsum('nch,nhd->ncd', h, W2) + b2[:, None, :]).reshape(N * C, D)
            gathered = o[jnp.minimum(dest, N * C - 1)]
            w = vals.reshape(BTK) * keep.astype(x.dtype)
            y_flat = jax.ops.segment_sum(gathered * w[:, None], token, num_segments=BT)
            contrib = jax.ops.segment_sum(w, token, num_segments=BT)
            y_flat = jnp.where(contrib[:, None] <= 1e-12, x_flat, y_flat)
            return y_flat.reshape(B, T, D)
        key = jax.random.key(seed)
        ks = jax.random.split(key, 4)
        B, T, D, H, N = (8, 1024, 512, 512, 32)
        x = jax.random.normal(ks[0], (B, T, D), jnp.float32)
        Wg = jax.random.normal(ks[1], (D, N), jnp.float32) * 0.02
        W1 = jax.random.normal(ks[2], (N, D, H), jnp.float32) * 0.02
        b1 = jnp.zeros((N, H), jnp.float32)
        W2 = jax.random.normal(ks[3], (N, H, D), jnp.float32) * 0.02
        b2 = jnp.zeros((N, D), jnp.float32)
        return {'x': x, 'Wg': Wg, 'W1': W1, 'b1': b1, 'W2': W2, 'b2': b2}
    _L0_ffn_all = _L0_ffn_setup()
    _L0_ffn_in = {k: v for k, v in _L0_ffn_all.items() if k in ('Wg', 'W1', 'b1', 'W2', 'b2')}
    del _L0_ffn_all
    return {'x': x, 'src': src, 'dst': dst, 'edge_weight': edge_weight, 'L0_gnn_weight': _L0_gnn_in['weight'], 'L0_mix_gamma': _L0_mix_in['gamma'], 'L0_mix_w_qkv': _L0_mix_in['w_qkv'], 'L0_mix_temperature': _L0_mix_in['temperature'], 'L0_mix_w_out': _L0_mix_in['w_out'], 'L0_ffn_Wg': _L0_ffn_in['Wg'], 'L0_ffn_W1': _L0_ffn_in['W1'], 'L0_ffn_b1': _L0_ffn_in['b1'], 'L0_ffn_W2': _L0_ffn_in['W2'], 'L0_ffn_b2': _L0_ffn_in['b2']}

def reference(x, src, dst, edge_weight, L0_gnn_weight, L0_mix_gamma, L0_mix_w_qkv, L0_mix_temperature, L0_mix_w_out, L0_ffn_Wg, L0_ffn_W1, L0_ffn_b1, L0_ffn_W2, L0_ffn_b2):
    import jax
    import jax.numpy as jnp

    def _L0_gnn_ref(x, weight, row, col, vals):
        import jax, jax.numpy as jnp
        import numpy as np
        N_NODES = 8192
        N_EDGES = 65536
        FEAT_DIM = 512
        EMBED_DIM = 512
        h = jnp.einsum('nf,ef->ne', x, weight)
        msgs = vals[:, None] * h[col]
        out = jax.ops.segment_sum(msgs, row, num_segments=N_NODES)
        return out

    def _L0_mix_ref(x, gamma, w_qkv, temperature, w_out):
        import jax, jax.numpy as jnp
        import numpy as np
        DIM = 512
        DIM_HEAD = 64
        HEADS = 8
        SCALE = 8.0
        DIM_INNER = DIM_HEAD * HEADS

        def _l2norm(t, axis=-1, eps=1e-12):
            return t / jnp.maximum(jnp.linalg.norm(t, axis=axis, keepdims=True), eps)
        b, n, _ = x.shape
        xn = _l2norm(x) * DIM ** 0.5 * gamma
        qkv = xn @ w_qkv
        qkv = qkv.reshape(b, n, 3, HEADS, DIM_HEAD)
        qkv = jnp.transpose(qkv, (2, 0, 3, 4, 1))
        q, k, v = (qkv[0], qkv[1], qkv[2])
        q = _l2norm(q)
        k = _l2norm(k)
        q = q * jnp.exp(temperature)
        sim = jnp.einsum('bhdn,bhen->bhde', q, k) * SCALE
        attn = jax.nn.softmax(sim, axis=-1)
        out = jnp.einsum('bhde,bhen->bhdn', attn, v)
        out = jnp.transpose(out, (0, 3, 1, 2)).reshape(b, n, DIM_INNER)
        return out @ w_out

    def _L0_ffn_ref(x, Wg, W1, b1, W2, b2):
        import jax, jax.numpy as jnp
        import numpy as np
        CAPACITY_FACTOR = 1.25
        TOP_K = 2

        def _moe(x, Wg, W1, b1, W2, b2):
            B, T, D = x.shape
            N = Wg.shape[1]
            K = TOP_K
            BT = B * T
            BTK = BT * K
            C = int(np.ceil(CAPACITY_FACTOR * BTK / N))
            x_flat = x.reshape(BT, D)
            probs = jax.nn.softmax(x_flat @ Wg, axis=-1)
            vals, idx = jax.lax.top_k(probs, K)
            vals = vals / jnp.clip(vals.sum(-1, keepdims=True), 1e-09)
            a = idx.reshape(BTK)
            oh = jax.nn.one_hot(a, N, dtype=jnp.int32)
            rank = jnp.cumsum(oh, axis=0) - oh
            pos = jnp.take_along_axis(rank, a[:, None], axis=1)[:, 0]
            keep = pos < C
            dest = jnp.where(keep, a * C + pos, N * C)
            token = jnp.arange(BTK) // K
            buf = jnp.zeros((N * C, D), x.dtype).at[dest].set(x_flat[token], mode='drop')
            buf = buf.reshape(N, C, D)
            h = jax.nn.relu(jnp.einsum('ncd,ndh->nch', buf, W1) + b1[:, None, :])
            o = (jnp.einsum('nch,nhd->ncd', h, W2) + b2[:, None, :]).reshape(N * C, D)
            gathered = o[jnp.minimum(dest, N * C - 1)]
            w = vals.reshape(BTK) * keep.astype(x.dtype)
            y_flat = jax.ops.segment_sum(gathered * w[:, None], token, num_segments=BT)
            contrib = jax.ops.segment_sum(w, token, num_segments=BT)
            y_flat = jnp.where(contrib[:, None] <= 1e-12, x_flat, y_flat)
            return y_flat.reshape(B, T, D)
        return _moe(x, Wg, W1, b1, W2, b2)
    xn = _layernorm(x, axis=-1)
    x = x + _L0_gnn_ref(xn, L0_gnn_weight, src, dst, edge_weight) + _L0_mix_ref(xn[None], L0_mix_gamma, L0_mix_w_qkv, L0_mix_temperature, L0_mix_w_out)[0]
    x = x + _L0_ffn_ref(_layernorm(x, axis=-1)[None], L0_ffn_Wg, L0_ffn_W1, L0_ffn_b1, L0_ffn_W2, L0_ffn_b2)[0]
    return x

_drawn_inputs = setup_inputs


def setup_inputs(seed=0):
    import zlib

    import numpy as np

    out = dict(_drawn_inputs(seed))
    spreads = {'L0_mix_gamma': (1.0, 0.2),
     'L0_mix_temperature': (1.0, 0.2),
     'L0_ffn_b1': (0.0, 0.8),
     'L0_ffn_b2': (0.0, 0.292)}
    factors = {}
    for name, (base, spread) in spreads.items():
        noise = np.random.default_rng([zlib.crc32(name.encode()), seed]).standard_normal(out[name].shape)
        drawn = base * np.exp(spread * noise) if base else spread * noise
        out[name] = jnp.asarray(drawn.astype(out[name].dtype))
    for name, factor in factors.items():
        out[name] = (out[name] * factor).astype(out[name].dtype)
    return out
```

```python
import concourse.bass as bass
from concourse import mybir
from contextlib import ExitStack
import math

P = 128
BANK = 512
D = 512
DC = D // P


class Chain:

    def __init__(self, eng, sem, passed=None):
        self.eng, self.sem, self.base, self.k, self.i, self.per = eng, sem, 0, 0, 0, 0
        self.passed = passed

    def at(self):
        return self.i * self.per + (self.base + self.k)

    def __call__(self, ins):
        ins.then_inc(self.sem, 1)
        self.k += 1
        self.eng.wait_ge(self.sem, self.at())
        if self.passed is not None and not isinstance(self.at(), int):
            self.eng.sem_inc(self.passed, 1)

    def round(self, i, per):
        if isinstance(i, int) and i == 0:
            self.base, self.k = self.base + self.k, 0
        self.i, self.per, self.k = i, per, 0

    def end(self, n):
        assert self.k == self.per, (self.k, self.per)
        self.base, self.k, self.i, self.per = self.base + n * self.per, 0, 0, 0


def hold(eng, sem, value, passed):
    eng.wait_ge(sem, value)
    eng.sem_inc(passed, 1)


def rounds(eng, n, body):
    body(0)
    with eng.Fori(1, n) as i:
        body(i)


def first(i):
    return isinstance(i, int) and i == 0


def build(nc, x, src, dst, edge_w, gnn_w, gamma, w_qkv, temp, w_out, Wg, W1, b1, W2, b2, out):
    f32, bf16, i32, u32 = mybir.dt.float32, mybir.dt.bfloat16, mybir.dt.int32, mybir.dt.uint32
    ALU, ACT, AX = mybir.AluOpType, mybir.ActivationFunctionType, mybir.AxisListType.X
    ds = bass.ds

    N = x.shape[0]
    NT = N // P
    E = src.shape[0]
    EC = E // P
    ET = EC + NT
    CH, KC = 4, 8
    HC = CH * KC
    BR = EC // (2 * HC)
    HEADS, DH, SCALE = 8, 64, 8.0
    LN_EPS, L2_EPS = 1e-5, 1e-12
    NX = Wg.shape[1]
    CAP = int(math.ceil(1.25 * 2 * N / NX))
    CT = CAP // P
    HN = CAP // 2
    SLOTS = NX * CAP
    FAR = 65536.0

    H_d = nc.dram_tensor("h_rows", (N, D), f32, kind="Internal").ap()
    rec_d = nc.dram_tensor("edge_records", (P * ET, 4), f32, kind="Internal").ap()
    x1_d = nc.dram_tensor("x1_rows", (N, D), f32, kind="Internal").ap()
    buf_d = nc.dram_tensor("expert_in", (SLOTS, D), f32, kind="Internal").ap()
    o_d = nc.dram_tensor("expert_out", (SLOTS, D), f32, kind="Internal").ap()

    ctx = ExitStack()
    with ctx:
        def sb(name, shape, dt):
            return ctx.enter_context(nc.sbuf_tensor(name, shape, dt))

        def sem(name):
            return ctx.enter_context(nc.semaphore(name))

        arena = sb("arena", [P, NT * D], f32)
        work = sb("work", [P, 14336], f32)
        ring = sb("ring", [P, 8, D], f32)

        def cut(t, at, n):
            return t[:, at:at + n]

        def v3(t, a):
            return t.rearrange("p (a b) -> p a b", a=a)

        acc = v3(arena[:, :], NT)
        oh_all = arena[:, :].bitcast(bf16)
        src_i = cut(work, 0, EC).bitcast(i32)
        srcl_f = cut(work, 0, EC)
        dst_i = cut(work, EC, EC).bitcast(i32)
        w_f = cut(work, 2 * EC, EC)
        tmp_i = cut(work, 3 * EC, EC).bitcast(i32)
        addr_all = cut(work, 3 * EC, EC).bitcast(u32)
        win_bf = cut(work, 4 * EC, EC // 2).bitcast(bf16)
        o_rec = 4 * EC + EC // 2
        recs_flat = cut(work, o_rec, 4 * ET)
        recs = v3(recs_flat, ET)
        recs_i = v3(recs_flat.bitcast(u32), ET)
        o_wT = o_rec + 4 * ET
        wT = v3(cut(work, o_wT, 2048), DC)
        o_M = o_wT + 2048
        Msb = v3(cut(work, o_M, 2048), DC)
        o_h = o_M + 2048
        h_sb = v3(cut(work, o_h, 1024), 2)
        assert o_h + 1024 <= 14336
        tot_sb = v3(cut(work, o_M, 2048), CH * KC)
        init_sb = v3(cut(work, o_wT, 2048), CH * KC)
        prod = v3(cut(work, o_M, 1024), 2)
        stat1 = cut(work, o_h, NT * 6).rearrange("p (t s) -> p t s", s=6)
        xt, xn, xh, xT = (ring[:, 2 * k:2 * k + 2, :] for k in range(4))
        o = 0
        wqkv = v3(cut(arena, o, 6144), DC); o += 6144
        wout = v3(cut(arena, o, 2048), DC); o += 2048
        gwr = v3(cut(arena, o, 2048), DC); o += 2048
        G = v3(cut(arena, o, 2048), DC); o += 2048
        Tk = v3(cut(arena, o, 2048), DC); o += 2048
        prk = v3(cut(arena, o, 2048), DC); o += 2048
        prq = v3(cut(arena, o, 2048), DC); o += 2048
        wvT = v3(cut(arena, o, 2048), DC); o += 2048
        Bm = v3(cut(arena, o, 2048), DC); o += 2048
        kinv = cut(arena, o, 512); o += 512
        sim = v3(cut(arena, o, 256), DC); o += 256
        Abd = v3(cut(arena, o, 512), DC); o += 512
        oh = v3(cut(work, o_wT, 1024), 8)
        iotaT = cut(work, 0, ET)
        maskT = cut(work, ET, ET)
        wt_i = cut(work, 2 * ET, ET)[0:1, :].bitcast(i32)
        L = v3(cut(work, 0, 2048), NT)
        OHA = v3(cut(work, 2048, 2048).bitcast(bf16), 2)
        Tsb = v3(cut(work, 4096, 2048), NT)
        Cin = v3(cut(work, 6144, 2048), NT)
        Pfx = cut(work, 8192, 2048)
        prd = cut(work, 10240, 2048)
        top, topi, wts, rank, sidx, gidx = (v3(cut(work, 12288 + k * 2 * NT, 2 * NT), 2) for k in range(6))
        sidx, gidx = sidx.bitcast(u32), gidx.bitcast(u32)
        stat2 = cut(work, 10240, NT * 6).rearrange("p (t s) -> p t s", s=6)
        xs2, xT2 = ring[:, 0:2, :], ring[:, 2:4, :]
        xsc = ring[:, 4:8, :]
        o = 0
        w1s = [v3(cut(arena, o + k * 2048, 2048), DC) for k in range(2)]; o += 4096
        w2s = [v3(cut(arena, o + k * 2048, 2048), DC) for k in range(2)]; o += 4096
        bin_ = [v3(cut(arena, o + k * CT * D, CT * D), CT) for k in range(2)]; o += 2 * CT * D
        bT = v3(cut(arena, o, DC * CAP), DC); o += DC * CAP
        hT = v3(cut(arena, o, DC * CAP), DC); o += DC * CAP
        osb = [v3(cut(arena, o + k * CT * D, CT * D), CT) for k in range(2)]; o += 2 * CT * D
        b2s = [cut(arena, o + k * D, D) for k in range(2)]; o += 2 * D
        xr = v3(cut(arena, o, 2048), 4); o += 2048
        assert o <= NT * D
        fin = v3(cut(work, 0, 2048), 4)
        b1_sb = cut(work, o_h, D)[0:NX, :]

        ident = sb("ident", [P, P], f32)
        ones_f = sb("ones_f", [P, P], f32)
        iota_f = sb("iota_f", [P, P], f32)
        before = sb("before", [P, P], bf16)
        notbefore = sb("notbefore", [P, P], bf16)
        ones_b = sb("ones_b", [P, P], bf16)
        zero_b = sb("zero_b", [P, P], bf16)
        iota_b = sb("iota_b", [P, NT], bf16)
        eps = sb("eps", [P, 2], f32)
        mean1 = sb("mean1", [P, NT], f32)
        rstd1 = sb("rstd1", [P, NT], f32)
        l2s = sb("l2s", [P, NT], f32)
        xhs = sb("xhs", [P, NT], f32)
        sA = sb("sA", [P, NT], f32)
        sB = sb("sB", [P, NT], f32)
        addr_st = sb("addr_st", [P, 2, HC], u32)
        rec_st = sb("rec_st", [P, 2, HC, 4], f32)
        idx_st = sb("idx_st", [P, 2, 4], u32)
        ends = sb("ends", [P, NT], f32)
        wtot = sb("wtot", [P, NT], f32)
        nt_i = sb("nt_i", [P, NT], i32)
        ecol = sb("ecol", [NT, 1], f32)
        gcol = sb("gcol", [P, DC], f32)
        tcol = sb("tcol", [P, DC], f32)
        qs = sb("qs", [P, DC], f32)
        mx = sb("mx", [P, DC], f32)
        wg_sb = sb("wg_sb", [P, DC, NX], f32)
        b1T = sb("b1T", [P, DC, NX], f32)
        m8 = sb("m8", [P, 2, 8], f32)
        i8 = sb("i8", [P, 2, 8], u32)
        rt_st = sb("rt_st", [P, 2, 4], u32)
        mean2, rstd2, nb2, ca, cb = mean1, rstd1, l2s, xhs, ends

        bank = [ctx.enter_context(nc.psum_tensor(f"bank{k}", [P, BANK], f32)) for k in range(8)]

        const_made = sem("const_made")
        fill_made = sem("fill_made")
        pool_step = sem("pool_step")
        dve_step = sem("dve_step")
        pool_passed = sem("pool_passed")
        dve_passed = sem("dve_passed")
        act_passed = sem("act_passed")
        edges_in = sem("edges_in")
        rec_filled = sem("rec_filled")
        buf_filled = sem("buf_filled")
        xs_in = [sem(f"xs_in{k}") for k in range(8)]
        stat_read = sem("stat_read")
        var_made = sem("var_made")
        sd_made = sem("sd_made")
        oh_built = sem("oh_built")
        totals_made = sem("totals_made")
        init_made = sem("init_made")
        ecol_made = sem("ecol_made")
        ranked = sem("ranked")
        rank_read = sem("rank_read")
        addr_made = sem("addr_made")
        scat = [sem(f"scat{k}") for k in range(2)]
        gw_in = sem("gw_in")
        qkv_in = sem("qkv_in")
        wt_tr = sem("wt_tr")
        wt_made = sem("wt_made")
        a1_in = [sem(f"a1_in{k}") for k in range(2)]
        xn_made = sem("xn_made")
        xh_made = sem("xh_made")
        xn_turned = sem("xn_turned")
        xT_made = sem("xT_made")
        gram_done = sem("gram_done")
        h_summed = sem("h_summed")
        h_made = sem("h_made")
        h_out = [sem(f"h_out{k}") for k in range(2)]
        qkv_scaled = sem("qkv_scaled")
        m_pe = sem("m_pe")
        m_act = sem("m_act")
        m_dve = sem("m_dve")
        a2_in = [sem(f"a2_in{k}") for k in range(2)]
        yn_made = sem("yn_made")
        yn_turned = sem("yn_turned")
        yT_made = sem("yT_made")
        mix_summed = sem("mix_summed")
        acc_set = sem("acc_set")
        recs_in = sem("recs_in")
        iota_t = sem("iota_t")
        mask_made = sem("mask_made")
        wt_summed = sem("wt_summed")
        row_in = [sem(f"row_in{k}") for k in range(8)]
        oh_made = sem("oh_made")
        msg_summed = sem("msg_summed")
        acc_added = sem("acc_added")
        x1_out = sem("x1_out")
        var2_made = sem("var2_made")
        sd2_made = sem("sd2_made")
        xs_made = sem("xs_made")
        xs_turned = sem("xs_turned")
        xsT_made = sem("xsT_made")
        gated = sem("gated")
        L_made = sem("L_made")
        top_made = sem("top_made")
        small_in = sem("small_in")
        b1_in = sem("b1_in")
        b1_turned = sem("b1_turned")
        b1T_made = sem("b1T_made")
        lsub_made = sem("lsub_made")
        exp_made = sem("exp_made")
        oha_made = sem("oha_made")
        pfx_made = sem("pfx_made")
        T_made = sem("T_made")
        route_made = sem("route_made")
        row_staged = sem("row_staged")
        disp = [sem(f"disp{k}") for k in range(4)]
        bin_in = [sem(f"bin_in{k}") for k in range(2)]
        w1_in = [sem(f"w1_in{k}") for k in range(2)]
        w2_in = [sem(f"w2_in{k}") for k in range(2)]
        e_turned = sem("e_turned")
        e_bT = sem("e_bT")
        e_up = sem("e_up")
        e_h = sem("e_h")
        e_down = sem("e_down")
        e_o = sem("e_o")
        e_out = [sem(f"e_out{k}") for k in range(2)]
        og_in = [sem(f"og_in{k}") for k in range(4)]
        xr_in = [sem(f"xr_in{k}") for k in range(4)]
        fin_made = sem("fin_made")
        fin_out = [sem(f"fin_out{k}") for k in range(4)]

        x_t = x.rearrange("(t p) d -> t p d", p=P)
        H_t = H_d.rearrange("(t p) d -> t p d", p=P)
        x1_pt = x1_d.rearrange("(t p) d -> p t d", p=P)
        x1_t = x1_d.rearrange("(t p) d -> t p d", p=P)
        out_t = out.rearrange("(t p) d -> t p d", p=P)
        buf_e = buf_d.rearrange("(e c p) d -> e p c d", p=P, c=CT)
        o_e = o_d.rearrange("(e c p) d -> e p c d", p=P, c=CT)
        w1_e = W1.rearrange("e (c p) h -> e p c h", p=P)
        w2_e = W2.rearrange("e (c p) h -> e p c h", p=P)

        NCONST = 11
        block = ctx.enter_context(nc.Block())

        @block.sync
        def _(sp):
            for t_, s_ in ((src_i, src), (dst_i, dst), (w_f, edge_w)):
                sp.dma_start(t_, s_.rearrange("(p c) -> p c", p=P)).then_inc(edges_in, 16)

            def s_body(i):
                for k in range(8):
                    if not first(i):
                        sp.wait_ge(stat_read, i * 8 + (k - 7))
                    sp.dma_start(acc[:, k, :], x_t[i * 8 + k]).then_inc(xs_in[k], 16)
            rounds(sp, NT // 8, s_body)

            sp.wait_ge(fill_made, 3)
            sp.dma_start(rec_d.rearrange("(q t) c -> q (t c)", q=P), recs_flat).then_inc(rec_filled, 16)
            zrow = ring[:, :, :].rearrange("p a b -> p (a b)")
            z_dst = buf_d.rearrange("(p k r) d -> p k (r d)", p=P, r=8)
            sp.dma_start(z_dst, zrow[:, None, :].to_broadcast([P, SLOTS // P // 8, 8 * D])).then_inc(buf_filled, 16)
            sp.dma_start(wg_sb[:, :, :], Wg.rearrange("(c p) e -> p c e", p=P)).then_inc(small_in, 16)
            with nc.allow_non_contiguous_dma(reason="small"):
                sp.dma_start(gcol[:, :], gamma.rearrange("(c p) -> p c", p=P)).then_inc(small_in, 16)
                t2 = temp.rearrange("(c two) a b -> two c (a b)", two=2)
                for hh in range(2):
                    tv = t2[hh].rearrange("c b -> b c")
                    sp.dma_start(tcol[hh * 64:hh * 64 + 64, :], tv.to_broadcast([64, DC])).then_inc(small_in, 16)

            sp.wait_ge(rank_read, 2 * CH * BR)
            sp.dma_start(gwr, gnn_w.rearrange("(c p) f -> p c f", p=P)).then_inc(gw_in, 16)
            sp.dma_start(wqkv, w_qkv.rearrange("(c p) f -> p c f", p=P)).then_inc(qkv_in, 16)
            sp.dma_start(wout, w_out.rearrange("(c p) f -> p c f", p=P)).then_inc(qkv_in, 16)
            sp.wait_ge(buf_filled, 16)

            def a1_body(i):
                for s in range(2):
                    if not first(i):
                        sp.wait_ge(xh_made, i * 2 + (s - 1))
                    sp.dma_start(xt[:, s, :], x_t[i * 2 + s]).then_inc(a1_in[s], 16)
            rounds(sp, NT // 2, a1_body)

            sp.wait_ge(xh_made, NT)

            def a2_body(i):
                for s in range(2):
                    if not first(i):
                        sp.wait_ge(acc_set, i * 2 + (s - 1))
                    sp.dma_start(xt[:, s, :], x_t[i * 2 + s]).then_inc(a2_in[s], 16)
            rounds(sp, NT // 2, a2_body)

            for k in range(2):
                sp.wait_ge(scat[k], 16 * HC * BR)
            sp.dma_start(recs_flat, rec_d.rearrange("(q t) c -> q (t c)", q=P)).then_inc(recs_in, 16)

            for k in range(2):
                sp.wait_ge(h_out[k], 16 * (NT // 2))
            sp.dma_start(b1_sb, b1[:, :]).then_inc(b1_in, 16)

            sp.wait_ge(acc_added, ET)
            for k in range(8):
                n = NT // 8
                sp.dma_start(x1_pt[:, k * n:(k + 1) * n, :], acc[:, k * n:(k + 1) * n, :]).then_inc(x1_out, 16)

            sp.wait_ge(x1_out, 16 * 8)
            for k in range(4):
                sp.wait_ge(disp[k], 16 * 2 * (NT // 4))

            def e_body(i):
                for s in range(2):
                    e = i * 2 + s
                    if not first(i):
                        sp.wait_ge(e_turned, i * 2 * CT + (s - 1) * CT)
                    sp.dma_start(bin_[s], buf_e[e]).then_inc(bin_in[s], 16)
                    if not first(i):
                        sp.wait_ge(e_up, i * 16 + (s - 1) * 8)
                    sp.dma_start(w1s[s], w1_e[e]).then_inc(w1_in[s], 16)
                    if not first(i):
                        sp.wait_ge(e_down, i * 2 * CT + (s - 1) * CT)
                    sp.dma_start(w2s[s], w2_e[e]).then_inc(w2_in[s], 16)
                    if not first(i):
                        sp.wait_ge(e_o, i * 2 * CT + (s - 1) * CT)
                    sp.dma_start(b2s[s], b2[ds(e, 1), :].to_broadcast([P, D])).then_inc(w2_in[s], 16)
                    if not (first(i) and s == 0):
                        sp.wait_ge(e_o, i * 2 * CT + s * CT)
                        sp.dma_start(o_e[i * 2 + (s - 1)], osb[1 - s]).then_inc(e_out[1 - s], 16)
            rounds(sp, NX // 2, e_body)
            sp.wait_ge(e_o, NX * CT)
            sp.dma_start(o_e[NX - 1], osb[1]).then_inc(e_out[1], 16)

            def f_body(i):
                for k in range(4):
                    if not first(i):
                        sp.wait_ge(fin_made, i * 4 + (k - 3))
                    sp.dma_start(xr[:, k, :], x1_t[i * 4 + k]).then_inc(xr_in[k], 16)
                for k in range(4):
                    sp.wait_ge(fin_made, i * 4 + (k + 1))
                    sp.dma_start(out_t[i * 4 + k], fin[:, k, :]).then_inc(fin_out[k], 16)
            rounds(sp, NT // 4, f_body)
            for k in range(4):
                sp.wait_ge(fin_out[k], 16 * (NT // 4))

        @block.gpsimd
        def _(pool):
            step = Chain(pool, pool_step, pool_passed)
            step(pool.memset(ident[:, :], 0.0))
            step(pool.memset(ones_b[:, :], 1.0))
            pool.affine_select(out=ident[:, :], in_=ident[:, :], compare_op=ALU.not_equal, fill=1.0, base=0,
                               pattern=[[-1, P]], channel_multiplier=1).then_inc(const_made, 1)
            pool.affine_select(out=before[:, :], in_=ones_b[:, :], compare_op=ALU.is_gt, fill=0.0, base=0,
                               pattern=[[1, P]], channel_multiplier=-1).then_inc(const_made, 1)
            pool.affine_select(out=notbefore[:, :], in_=ones_b[:, :], compare_op=ALU.is_ge, fill=0.0, base=0,
                               pattern=[[-1, P]], channel_multiplier=1).then_inc(const_made, 1)
            pool.memset(ones_f[:, :], 1.0).then_inc(const_made, 1)
            pool.memset(zero_b[:, :], 0.0).then_inc(const_made, 1)
            pool.memset(eps[:, 0:1], LN_EPS).then_inc(const_made, 1)
            pool.memset(eps[:, 1:2], 0.0).then_inc(const_made, 1)
            pool.iota(iota_b[:, :], [[1, NT]], base=0, channel_multiplier=0,
                      allow_small_or_imprecise_dtypes=True).then_inc(const_made, 1)
            pool.iota(iota_f[:, :], [[1, P]], base=0, channel_multiplier=0,
                      allow_small_or_imprecise_dtypes=True).then_inc(const_made, 1)
            pool.memset(rec_st[:, :, :, :], 0.0).then_inc(const_made, 1)
            pool.memset(b1T[:, :, :], 0.0).then_inc(const_made, 1)
            pool.memset(recs_flat, 0.0).then_inc(fill_made, 1)
            pool.wait_ge(fill_made, 1)
            pool.memset(recs[:, :, 1:2], -1.0).then_inc(fill_made, 1)
            pool.memset(ring[:, :, :], 0.0).then_inc(fill_made, 1)

            pool.wait_ge(rec_filled, 16)

            def b_body(i):
                step.round(i, 8)
                for h in range(2):
                    if not first(i):
                        pool.wait_ge(scat[h], i * (16 * HC))
                    pool.wait_ge(addr_made, i * 2 + (h + 1))
                    c0 = i * (2 * HC) + h * HC
                    step(pool.tensor_copy(addr_st[:, h, :], addr_all[:, ds(c0, HC)]))
                    step(pool.tensor_copy(rec_st[:, h, :, 0].bitcast(i32), dst_i[:, ds(c0, HC)]))
                    step(pool.tensor_copy(rec_st[:, h, :, 1], srcl_f[:, ds(c0, HC)]))
                    step(pool.tensor_copy(rec_st[:, h, :, 2], w_f[:, ds(c0, HC)]))
                    for c in range(HC):
                        pool.indirect_dma_start(
                            rec_d, bass.IndirectOffsetOnAxis(addr_st[:, h, c:c + 1], 0),
                            rec_st[:, h, c, :], None).then_inc(scat[h], 16)
            rounds(pool, BR, b_body)
            step.end(BR)

            for k in range(2):
                pool.wait_ge(scat[k], 16 * HC * BR)
            pool.iota(iotaT, [[1, ET]], base=0, channel_multiplier=0,
                      allow_small_or_imprecise_dtypes=True).then_inc(iota_t, 1)
            pool.wait_ge(recs_in, 16)
            for k in range(2):
                pool.wait_ge(h_out[k], 16 * (NT // 2))
            pool.wait_ge(acc_set, NT)

            def c_body(i):
                step.round(i, 2)
                for h in range(2):
                    if not first(i):
                        for k in range(4):
                            hold(pool, row_in[h * 4 + k], i * 16, pool_passed)
                    step(pool.tensor_copy(idx_st[:, h, :], recs_i[:, ds(i * 8 + h * 4, 4), 0]))
                    for k in range(4):
                        s = h * 4 + k
                        if not first(i):
                            hold(pool, msg_summed, i * 8 + (s - 7), pool_passed)
                        pool.indirect_dma_start(
                            ring[:, s, :], None, H_d,
                            bass.IndirectOffsetOnAxis(idx_st[:, h, k:k + 1], 0)).then_inc(row_in[s], 16)
            rounds(pool, ET // 8, c_body)
            step.end(ET // 8)

            pool.wait_ge(route_made, 1)
            pool.wait_ge(buf_filled, 16)

            def d_body(i):
                step.round(i, 1)
                if not first(i):
                    for k in range(4):
                        pool.wait_ge(disp[k], i * 32)
                step(pool.tensor_copy(rt_st[:, :, :], sidx[:, :, ds(i * 4, 4)]))
                for k in range(4):
                    hold(pool, row_staged, i * 4 + (k + 1), pool_passed)
                    for j in range(2):
                        pool.indirect_dma_start(
                            buf_d, bass.IndirectOffsetOnAxis(rt_st[:, j, k:k + 1], 0), xsc[:, k, :], None,
                            bounds_check=SLOTS - 1, oob_is_err=False).then_inc(disp[k], 16)
            rounds(pool, NT // 4, d_body)
            step.end(NT // 4)

            for k in range(4):
                pool.wait_ge(disp[k], 16 * 2 * (NT // 4))
            for k in range(2):
                pool.wait_ge(e_out[k], 16 * (NX // 2))

            def f_body(i):
                step.round(i, 1)
                if not first(i):
                    for k in range(4):
                        pool.wait_ge(og_in[k], i * 32)
                step(pool.tensor_copy(rt_st[:, :, :], gidx[:, :, ds(i * 4, 4)]))
                for k in range(4):
                    if not first(i):
                        hold(pool, fin_made, i * 4 + (k - 3), pool_passed)
                    for j in range(2):
                        pool.indirect_dma_start(
                            ring[:, 2 * k + j, :], None, o_d,
                            bass.IndirectOffsetOnAxis(rt_st[:, j, k:k + 1], 0)).then_inc(og_in[k], 16)
            rounds(pool, NT // 4, f_body)
            step.end(NT // 4)

        @block.scalar
        def _(act):
            act.wait_ge(const_made, NCONST)
            act.wait_ge(var_made, 1)
            act.activation(sA[:, :], l2s[:, :], ACT.Sqrt, bias=eps[:, 0:1], scale=1.0).then_inc(sd_made, 1)
            act.activation(sB[:, :], l2s[:, :], ACT.Sqrt, bias=eps[:, 1:2], scale=float(D)).then_inc(sd_made, 1)
            for m in range(DC):
                act.wait_ge(wt_tr, m + 1)
                act.copy(wT[:, m, :], bank[4 + m][:, :]).then_inc(wt_made, 1)

            def a1_body(i):
                for s in range(2):
                    n = i * 2 + s
                    act.wait_ge(xn_turned, n + 1)
                    if not first(i):
                        act.wait_ge(h_summed, i * 2 + (s - 1))
                    act.copy(xT[:, s, :], bank[4 + s][:, :]).then_inc(xT_made, 1)
                    act.wait_ge(h_summed, n + 1)
                    if not first(i):
                        act.wait_ge(h_out[s], i * 16)
                    act.copy(h_sb[:, s, :], bank[6 + s][:, :]).then_inc(h_made, 1)
                    act.wait_ge(h_made, n + 1)
                    act.dma_start(H_t[n], h_sb[:, s, :]).then_inc(h_out[s], 16)
            rounds(act, NT // 2, a1_body)

            act.wait_ge(gram_done, NT)
            for m in range(DC):
                act.copy(G[:, m, :], bank[m][:, :]).then_inc(m_act, 1)
            for m in range(DC):
                act.wait_ge(m_pe, m + 1)
                act.copy(wvT[:, m, :], bank[4 + m][:, :]).then_inc(m_act, 1)
            for m in range(DC):
                act.wait_ge(m_pe, 4 + m + 1)
                act.copy(Tk[:, m, :], bank[m][:, :]).then_inc(m_act, 1)
            act.wait_ge(small_in, 16 * 4)
            act.activation(tcol[:, :], tcol[:, :], ACT.Exp).then_inc(m_act, 1)
            act.wait_ge(m_dve, 9)
            act.activation(qs[:, :], qs[:, :], ACT.Sqrt).then_inc(m_act, 1)
            act.wait_ge(m_dve, 10)
            act.activation(kinv, kinv, ACT.Sqrt).then_inc(m_act, 1)
            act.wait_ge(m_dve, 11)
            act.activation(sim, sim, ACT.Exp).then_inc(m_act, 1)
            for m in range(DC):
                act.wait_ge(m_pe, 18 + m)
                act.copy(Bm[:, m, :], bank[m][:, :]).then_inc(m_act, 1)
            for m in range(DC):
                act.wait_ge(m_pe, 22 + m)
                act.copy(Msb[:, m, :], bank[4 + m][:, :]).then_inc(m_act, 1)

            def a2_body(i):
                for s in range(2):
                    act.wait_ge(yn_turned, i * 2 + (s + 1))
                    if not first(i):
                        act.wait_ge(mix_summed, i * 2 + (s - 1))
                    act.copy(xT[:, s, :], bank[s][:, :]).then_inc(yT_made, 1)
            rounds(act, NT // 2, a2_body)

            act.wait_ge(var2_made, 1)
            act.activation(sA[:, :], sB[:, :], ACT.Sqrt, bias=eps[:, 0:1], scale=1.0).then_inc(sd2_made, 1)
            act.wait_ge(b1_turned, 1)
            act.copy(b1T[:, :, :].rearrange("p c e -> p (c e)"), bank[6][:, 0:DC * NX]).then_inc(b1T_made, 1)

            def d_body(i):
                for s in range(2):
                    act.wait_ge(xs_turned, i * 2 + (s + 1))
                    if not first(i):
                        act.wait_ge(gated, i * 2 + (s - 1))
                    act.copy(xT2[:, s, :], bank[s][:, :]).then_inc(xsT_made, 1)
                    act.wait_ge(gated, i * 2 + (s + 1))
                    act.copy(L[:, ds(i * 2 + s, 1), :], bank[2 + s][:, 0:NX][:, None, :]).then_inc(L_made, 1)
            rounds(act, NT // 2, d_body)
            act.wait_ge(lsub_made, 1)
            act.activation(L, L, ACT.Exp).then_inc(exp_made, 1)
            act.activation(wts[:, 1, :], sB[:, :], ACT.Exp).then_inc(exp_made, 1)
            act.wait_ge(pfx_made, 1)
            for m in range(4):
                act.copy(Tsb[:, 16 * m:16 * m + 16, :].rearrange("p a b -> p (a b)"),
                         bank[4 + m][:, :]).then_inc(T_made, 1)
            act.wait_ge(route_made, 1)

            def ds_body(i):
                for k in range(4):
                    if not first(i):
                        hold(act, disp[k], i * 32, act_passed)
                    t = i * 4 + k
                    act.activation(xsc[:, k, :], acc[:, ds(t, 1), :].rearrange("p a d -> p (a d)"), ACT.Identity,
                                   bias=nb2[:, ds(t, 1)], scale=rstd2[:, ds(t, 1)]).then_inc(row_staged, 1)
            rounds(act, NT // 4, ds_body)

            def e_body(i):
                for s in range(2):
                    for g in range(8):
                        hc, hf = g // 2, g % 2
                        act.wait_ge(e_up, i * 16 + (s * 8 + g + 1))
                        if g == 0 and not (first(i) and s == 0):
                            act.wait_ge(e_down, i * 2 * CT + s * CT)
                        act.sem_inc(act_passed, 1)
                        act.activation(hT[:, hc, hf * HN:(hf + 1) * HN], bank[2 + g % 4][:, 0:HN], ACT.Relu,
                                       bias=b1T[:, hc, ds(i * 2 + s, 1)], scale=1.0).then_inc(e_h, 1)
            rounds(act, NX // 2, e_body)

        @block.vector
        def _(dve):
            step = Chain(dve, dve_step)
            dve.wait_ge(const_made, NCONST)

            def moments(stat, mean, var, a, b):
                step(dve.tensor_tensor(a, stat[:, :, 1], stat[:, :, 4], ALU.subtract))
                step(dve.tensor_tensor(mean, stat[:, :, 1], stat[:, :, 4], ALU.add))
                step(dve.tensor_scalar(mean, mean, 0.5, None, ALU.mult))
                step(dve.tensor_tensor(a, a, a, ALU.mult))
                step(dve.tensor_scalar(a, a, 0.25, None, ALU.mult))
                step(dve.tensor_tensor(b, stat[:, :, 2], stat[:, :, 5], ALU.add))
                step(dve.scalar_tensor_tensor(out=var, in0=b, scalar=1.0 / D, in1=a, op0=ALU.mult, op1=ALU.add))

            dve.wait_ge(edges_in, 48)
            sh = P.bit_length() - 1
            step(dve.tensor_scalar(tmp_i, src_i, sh, None, ALU.logical_shift_right))
            step(dve.tensor_copy(win_bf, tmp_i))
            step(dve.tensor_scalar(tmp_i, src_i, P - 1, None, ALU.bitwise_and))
            step(dve.tensor_copy(srcl_f, tmp_i))

            def s_body(i):
                for k in range(8):
                    dve.wait_ge(xs_in[k], i * 16 + 16)
                    dve.bn_stats(stat1[:, ds(i * 8 + k, 1), :].rearrange("p a s -> p (a s)"),
                                 acc[:, k, :]).then_inc(stat_read, 1)
            rounds(dve, NT // 8, s_body)
            dve.wait_ge(stat_read, NT)
            moments(stat1, mean1[:, :], l2s[:, :], sA[:, :], sB[:, :])
            dve.sem_inc(var_made, 1)
            dve.wait_ge(sd_made, 2)
            step(dve.reciprocal(rstd1[:, :], sA[:, :]))
            step(dve.tensor_tensor(sB[:, :], sB[:, :], rstd1[:, :], ALU.mult))
            step(dve.tensor_scalar(sB[:, :], sB[:, :], L2_EPS, None, ALU.max))
            step(dve.reciprocal(l2s[:, :], sB[:, :]))
            step(dve.tensor_scalar(l2s[:, :], l2s[:, :], float(D) ** 0.5, None, ALU.mult))
            step(dve.tensor_tensor(xhs[:, :], l2s[:, :], rstd1[:, :], ALU.mult))

            io = iota_b[:, None, :].to_broadcast([P, KC, NT])

            def oh_body(i):
                for c in range(CH):
                    g = i * CH + c
                    dve.tensor_tensor(oh_all[:, ds(g * 512, 512)].rearrange("p (k w) -> p k w", k=KC),
                                      win_bf[:, ds(g * KC, KC)][:, :, None].to_broadcast([P, KC, NT]), io,
                                      ALU.is_equal).then_inc(oh_built, 1)
            rounds(dve, 2 * BR, oh_body)
            dve.wait_ge(totals_made, 1)
            for c in range(CH):
                t_ = tot_sb[:, c * KC:(c + 1) * KC, :].rearrange("p k w -> p (k w)")
                step(dve.tensor_copy(t_, bank[c][:, :]))
            step(dve.memset(init_sb[:, 0, :], 0.0))
            for m in range(CH * KC - 1):
                step(dve.tensor_tensor(init_sb[:, m + 1, :], init_sb[:, m, :], tot_sb[:, m, :], ALU.add))
            step(dve.tensor_tensor(wtot[:, :], init_sb[:, CH * KC - 1, :], tot_sb[:, CH * KC - 1, :], ALU.add))
            step(dve.tensor_scalar(wtot[:, :], wtot[:, :], float(P - 1), None, ALU.add))
            step(dve.tensor_copy(nt_i[:, :], wtot[:, :]))
            step(dve.tensor_scalar(nt_i[:, :], nt_i[:, :], sh, None, ALU.logical_shift_right))
            step(dve.tensor_copy(wtot[:, :], nt_i[:, :]))
            step(dve.memset(sA[:, :], 0.0))
            step(dve.tensor_tensor_scan(ends[:, :], wtot[:, :], sA[:, :], 0.0, ALU.add, ALU.add))
            step(dve.tensor_tensor(sA[:, :], ends[:, :], wtot[:, :], ALU.subtract))
            step(dve.tensor_scalar(sA[:, :], sA[:, :], float(P), None, ALU.mult))
            dve.tensor_tensor(init_sb, init_sb, sA[:, None, :].to_broadcast([P, CH * KC, NT]),
                              ALU.add).then_inc(init_made, 1)

            def rank_body(i):
                step.round(i, 2 * (2 * CH + 3))
                for h in range(2):
                    for c in range(CH):
                        g = i * (2 * CH) + (h * CH + c)
                        dve.wait_ge(ranked, g + 1)
                        ins = dve.tensor_tensor(prod[:, c % 2, :], bank[4 + c][:, :], oh_all[:, ds(g * 512, 512)],
                                                ALU.mult)
                        ins.then_inc(rank_read, 1)
                        dve.wait_ge(rank_read, g + 1)
                        step(dve.tensor_reduce(sA[:, c * KC:(c + 1) * KC],
                                               prod[:, c % 2, :].rearrange("p (k w) -> p k w", k=KC), AX, ALU.add))
                        step(dve.tensor_copy(nt_i[:, c * KC:(c + 1) * KC], sA[:, c * KC:(c + 1) * KC]))
                    step(dve.tensor_scalar(nt_i[:, HC:2 * HC], nt_i[:, 0:HC], sh, None, ALU.logical_shift_right))
                    step(dve.tensor_scalar(nt_i[:, 0:HC], nt_i[:, 0:HC], P - 1, None, ALU.bitwise_and))
                    step(dve.scalar_tensor_tensor(
                        out=addr_all[:, ds(i * (2 * HC) + h * HC, HC)], in0=nt_i[:, 0:HC], scalar=float(ET),
                        in1=nt_i[:, HC:2 * HC], op0=ALU.mult, op1=ALU.add))
                    dve.sem_inc(addr_made, 1)
            rounds(dve, BR, rank_body)
            step.end(BR)

            def a1_body(i):
                for s in range(2):
                    n = i * 2 + s
                    dve.wait_ge(a1_in[s], i * 16 + 16)
                    if not first(i):
                        dve.wait_ge(xn_turned, i * 2 + (s - 1))
                    dve.tensor_scalar(xn[:, s, :], xt[:, s, :], mean1[:, ds(n, 1)], rstd1[:, ds(n, 1)],
                                      ALU.subtract, ALU.mult).then_inc(xn_made, 1)
                    if not first(i):
                        dve.wait_ge(gram_done, i * 2 + (s - 1))
                    dve.tensor_scalar(xh[:, s, :], xt[:, s, :], mean1[:, ds(n, 1)], xhs[:, ds(n, 1)],
                                      ALU.subtract, ALU.mult).then_inc(xh_made, 1)
            rounds(dve, NT // 2, a1_body)

            dve.wait_ge(qkv_in, 32)
            dve.wait_ge(small_in, 16 * 4)
            for m in range(DC):
                dve.tensor_scalar(wqkv[:, m, :], wqkv[:, m, :], gcol[:, m:m + 1], None,
                                  ALU.mult).then_inc(qkv_scaled, 1)
            dve.wait_ge(qkv_scaled, DC)
            for m in range(DC):
                dve.wait_ge(m_act, 9 + m)
                dve.tensor_tensor(prk[:, m, :], bank[m][:, :], wqkv[:, m, D:2 * D], ALU.mult).then_inc(m_dve, 1)
            for m in range(DC):
                dve.wait_ge(m_pe, 8 + m + 1)
                dve.tensor_tensor(prq[:, m, :], bank[4 + m][:, :], wqkv[:, m, 0:D], ALU.mult).then_inc(m_dve, 1)
            step(dve.memset(Abd, 0.0))
            dve.wait_ge(m_pe, 13)
            dve.tensor_scalar(qs[:, :], bank[4][:, 0:DC], 0.0, None, ALU.max).then_inc(m_dve, 1)
            dve.tensor_scalar(kinv, bank[5][:, :], 0.0, None, ALU.max).then_inc(m_dve, 1)
            dve.wait_ge(m_act, 14)
            step(dve.tensor_scalar(qs[:, :], qs[:, :], L2_EPS, None, ALU.max))
            step(dve.reciprocal(qs[:, :], qs[:, :]))
            step(dve.tensor_tensor(qs[:, :], qs[:, :], tcol[:, :], ALU.mult))
            step(dve.tensor_scalar(qs[:, :], qs[:, :], SCALE, None, ALU.mult))
            dve.wait_ge(m_act, 15)
            step(dve.tensor_scalar(kinv, kinv, L2_EPS, None, ALU.max))
            step(dve.reciprocal(kinv, kinv))
            dve.wait_ge(m_pe, 17)
            for m in range(DC):
                for lo in (0, DH):
                    r = slice(lo, lo + DH)
                    step(dve.tensor_tensor(sim[r, m, :], bank[m][r, lo:lo + DH],
                                           kinv[r, m * P + lo:m * P + lo + DH], ALU.mult))
                step(dve.tensor_scalar(sim[:, m, :], sim[:, m, :], qs[:, m:m + 1], None, ALU.mult))
            step(dve.tensor_reduce(mx[:, :], sim, AX, ALU.max))
            dve.tensor_tensor(sim, sim, mx[:, :, None].to_broadcast([P, DC, DH]),
                              ALU.subtract).then_inc(m_dve, 1)
            dve.wait_ge(m_act, 16)
            step(dve.tensor_reduce(mx[:, :], sim, AX, ALU.add))
            step(dve.reciprocal(mx[:, :], mx[:, :]))
            for m in range(DC):
                for lo in (0, DH):
                    r = slice(lo, lo + DH)
                    dve.tensor_scalar(Abd[r, m, lo:lo + DH], sim[r, m, :], mx[r, m:m + 1], None,
                                      ALU.mult).then_inc(m_dve, 1)

            def a2_body(i):
                for s in range(2):
                    n = i * 2 + s
                    dve.wait_ge(a2_in[s], i * 16 + 16)
                    if not first(i):
                        dve.wait_ge(yn_turned, i * 2 + (s - 1))
                    dve.tensor_scalar(xn[:, s, :], xt[:, s, :], mean1[:, ds(n, 1)], rstd1[:, ds(n, 1)],
                                      ALU.subtract, ALU.mult).then_inc(yn_made, 1)
                for s in range(2):
                    n = i * 2 + s
                    dve.wait_ge(mix_summed, n + 1)
                    dve.scalar_tensor_tensor(
                        out=acc[:, ds(n, 1), :].rearrange("p a d -> p (a d)"), in0=bank[2 + s][:, :],
                        scalar=l2s[:, ds(n, 1)], in1=xt[:, s, :], op0=ALU.mult, op1=ALU.add).then_inc(acc_set, 1)
            rounds(dve, NT // 2, a2_body)
            dve.wait_ge(acc_set, NT)

            dve.wait_ge(iota_t, 1)
            dve.wait_ge(ecol_made, 1)
            step(dve.tensor_copy(ecol[:, :], bank[0][0:NT, 0:1]))
            dve.tensor_scalar(maskT[0:NT, :], iotaT[0:NT, :], ecol[:, 0:1], None, ALU.is_ge).then_inc(mask_made, 1)
            dve.wait_ge(wt_summed, 1)
            for c0 in range(0, ET, BANK):
                n = min(BANK, ET - c0)
                step(dve.tensor_scalar(wt_i[:, c0:c0 + n], bank[1 + c0 // BANK][0:1, 0:n], float(NT - 1), float(D),
                                       ALU.min, ALU.mult))
            dve.wait_ge(recs_in, 16)

            def onehots(i, h):
                for k in range(4):
                    s = h * 4 + k
                    t = i * 8 + s
                    if not first(i):
                        dve.wait_ge(msg_summed, i * 8 + (s - 7))
                    dve.tensor_scalar(oh[:, s, :], iota_f[:, :], recs[:, ds(t, 1), 1], recs[:, ds(t, 1), 2],
                                      ALU.is_equal, ALU.mult).then_inc(oh_made, 1)

            def adds(i, h, back=0):
                for k in range(4):
                    s = h * 4 + k
                    t = i * 8 + (s - back)
                    off = dve.value_load(wt_i[0:1, ds(t, 1)], min_val=0, max_val=(NT - 1) * D)
                    dve.wait_ge(msg_summed, t + 1)
                    if not (isinstance(t, int) and t == 0):
                        dve.wait_ge(acc_added, t)
                    dve.tensor_tensor(arena[:, ds(off, D)], arena[:, ds(off, D)], bank[s][:, :],
                                      ALU.add).then_inc(acc_added, 1)

            def c_body(i):
                onehots(i, 0)
                if not first(i):
                    adds(i, 1, 8)
                onehots(i, 1)
                adds(i, 0)
            rounds(dve, ET // 8, c_body)
            adds(ET // 8, 1, 8)
            dve.wait_ge(acc_added, ET)

            def s2_body(i):
                for k in range(4):
                    t = i * 4 + k
                    step2 = dve.bn_stats(stat2[:, ds(t, 1), :].rearrange("p a s -> p (a s)"),
                                         acc[:, ds(t, 1), :].rearrange("p a d -> p (a d)"))
                    step2.then_inc(stat_read, 1)
            rounds(dve, NT // 4, s2_body)
            dve.wait_ge(stat_read, 2 * NT)
            moments(stat2, mean2[:, :], sB[:, :], sA[:, :], nb2[:, :])
            dve.sem_inc(var2_made, 1)
            dve.wait_ge(sd2_made, 1)
            step(dve.reciprocal(rstd2[:, :], sA[:, :]))
            step(dve.scalar_tensor_tensor(out=nb2[:, :], in0=mean2[:, :], scalar=-1.0, in1=rstd2[:, :],
                                          op0=ALU.mult, op1=ALU.mult))

            def top_body(i):
                step.round(i, 4)
                for s in range(2):
                    t = i * 2 + s
                    if not first(i):
                        dve.wait_ge(xs_turned, i * 2 + (s - 1))
                    dve.tensor_scalar(xs2[:, s, :], acc[:, ds(t, 1), :].rearrange("p a d -> p (a d)"),
                                      mean2[:, ds(t, 1)], rstd2[:, ds(t, 1)], ALU.subtract,
                                      ALU.mult).then_inc(xs_made, 1)
                for s in range(2):
                    t = i * 2 + s
                    hold(dve, L_made, t + 1, dve_passed)
                    step(dve.max(m8[:, s, :], bank[2 + s][:, 0:NX]))
                    dve.sem_inc(dve_passed, 1)
                    step(dve.max_index(i8[:, s, :], m8[:, s, :], bank[2 + s][:, 0:NX]))
                    dve.tensor_copy(top[:, :, ds(t, 1)], m8[:, s, 0:2][:, :, None]).then_inc(top_made, 1)
                    dve.tensor_copy(topi[:, :, ds(t, 1)], i8[:, s, 0:2][:, :, None]).then_inc(top_made, 1)
                dve.wait_ge(top_made, i * 4 + 4)
            rounds(dve, NT // 2, top_body)
            step.end(NT // 2)

            dve.wait_ge(L_made, NT)
            step(dve.tensor_tensor(sB[:, :], top[:, 1, :], top[:, 0, :], ALU.subtract))
            dve.tensor_tensor(L, L, top[:, 0, :][:, :, None].to_broadcast([P, NT, NX]),
                              ALU.subtract).then_inc(lsub_made, 1)
            io32 = iota_f[:, None, 0:NX].to_broadcast([P, NT, NX])
            for j in range(2):
                dve.tensor_tensor(OHA[:, j, :].rearrange("p (t e) -> p t e", e=NX),
                                  topi[:, j, :][:, :, None].to_broadcast([P, NT, NX]), io32,
                                  ALU.is_equal).then_inc(oha_made, 1)
            dve.wait_ge(exp_made, 2)
            step(dve.tensor_reduce(sA[:, :], L, AX, ALU.add))
            step(dve.reciprocal(wts[:, 0, :], sA[:, :]))
            step(dve.tensor_tensor(wts[:, 1, :], wts[:, 1, :], wts[:, 0, :], ALU.mult))
            step(dve.tensor_tensor(sA[:, :], wts[:, 0, :], wts[:, 1, :], ALU.add))
            step(dve.tensor_scalar(sA[:, :], sA[:, :], 1e-9, None, ALU.max))
            step(dve.reciprocal(sA[:, :], sA[:, :]))
            step(dve.tensor_tensor(wts[:, :, :], wts[:, :, :], sA[:, None, :].to_broadcast([P, 2, NT]), ALU.mult))
            dve.wait_ge(T_made, 4)
            step(dve.memset(Pfx, 0.0))
            for e in range(NX):
                dve.tensor_tensor_scan(Cin[:, :, e], Tsb[:, :, e], v3(Pfx, NT)[:, :, e], 0.0, ALU.add,
                                       ALU.add).then_inc(lsub_made, 1)
            dve.wait_ge(lsub_made, 1 + NX)
            step(dve.tensor_tensor(Cin, Cin, Tsb, ALU.subtract))
            for m in range(4):
                step(dve.tensor_tensor(Pfx[:, m * 512:(m + 1) * 512], bank[m][:, :],
                                       Cin[:, 16 * m:16 * m + 16, :].rearrange("p a b -> p (a b)"), ALU.add))
            for j in range(2):
                step(dve.tensor_tensor(prd, OHA[:, j, :], Pfx, ALU.mult))
                step(dve.tensor_reduce(rank[:, j, :], prd.rearrange("p (t e) -> p t e", e=NX), AX, ALU.add))
            step(dve.scalar_tensor_tensor(out=topi[:, :, :], in0=topi[:, :, :], scalar=float(CAP), in1=rank[:, :, :],
                                          op0=ALU.mult, op1=ALU.add))
            step(dve.tensor_scalar(rank[:, :, :], rank[:, :, :], float(CAP), None, ALU.is_lt))
            step(dve.tensor_tensor(wts[:, :, :], wts[:, :, :], rank[:, :, :], ALU.mult))
            step(dve.scalar_tensor_tensor(out=topi[:, :, :], in0=rank[:, :, :], scalar=-FAR, in1=topi[:, :, :],
                                          op0=ALU.mult, op1=ALU.add))
            step(dve.tensor_scalar(topi[:, :, :], topi[:, :, :], FAR, None, ALU.add))
            step(dve.tensor_copy(sidx[:, :, :], topi[:, :, :]))
            step(dve.tensor_scalar(gidx[:, :, :], topi[:, :, :], float(SLOTS - 1), None, ALU.min))
            step(dve.tensor_tensor(sA[:, :], wts[:, 0, :], wts[:, 1, :], ALU.add))
            step(dve.tensor_scalar(sA[:, :], sA[:, :], 1e-12, None, ALU.is_le))
            step(dve.tensor_tensor(ca[:, :], sA[:, :], rstd2[:, :], ALU.mult))
            step(dve.tensor_scalar(ca[:, :], ca[:, :], 1.0, None, ALU.add))
            step(dve.tensor_tensor(cb[:, :], sA[:, :], nb2[:, :], ALU.mult))
            dve.sem_inc(route_made, 1)

            def bias_add(i, s):
                for c in range(CT):
                    n = i * 2 * CT + (s * CT + c)
                    dve.wait_ge(e_down, n + 1)
                    if c == 0:
                        dve.wait_ge(w2_in[s], i * 32 + 32)
                        if not first(i):
                            dve.wait_ge(e_out[s], i * 16)
                    dve.tensor_tensor(osb[s][:, c, :], bank[6 + (s * CT + c) % 2][:, :], b2s[s],
                                      ALU.add).then_inc(e_o, 1)

            def e_body(i):
                for s in range(2):
                    for c in range(CT):
                        n = i * 2 * CT + (s * CT + c)
                        dve.wait_ge(e_turned, n + 1)
                        if c == 0 and not (first(i) and s == 0):
                            dve.wait_ge(e_up, i * 16 + s * 8)
                        dve.tensor_copy(bT[:, :, c * P:(c + 1) * P],
                                        v3(bank[(s * CT + c) % 2][:, :], DC)).then_inc(e_bT, 1)
                    if s == 1:
                        bias_add(i, 0)
                    elif not first(i):
                        for c in range(CT):
                            dve.wait_ge(e_down, i * 2 * CT + (c + 1 - CT))
                            if c == 0:
                                dve.wait_ge(w2_in[1], i * 32)
                                if last_two(i):
                                    dve.wait_ge(e_out[1], i * 16 - 16)
                            dve.tensor_tensor(osb[1][:, c, :], bank[6 + (CT + c) % 2][:, :], b2s[1],
                                              ALU.add).then_inc(e_o, 1)

            def last_two(i):
                return not (isinstance(i, int) and i < 2)
            e_body(0)
            e_body(1)
            with dve.Fori(2, NX // 2) as i:
                e_body(i)
            bias_add(NX // 2 - 1, 1)

            def f_body(i):
                step.round(i, 8)
                for k in range(4):
                    t = i * 4 + k
                    dve.wait_ge(xr_in[k], i * 16 + 16)
                    if not first(i):
                        dve.wait_ge(fin_out[k], i * 16)
                    step(dve.tensor_scalar(fin[:, k, :], xr[:, k, :], ca[:, ds(t, 1)], cb[:, ds(t, 1)], ALU.mult,
                                           ALU.add))
                    dve.wait_ge(og_in[k], i * 32 + 32)
                    step(dve.scalar_tensor_tensor(out=fin[:, k, :], in0=ring[:, 2 * k, :],
                                                  scalar=wts[:, 0, ds(t, 1)], in1=fin[:, k, :],
                                                  op0=ALU.mult, op1=ALU.add))
                    dve.scalar_tensor_tensor(out=fin[:, k, :], in0=ring[:, 2 * k + 1, :],
                                             scalar=wts[:, 1, ds(t, 1)], in1=fin[:, k, :],
                                             op0=ALU.mult, op1=ALU.add).then_inc(fin_made, 1)
            rounds(dve, NT // 4, f_body)
            step.end(NT // 4)

        @block.tensor
        def _(pe):
            def mm(o_, l_, r_, start, stop, **kw):
                return nc.tensor.matmul(o_, l_, r_, start=start, stop=stop, **kw)

            def turn(o_, in_):
                return nc.tensor.transpose(o_, in_, ident[:, :])

            pe.wait_ge(const_made, NCONST)
            for c in range(CH):
                mm(bank[c][:, 0:P], zero_b[:, :], zero_b[:, :], True, False, skip_group_check=True)

            def tot_body(i):
                for c in range(CH):
                    g = i * CH + c
                    pe.wait_ge(oh_built, g + 1)
                    mm(bank[c][:, :], ones_b[:, :], oh_all[:, ds(g * 512, 512)], False, False,
                       skip_group_check=True)
            rounds(pe, 2 * BR, tot_body)
            for c in range(CH):
                last = mm(bank[c][:, 0:P], zero_b[:, :], zero_b[:, :], False, True, skip_group_check=True)
            last.then_inc(totals_made, 1)
            pe.wait_ge(init_made, 1)
            for c in range(CH):
                mm(bank[4 + c][:, :], ident[:, :],
                   init_sb[:, c * KC:(c + 1) * KC, :].rearrange("p k w -> p (k w)"), True, False,
                   skip_group_check=True)

            def rank_body(i):
                for h in range(2):
                    for c in range(CH):
                        g = i * (2 * CH) + (h * CH + c)
                        mm(bank[4 + c][:, :], before[:, :], oh_all[:, ds(g * 512, 512)], False, True,
                           skip_group_check=True).then_inc(ranked, 1)
                    for c in range(CH):
                        g = i * (2 * CH) + (h * CH + c)
                        pe.wait_ge(rank_read, g + 1)
                        mm(bank[4 + c][:, :], notbefore[:, :], oh_all[:, ds(g * 512, 512)], False, True,
                           skip_group_check=True)
            rounds(pe, BR, rank_body)

            pe.wait_ge(gw_in, 16)
            for m in range(DC):
                for k in range(DC):
                    last = turn(bank[4 + m][:, k * P:(k + 1) * P], gwr[:, k, m * P:(m + 1) * P])
                last.then_inc(wt_tr, 1)
            pe.wait_ge(wt_made, DC)

            for m in range(DC):
                mm(bank[m][:, 0:P], zero_b[:, :], zero_b[:, :], True, False, skip_group_check=True)

            def a1_body(i):
                for s in range(2):
                    n = i * 2 + s
                    pe.wait_ge(xn_made, n + 1)
                    if not first(i):
                        pe.wait_ge(xT_made, i * 2 + (s - 1))
                    for m in range(DC):
                        last = turn(bank[4 + s][:, m * P:(m + 1) * P], xn[:, s, m * P:(m + 1) * P])
                    last.then_inc(xn_turned, 1)
                    pe.wait_ge(xh_made, n + 1)
                    for m in range(DC):
                        last = mm(bank[m][:, :], xh[:, s, m * P:(m + 1) * P], xh[:, s, :], False, False,
                                  skip_group_check=True)
                    last.then_inc(gram_done, 1)
                    pe.wait_ge(xT_made, n + 1)
                    if not first(i):
                        pe.wait_ge(h_made, i * 2 + (s - 1))
                    for m in range(DC):
                        last = mm(bank[6 + s][:, :], xT[:, s, m * P:(m + 1) * P], wT[:, m, :], m == 0, m == DC - 1)
                    last.then_inc(h_summed, 1)
            rounds(pe, NT // 2, a1_body)

            pe.wait_ge(qkv_scaled, DC)
            pe.wait_ge(h_made, NT)
            for m in range(DC):
                for k in range(DC):
                    last = turn(bank[4 + m][:, k * P:(k + 1) * P],
                                wqkv[:, k, 2 * D + m * P:2 * D + (m + 1) * P])
                last.then_inc(m_pe, 1)
            pe.wait_ge(m_act, 4)
            for m in range(DC):
                for k in range(DC):
                    last = mm(bank[m][:, :], G[:, k, m * P:(m + 1) * P], wqkv[:, k, D:2 * D], k == 0, k == DC - 1)
                last.then_inc(m_pe, 1)
            pe.wait_ge(m_act, 8)
            for m in range(DC):
                for k in range(DC):
                    last = mm(bank[4 + m][:, :], G[:, k, m * P:(m + 1) * P], wqkv[:, k, 0:D], k == 0, k == DC - 1)
                last.then_inc(m_pe, 1)
            pe.wait_ge(m_dve, 8)
            for m in range(DC):
                for k in range(DC):
                    mm(bank[4][:, m:m + 1], prq[:, k, m * P:(m + 1) * P], ones_f[:, 0:1], k == 0, k == DC - 1)
            for k in range(DC):
                last = mm(bank[5][:, :], ones_f[:, :], prk[:, k, :], k == 0, k == DC - 1)
            last.then_inc(m_pe, 1)
            pe.wait_ge(m_act, 12)
            for m in range(DC):
                for k in range(DC):
                    last = mm(bank[m][:, 0:P], wqkv[:, k, m * P:(m + 1) * P], Tk[:, k, m * P:(m + 1) * P],
                              k == 0, k == DC - 1)
                last.then_inc(m_pe, 1)
            pe.wait_ge(m_dve, 19)
            for m in range(DC):
                mm(bank[m][:, :], Abd[:, m, :], wout[:, m, :], True, True).then_inc(m_pe, 1)
            pe.wait_ge(m_act, 20)
            for m in range(DC):
                for k in range(DC):
                    last = mm(bank[4 + m][:, :], wvT[:, k, m * P:(m + 1) * P], Bm[:, k, :], k == 0, k == DC - 1)
                last.then_inc(m_pe, 1)
            pe.wait_ge(m_act, 24)

            def a2_body(i):
                for s in range(2):
                    n = i * 2 + s
                    pe.wait_ge(yn_made, n + 1)
                    if not first(i):
                        pe.wait_ge(yT_made, i * 2 + (s - 1))
                    for m in range(DC):
                        last = turn(bank[s][:, m * P:(m + 1) * P], xn[:, s, m * P:(m + 1) * P])
                    last.then_inc(yn_turned, 1)
                for s in range(2):
                    n = i * 2 + s
                    pe.wait_ge(yT_made, n + 1)
                    if not first(i):
                        pe.wait_ge(acc_set, i * 2 + (s - 1))
                    for m in range(DC):
                        last = mm(bank[2 + s][:, :], xT[:, s, m * P:(m + 1) * P], Msb[:, m, :], m == 0, m == DC - 1)
                    last.then_inc(mix_summed, 1)
            rounds(pe, NT // 2, a2_body)

            pe.wait_ge(acc_set, NT)
            pe.wait_ge(yT_made, NT)
            mm(bank[0][0:NT, 0:1], ends[0:1, :], ones_f[0:1, 0:1], True, True).then_inc(ecol_made, 1)
            pe.wait_ge(mask_made, 1)
            for c0 in range(0, ET, BANK):
                n = min(BANK, ET - c0)
                last = mm(bank[1 + c0 // BANK][0:1, 0:n], ones_f[0:NT, 0:1], maskT[0:NT, c0:c0 + n], True, True)
            last.then_inc(wt_summed, 1)

            def c_body(i):
                for s in range(8):
                    t = i * 8 + s
                    pe.wait_ge(oh_made, t + 1)
                    pe.wait_ge(row_in[s], i * 16 + 16)
                    if not first(i):
                        pe.wait_ge(acc_added, i * 8 + (s - 7))
                    mm(bank[s][:, :], oh[:, s, :], ring[:, s, :], True, True).then_inc(msg_summed, 1)
            rounds(pe, ET // 8, c_body)
            pe.wait_ge(acc_added, ET)

            pe.wait_ge(b1_in, 16)
            for m in range(DC):
                last = nc.tensor.transpose(bank[6][:, m * NX:(m + 1) * NX], b1_sb[:, m * P:(m + 1) * P],
                                           ident[0:NX, 0:NX])
            last.then_inc(b1_turned, 1)

            def d_body(i):
                for s in range(2):
                    n = i * 2 + s
                    pe.wait_ge(xs_made, n + 1)
                    if not first(i):
                        pe.wait_ge(xsT_made, i * 2 + (s - 1))
                    for m in range(DC):
                        last = turn(bank[s][:, m * P:(m + 1) * P], xs2[:, s, m * P:(m + 1) * P])
                    last.then_inc(xs_turned, 1)
                for s in range(2):
                    n = i * 2 + s
                    pe.wait_ge(xsT_made, n + 1)
                    if not first(i):
                        pe.wait_ge(top_made, i * 4)
                        pe.wait_ge(L_made, i * 2 + (s - 1))
                    for m in range(DC):
                        last = mm(bank[2 + s][:, 0:NX], xT2[:, s, m * P:(m + 1) * P], wg_sb[:, m, :],
                                  m == 0, m == DC - 1)
                    last.then_inc(gated, 1)
            rounds(pe, NT // 2, d_body)
            pe.wait_ge(oha_made, 2)
            pe.wait_ge(L_made, NT)
            pe.wait_ge(top_made, 2 * NT)
            pe.wait_ge(b1T_made, 1)
            for m in range(4):
                for j in range(2):
                    mm(bank[m][:, :], before[:, :], OHA[:, j, m * 512:(m + 1) * 512], j == 0, j == 1)
                for j in range(2):
                    last = mm(bank[4 + m][:, :], ones_b[:, :], OHA[:, j, m * 512:(m + 1) * 512], j == 0, j == 1)
            last.then_inc(pfx_made, 1)
            pe.wait_ge(route_made, 1)
            pe.wait_ge(T_made, 4)

            def down(i, s):
                w = s % 2
                for c in range(CT):
                    if c == 0:
                        pe.wait_ge(w2_in[w], i * 32 + (0 if s < 0 else 32))
                        pe.wait_ge(e_h, i * 16 + (s + 1) * 8)
                    n = i * 2 * CT + (s * CT + c)
                    if not (isinstance(n, int) and n < 2):
                        pe.wait_ge(e_o, n - 1)
                    for k in range(DC):
                        last = mm(bank[6 + (w * CT + c) % 2][:, :], hT[:, k, c * P:(c + 1) * P], w2s[w][:, k, :],
                                  k == 0, k == DC - 1)
                    last.then_inc(e_down, 1)

            def e_body(i):
                for s in range(2):
                    pe.wait_ge(bin_in[s], i * 16 + 16)
                    for c in range(CT):
                        n = i * 2 * CT + (s * CT + c)
                        if not (isinstance(n, int) and n < 2):
                            pe.wait_ge(e_bT, n - 1)
                        for k in range(DC):
                            last = turn(bank[(s * CT + c) % 2][:, k * P:(k + 1) * P],
                                        bin_[s][:, c, k * P:(k + 1) * P])
                        last.then_inc(e_turned, 1)
                    if not (first(i) and s == 0):
                        down(i, s - 1)
                    pe.wait_ge(w1_in[s], i * 16 + 16)
                    pe.wait_ge(e_bT, i * 2 * CT + (s + 1) * CT)
                    for g in range(8):
                        hc, hf = g // 2, g % 2
                        n = i * 16 + (s * 8 + g)
                        if not (isinstance(n, int) and n < 4):
                            pe.wait_ge(e_h, n - 3)
                        for k in range(DC):
                            last = mm(bank[2 + g % 4][:, 0:HN], w1s[s][:, k, hc * P:(hc + 1) * P],
                                      bT[:, k, hf * HN:(hf + 1) * HN], k == 0, k == DC - 1)
                        last.then_inc(e_up, 1)
            rounds(pe, NX // 2, e_body)
            down(NX // 2 - 1, 1)


_INS = ['x', 'src', 'dst', 'edge_weight', 'L0_gnn_weight', 'L0_mix_gamma', 'L0_mix_w_qkv', 'L0_mix_temperature',
        'L0_mix_w_out', 'L0_ffn_Wg', 'L0_ffn_W1', 'L0_ffn_b1', 'L0_ffn_W2', 'L0_ffn_b2']


def kernel(**inputs):
    import numpy as _np
    import concourse.bacc as _bacc
    from concourse import mybir as _mybir
    from concourse.bass_utils import run_bass_kernel_spmd as _run

    nc = _bacc.Bacc("TRN2", target_bir_lowering=False, num_devices=1)
    arrays, args = {}, []
    for name in _INS:
        a = _np.ascontiguousarray(inputs[name])
        arrays[f"in_{name}"] = a
        args.append(nc.dram_tensor(f"in_{name}", a.shape, _mybir.dt.from_np(a.dtype), kind="ExternalInput").ap())
    shape = tuple(inputs['x'].shape)
    args.append(nc.dram_tensor("out_rows", shape, _mybir.dt.float32, kind="ExternalOutput").ap())
    build(nc, *args)
    r = _run(nc, [arrays], core_ids=[0])
    return r.results[0]["out_rows"]
```

```python
import concourse.bass as bass
from concourse import mybir
from contextlib import ExitStack
import math

P = 128
BANK = 512
D = 512
DC = D // P


class Chain:

    def __init__(self, eng, sem, passed=None):
        self.eng, self.sem, self.base, self.k, self.i, self.per = eng, sem, 0, 0, 0, 0
        self.passed = passed

    def at(self):
        return self.i * self.per + (self.base + self.k)

    def __call__(self, ins):
        ins.then_inc(self.sem, 1)
        self.k += 1
        self.eng.wait_ge(self.sem, self.at())
        if self.passed is not None and not isinstance(self.at(), int):
            self.eng.sem_inc(self.passed, 1)

    def round(self, i, per):
        if isinstance(i, int) and i == 0:
            self.base, self.k = self.base + self.k, 0
        else:
            assert self.k == per, (self.k, per)
        self.i, self.per, self.k = i, per, 0

    def end(self, n):
        assert self.k == self.per, (self.k, self.per)
        self.base, self.k, self.i, self.per = self.base + n * self.per, 0, 0, 0


def hold(eng, sem, value, passed):
    eng.wait_ge(sem, value)
    eng.sem_inc(passed, 1)


def rounds(eng, n, body):
    body(0)
    with eng.Fori(1, n) as i:
        body(i)


def lagged(eng, n, body, after):
    body(0)
    body(1)
    after(0)
    with eng.Fori(2, n) as q:
        body(q)
        after(q - 1)
    after(n - 1)


def first(i):
    return isinstance(i, int) and i == 0


def build(nc, x, src, dst, edge_w, gnn_w, gamma, w_qkv, temp, w_out, Wg, W1, b1, W2, b2, out):
    f32, bf16, i32, u32 = mybir.dt.float32, mybir.dt.bfloat16, mybir.dt.int32, mybir.dt.uint32
    f32r = mybir.dt.float32r
    ALU, ACT, AX = mybir.AluOpType, mybir.ActivationFunctionType, mybir.AxisListType.X
    ds = bass.ds

    N = x.shape[0]
    NT = N // P
    E = src.shape[0]
    EC = E // P
    ET = EC + NT
    KC = 8
    HG = 4
    HC = HG * KC
    NB = EC // HC
    EARLY = 2
    HEADS, DH, SCALE = 8, 64, 8.0
    LN_EPS, L2_EPS = 1e-5, 1e-12
    NX = Wg.shape[1]
    CAP = int(math.ceil(1.25 * 2 * N / NX))
    CT = CAP // P
    HN = CAP // 2
    SLOTS = NX * CAP
    TQ = 16
    TG = BANK // P
    NG = TQ // TG
    NQ = NT // TQ
    FAR = 65536.0

    H_d = nc.dram_tensor("h_rows", (N, D), f32, kind="Internal").ap()
    rec_d = nc.dram_tensor("edge_records", (P * ET, 4), f32, kind="Internal").ap()
    x1_d = nc.dram_tensor("x1_rows", (N, D), f32, kind="Internal").ap()
    zr = -(-SLOTS // (P * (NB - EARLY)))
    buf_all = nc.dram_tensor("expert_in", (P * zr * (NB - EARLY), D), f32, kind="Internal").ap()
    buf_d = buf_all[0:SLOTS, :]
    o_d = nc.dram_tensor("expert_out", (SLOTS, D), f32, kind="Internal").ap()

    ctx = ExitStack()
    with ctx:
        def sb(name, shape, dt):
            return ctx.enter_context(nc.sbuf_tensor(name, shape, dt))

        def sem(name):
            return ctx.enter_context(nc.semaphore(name))

        work = sb("work", [P, 14336], f32)
        with nc.sbuf_tensor("arena", [P, NT * D], f32) as arena, nc.sbuf_tensor("ring", [P, 8, D], f32) as ring:
            pass
        sets = ctx.enter_context(ExitStack())

        def late(name, shape, dt):
            return sets.enter_context(nc.sbuf_tensor(name, shape, dt))

        w1h, w1l, w2h, w2l = ([late(f"{name}_{k}", [P, DC, D], f32r) for k in range(2)]
                              for name in ("w1_high", "w1_low", "w2_high", "w2_low"))
        bTh, bTl, hTh, hTl = (late(name, [P, DC, CAP], f32r)
                              for name in ("rows_high", "rows_low", "hidden_high", "hidden_low"))
        bin_, osb = ([late(f"{name}_{k}", [P, CT, D], f32) for k in range(2)] for name in ("rows_in", "rows_out"))

        def cut(t, at, n):
            return t[:, at:at + n]

        def v3(t, a):
            return t.rearrange("p (a b) -> p a b", a=a)

        acc = v3(arena[:, :], NT)
        oh_all = arena[:, :].bitcast(bf16)
        src_i = cut(work, 0, EC).bitcast(i32)
        srcl_f = cut(work, 0, EC)
        dst_i = cut(work, EC, EC).bitcast(i32)
        w_f = cut(work, 2 * EC, EC)
        tmp_i = cut(work, 3 * EC, EC).bitcast(i32)
        addr_all = cut(work, 3 * EC, EC).bitcast(u32)
        win_bf = cut(work, 4 * EC, EC // 2).bitcast(bf16)
        o_rec = 4 * EC + EC // 2
        recs_flat = cut(work, o_rec, 4 * ET)
        recs = v3(recs_flat, ET)
        recs_i = v3(recs_flat.bitcast(u32), ET)
        o_wT = o_rec + 4 * ET
        wT = v3(cut(work, o_wT, 2048), DC)
        o_M = o_wT + 2048
        Msb = v3(cut(work, o_M, 2048), DC)
        o_h = o_M + 2048
        h_sb = v3(cut(work, o_h, 1024), 2)
        assert o_h + 1024 <= 14336
        tot_sb = v3(cut(work, o_M, 512), KC)
        init_sb = v3(cut(work, o_wT, 512), KC)
        prod = v3(cut(work, o_M, 1024), 2)
        zrow = cut(work, o_M + 1024, D)
        gwr = v3(cut(work, o_rec, 2048), DC)
        stat1 = cut(work, o_h, NT * 6).rearrange("p (t s) -> p t s", s=6)
        xt, xn, xh, xT = (ring[:, 2 * k:2 * k + 2, :] for k in range(4))
        o = 0
        wqkv = v3(cut(arena, o, 6144), DC); o += 6144
        wout = v3(cut(arena, o, 2048), DC); o += 2048
        G = v3(cut(arena, o, 2048), DC); o += 2048
        Tk = v3(cut(arena, o, 2048), DC); o += 2048
        prk = v3(cut(arena, o, 2048), DC); o += 2048
        prq = v3(cut(arena, o, 2048), DC); o += 2048
        wvT = v3(cut(arena, o, 2048), DC); o += 2048
        Bm = v3(cut(arena, o, 2048), DC); o += 2048
        kinv = cut(arena, o, 512); o += 512
        sim = v3(cut(arena, o, 256), DC); o += 256
        Abd = v3(cut(arena, o, 512), DC); o += 512
        oh = v3(cut(work, o_wT, 1024), 8)
        iotaT = cut(work, 0, ET)
        maskT = cut(work, ET, ET)
        wt_i = cut(work, 2 * ET, ET)[0:1, :].bitcast(i32)
        o = 8192
        L = v3(cut(work, o, NT * NX), NT); o += NT * NX
        Lx, eq = (v3(cut(work, o + k * 512, 512), TQ) for k in range(2)); o += 1024
        Pfx = Lx
        OHA = v3(cut(work, o, 512).bitcast(bf16), 2); o += 512
        assert o <= 12288
        lt = v3(cut(work, 5120, 2 * TG * P), 2)[0:NX, :, :]
        Cx = v3(cut(work, 13568, (TQ + 1) * NX), TQ + 1)
        stat2 = cut(work, 14112, TQ * 6).rearrange("p (t s) -> p t s", s=6)
        wts, sidx, gidx = (v3(cut(work, 12288 + k * 2 * NT, 2 * NT), 2) for k in range(3))
        sidx, gidx = sidx.bitcast(u32), gidx.bitcast(u32)
        small = [v3(cut(work, 12672 + k * 2 * TQ, 2 * TQ), 2) for k in range(2)]
        tops, share, tmp2 = (v3(cut(work, 12736 + k * 2 * NT, 2 * NT), 2) for k in range(3))
        xT4 = [ring[:, 4 * k:4 * k + 4, :] for k in range(2)]
        w1f, w2f = (v3(cut(work, k * 2048, 2048), DC) for k in range(2))
        b2s = [cut(work, 4096 + k * D, D) for k in range(2)]
        h_st = v3(cut(work, 5120, 4 * HN), 4)
        xr = v3(cut(work, 6400, 2048), 4)
        fin = v3(cut(work, 8448, 2048), 4)
        b1_sb = cut(work, o_h, D)[0:NX, :]

        ident = sb("ident", [P, P], f32)
        ones_f = sb("ones_f", [P, P], f32)
        iota_f = sb("iota_f", [P, P], f32)
        before = sb("before", [P, P], bf16)
        notbefore = sb("notbefore", [P, P], bf16)
        ones_b = sb("ones_b", [P, P], bf16)
        zero_b = sb("zero_b", [P, P], bf16)
        iota_b = sb("iota_b", [P, NT], bf16)
        eps = sb("eps", [P, 2], f32)
        mean1 = sb("mean1", [P, NT], f32)
        rstd1 = sb("rstd1", [P, NT], f32)
        l2s = sb("l2s", [P, NT], f32)
        xhs = sb("xhs", [P, NT], f32)
        sA = sb("sA", [P, NT], f32)
        sB = sb("sB", [P, NT], f32)
        addr_st = sb("addr_st", [P, 2, HC], u32)
        rec_st = sb("rec_st", [P, 2, HC, 4], f32)
        idx_st = sb("idx_st", [P, 2, 4], u32)
        ends = sb("ends", [P, NT], f32)
        wtot = sb("wtot", [P, NT], f32)
        nt_i = sb("nt_i", [P, NT], i32)
        ecol = sb("ecol", [NT, 1], f32)
        gcol = sb("gcol", [P, DC], f32)
        tcol = sb("tcol", [P, DC], f32)
        qs = sb("qs", [P, DC], f32)
        mx = sb("mx", [P, DC], f32)
        wg_sb = sb("wg_sb", [P, DC, NX], f32)
        b1T = sb("b1T", [P, DC, NX], f32)
        rt_st = sb("rt_st", [P, 2, 4], u32)
        rk_f = sb("rk_f", [P, HC], f32)
        rk_i = sb("rk_i", [P, 2 * HC], i32)
        rev = cut(work, 14208, NX)
        mean2, rstd2, nb2, ca, cb = mean1, rstd1, l2s, xhs, ends

        bank = [ctx.enter_context(nc.psum_tensor(f"bank{k}", [P, BANK], f32)) for k in range(8)]

        const_made = sem("const_made")
        fill_made = sem("fill_made")
        pool_step = sem("pool_step")
        dve_step = sem("dve_step")
        norm_step = sem("norm_step")
        route_step = sem("route_step")
        pool_passed = sem("pool_passed")
        dve_passed = sem("dve_passed")
        act_passed = sem("act_passed")
        edges_in = sem("edges_in")
        rec_filled = sem("rec_filled")
        buf_filled = sem("buf_filled")
        xs_in = [sem(f"xs_in{k}") for k in range(8)]
        stat_read = sem("stat_read")
        var_made = sem("var_made")
        sd_made = sem("sd_made")
        oh_built = sem("oh_built")
        totals_made = sem("totals_made")
        init_made = sem("init_made")
        ecol_made = sem("ecol_made")
        ranked = sem("ranked")
        rank_read = sem("rank_read")
        addr_made = sem("addr_made")
        scat = [sem(f"scat{k}") for k in range(2)]
        gw_in = sem("gw_in")
        qkv_in = sem("qkv_in")
        wt_tr = sem("wt_tr")
        wt_made = sem("wt_made")
        a1_in = [sem(f"a1_in{k}") for k in range(2)]
        xn_made = sem("xn_made")
        xh_made = sem("xh_made")
        xn_turned = sem("xn_turned")
        xT_made = sem("xT_made")
        gram_done = sem("gram_done")
        h_summed = sem("h_summed")
        h_made = sem("h_made")
        h_out = [sem(f"h_out{k}") for k in range(2)]
        qkv_scaled = sem("qkv_scaled")
        m_pe = sem("m_pe")
        m_act = sem("m_act")
        m_dve = sem("m_dve")
        a2_in = [sem(f"a2_in{k}") for k in range(2)]
        yn_made = sem("yn_made")
        yn_turned = sem("yn_turned")
        yT_made = sem("yT_made")
        mix_summed = sem("mix_summed")
        acc_set = sem("acc_set")
        recs_in = sem("recs_in")
        idx_made = sem("idx_made")
        iota_t = sem("iota_t")
        mask_made = sem("mask_made")
        wt_summed = sem("wt_summed")
        row_in = [sem(f"row_in{k}") for k in range(8)]
        oh_made = sem("oh_made")
        msg_summed = sem("msg_summed")
        acc_added = sem("acc_added")
        x1_out = [sem(f"x1_out{k}") for k in range(2)]
        var2_made = sem("var2_made")
        sd2_made = sem("sd2_made")
        xs_made = sem("xs_made")
        xs_turned = sem("xs_turned")
        xsT_made = sem("xsT_made")
        gated = sem("gated")
        L_made = sem("L_made")
        small_in = sem("small_in")
        b1_in = sem("b1_in")
        b1_turned = sem("b1_turned")
        b1T_made = sem("b1T_made")
        lsub_made = sem("lsub_made")
        x1b_made = sem("x1b_made")
        exp_made = sem("exp_made")
        oha_made = sem("oha_made")
        pfx_made = sem("pfx_made")
        route_made = sem("route_made")
        sent = sem("sent")
        norm2_made = sem("norm2_made")
        lt_made = sem("lt_made")
        turned_back = sem("turned_back")
        bin_in = [sem(f"bin_in{k}") for k in range(2)]
        w1_in = sem("w1_in")
        w2_in = sem("w2_in")
        b2_in = [sem(f"b2_in{k}") for k in range(2)]
        e_turned = sem("e_turned")
        e_bT = sem("e_bT")
        e_up = sem("e_up")
        e_h = sem("e_h")
        e_down = sem("e_down")
        e_o = sem("e_o")
        e_bTl = sem("e_bTl")
        e_hs = sem("e_hs")
        w1_high = sem("w1_high")
        w1_split = sem("w1_split")
        w2_high = sem("w2_high")
        w2_split = sem("w2_split")
        e_out = [sem(f"e_out{k}") for k in range(2)]
        og_in = [sem(f"og_in{k}") for k in range(4)]
        xr_in = [sem(f"xr_in{k}") for k in range(4)]
        fin_made = sem("fin_made")
        fin_out = [sem(f"fin_out{k}") for k in range(4)]

        x_t = x.rearrange("(t p) d -> t p d", p=P)
        ZR = -(-SLOTS // (P * (NB - EARLY)))
        buf_z = buf_all.rearrange("(k p r) d -> k p r d", p=P, r=ZR)
        H_t = H_d.rearrange("(t p) d -> t p d", p=P)
        x1_pt = x1_d.rearrange("(t p) d -> p t d", p=P)
        x1_t = x1_d.rearrange("(t p) d -> t p d", p=P)
        out_t = out.rearrange("(t p) d -> t p d", p=P)
        buf_e = buf_d.rearrange("(e c p) d -> e p c d", p=P, c=CT)
        o_e = o_d.rearrange("(e c p) d -> e p c d", p=P, c=CT)
        w1_e = W1.rearrange("e (c p) h -> e p c h", p=P)
        w2_e = W2.rearrange("e (c p) h -> e p c h", p=P)

        NCONST = 11
        block = ctx.enter_context(nc.Block())

        @block.sync
        def _(sp):
            for t_, s_ in ((src_i, src), (dst_i, dst), (w_f, edge_w)):
                sp.dma_start(t_, s_.rearrange("(p c) -> p c", p=P)).then_inc(edges_in, 16)

            sp.wait_ge(fill_made, 3)
            sp.dma_start(rec_d.rearrange("(q t) c -> q (t c)", q=P), recs_flat).then_inc(rec_filled, 16)

            def s_body(i):
                for k in range(8):
                    if not first(i):
                        sp.wait_ge(stat_read, i * 8 + (k - 7))
                    sp.dma_start(ring[:, k, :], x_t[i * 8 + k]).then_inc(xs_in[k], 16)
            rounds(sp, NT // 8, s_body)
            sp.wait_ge(rec_filled, 16)
            sp.dma_start(gwr, gnn_w.rearrange("(c p) f -> p c f", p=P)).then_inc(gw_in, 16)
            sp.wait_ge(stat_read, NT)

            def a1_body(i):
                for s in range(2):
                    if not first(i):
                        sp.wait_ge(xh_made, i * 2 + (s - 1))
                    sp.dma_start(xt[:, s, :], x_t[i * 2 + s]).then_inc(a1_in[s], 16)
                if not (isinstance(i, int) and i >= NB - EARLY):
                    sp.dma_start(buf_z[i], zrow[:, None, :].to_broadcast([P, ZR, D])).then_inc(buf_filled, 16)
                if first(i):
                    sp.dma_start(wg_sb[:, :, :], Wg.rearrange("(c p) e -> p c e", p=P)).then_inc(small_in, 16)
                    with nc.allow_non_contiguous_dma(reason="small"):
                        sp.dma_start(gcol[:, :], gamma.rearrange("(c p) -> p c", p=P)).then_inc(small_in, 16)
                        t2 = temp.rearrange("(c two) a b -> two c (a b)", two=2)
                        for hh in range(2):
                            tv = t2[hh].rearrange("c b -> b c")
                            sp.dma_start(tcol[hh * 64:hh * 64 + 64, :],
                                         tv.to_broadcast([64, DC])).then_inc(small_in, 16)
            rounds(sp, NB - EARLY, a1_body)
            sp.wait_ge(rank_read, HG * NB)
            sp.dma_start(wqkv, w_qkv.rearrange("(c p) f -> p c f", p=P)).then_inc(qkv_in, 16)
            sp.dma_start(wout, w_out.rearrange("(c p) f -> p c f", p=P)).then_inc(qkv_in, 16)
            for i in range(NB - EARLY, NT // 2):
                a1_body(i)

            sp.wait_ge(xh_made, NT)

            def a2_body(i):
                for s in range(2):
                    if not first(i):
                        sp.wait_ge(acc_set, i * 2 + (s - 1))
                    sp.dma_start(xt[:, s, :], x_t[i * 2 + s]).then_inc(a2_in[s], 16)
            rounds(sp, NT // 2, a2_body)

            for k in range(2):
                sp.wait_ge(scat[k], 16 * HC * (NB // 2))
            sp.dma_start(recs_flat, rec_d.rearrange("(q t) c -> q (t c)", q=P)).then_inc(recs_in, 16)

            for k in range(2):
                sp.wait_ge(h_out[k], 16 * (NT // 2))
            sp.dma_start(b1_sb, b1[:, :]).then_inc(b1_in, 16)

            sp.wait_ge(acc_added, ET)
            HQ = TQ // 2
            for q in range(NQ):
                for h in range(2):
                    if q > 0:
                        sp.wait_ge(x1_out[h], q * 16)
                    t = q * TQ + h * HQ
                    sp.dma_start(x1_pt[:, t:t + HQ, :], acc[:, t:t + HQ, :]).then_inc(x1_out[h], 16)

            sp.dma_start(w1f, w1_e[0]).then_inc(w1_in, 16)
            sp.dma_start(w2f, w2_e[0]).then_inc(w2_in, 16)
            sp.dma_start(b2s[0], b2[0:1, :].to_broadcast([P, D])).then_inc(b2_in[0], 16)
            sp.wait_ge(sent, 32 * NT)
            for h in range(2):
                sp.wait_ge(x1_out[h], 16 * NQ)

            def e_body(i):
                for s in range(2):
                    e = i * 2 + s
                    if not first(i):
                        sp.wait_ge(e_turned, i * 2 * CT + (s - 1) * CT)
                    sp.dma_start(bin_[s][:, :, :], buf_e[e]).then_inc(bin_in[s], 16)
                    if not (first(i) and s == 0):
                        sp.wait_ge(w1_split, i * 2 * DC + s * DC)
                        sp.dma_start(w1f, w1_e[e]).then_inc(w1_in, 16)
                        sp.wait_ge(w2_split, i * 2 * DC + s * DC)
                        sp.dma_start(w2f, w2_e[e]).then_inc(w2_in, 16)
                        if not first(i):
                            sp.wait_ge(e_o, i * 2 * CT + (s - 1) * CT)
                        sp.dma_start(b2s[s], b2[ds(e, 1), :].to_broadcast([P, D])).then_inc(b2_in[s], 16)
                    if not (first(i) and s == 0):
                        sp.wait_ge(e_o, i * 2 * CT + s * CT)
                        sp.dma_start(o_e[i * 2 + (s - 1)], osb[1 - s][:, :, :]).then_inc(e_out[1 - s], 16)
            rounds(sp, NX // 2, e_body)
            sp.wait_ge(e_o, NX * CT)
            sp.dma_start(o_e[NX - 1], osb[1][:, :, :]).then_inc(e_out[1], 16)

            def f_body(i):
                for k in range(4):
                    if not first(i):
                        sp.wait_ge(fin_made, i * 4 + (k - 3))
                    sp.dma_start(xr[:, k, :], x1_t[i * 4 + k]).then_inc(xr_in[k], 16)
                for k in range(4):
                    sp.wait_ge(fin_made, i * 4 + (k + 1))
                    sp.dma_start(out_t[i * 4 + k], fin[:, k, :]).then_inc(fin_out[k], 16)
            rounds(sp, NT // 4, f_body)
            for k in range(4):
                sp.wait_ge(fin_out[k], 16 * (NT // 4))

        @block.gpsimd
        def _(pool):
            step = Chain(pool, pool_step, pool_passed)
            step(pool.memset(ident[:, :], 0.0))
            step(pool.memset(ones_b[:, :], 1.0))
            pool.affine_select(out=ident[:, :], in_=ident[:, :], compare_op=ALU.not_equal, fill=1.0, base=0,
                               pattern=[[-1, P]], channel_multiplier=1).then_inc(const_made, 1)
            pool.affine_select(out=before[:, :], in_=ones_b[:, :], compare_op=ALU.is_gt, fill=0.0, base=0,
                               pattern=[[1, P]], channel_multiplier=-1).then_inc(const_made, 1)
            pool.affine_select(out=notbefore[:, :], in_=ones_b[:, :], compare_op=ALU.is_ge, fill=0.0, base=0,
                               pattern=[[-1, P]], channel_multiplier=1).then_inc(const_made, 1)
            pool.memset(ones_f[:, :], 1.0).then_inc(const_made, 1)
            pool.memset(zero_b[:, :], 0.0).then_inc(const_made, 1)
            pool.memset(eps[:, 0:1], LN_EPS).then_inc(const_made, 1)
            pool.memset(eps[:, 1:2], 0.0).then_inc(const_made, 1)
            pool.iota(iota_b[:, :], [[1, NT]], base=0, channel_multiplier=0,
                      allow_small_or_imprecise_dtypes=True).then_inc(const_made, 1)
            pool.iota(iota_f[:, :], [[1, P]], base=0, channel_multiplier=0,
                      allow_small_or_imprecise_dtypes=True).then_inc(const_made, 1)
            pool.memset(rec_st[:, :, :, :], 0.0).then_inc(const_made, 1)
            pool.memset(b1T[:, :, :], 0.0).then_inc(const_made, 1)
            pool.memset(recs_flat, 0.0).then_inc(fill_made, 1)
            pool.wait_ge(fill_made, 1)
            pool.memset(recs[:, :, 1:2], -1.0).then_inc(fill_made, 1)
            pool.memset(zrow, 0.0).then_inc(fill_made, 1)
            pool.iota(rev[:, :], [[-1, NX]], base=NX, channel_multiplier=0,
                      allow_small_or_imprecise_dtypes=True).then_inc(fill_made, 1)

            pool.wait_ge(rec_filled, 16)

            def b_body(i):
                step.round(i, 8)
                for h in range(2):
                    if not first(i):
                        pool.wait_ge(scat[h], i * (16 * HC))
                    pool.wait_ge(addr_made, i * 2 + (h + 1))
                    c0 = i * (2 * HC) + h * HC
                    step(pool.tensor_copy(addr_st[:, h, :], addr_all[:, ds(c0, HC)]))
                    step(pool.tensor_copy(rec_st[:, h, :, 0].bitcast(i32), dst_i[:, ds(c0, HC)]))
                    step(pool.tensor_copy(rec_st[:, h, :, 1], srcl_f[:, ds(c0, HC)]))
                    step(pool.tensor_copy(rec_st[:, h, :, 2], w_f[:, ds(c0, HC)]))
                    for c in range(HC):
                        pool.indirect_dma_start(
                            rec_d, bass.IndirectOffsetOnAxis(addr_st[:, h, c:c + 1], 0),
                            rec_st[:, h, c, :], None).then_inc(scat[h], 16)
            rounds(pool, NB // 2, b_body)
            step.end(NB // 2)

            for k in range(2):
                pool.wait_ge(scat[k], 16 * HC * (NB // 2))
            pool.iota(iotaT, [[1, ET]], base=0, channel_multiplier=0,
                      allow_small_or_imprecise_dtypes=True).then_inc(iota_t, 1)
            for k in range(2):
                pool.wait_ge(h_out[k], 16 * (NT // 2))
            pool.wait_ge(acc_set, NT)

            def c_body(i):
                for h in range(2):
                    hold(pool, idx_made, i * 2 + (h + 1), pool_passed)
                    for k in range(4):
                        s = h * 4 + k
                        if not first(i):
                            hold(pool, msg_summed, i * 8 + (s - 7), pool_passed)
                        pool.indirect_dma_start(
                            ring[:, s, :], None, H_d,
                            bass.IndirectOffsetOnAxis(idx_st[:, h, k:k + 1], 0)).then_inc(row_in[s], 16)
            rounds(pool, ET // 8, c_body)

            pool.wait_ge(buf_filled, 16 * (NB - EARLY))

            for t in range(NT):
                if t % TQ == 0:
                    pool.wait_ge(route_made, t // TQ + 1)
                for j in range(2):
                    pool.indirect_dma_start(
                        buf_d, bass.IndirectOffsetOnAxis(sidx[:, j, t:t + 1], 0), acc[:, t, :], None,
                        bounds_check=SLOTS - 1, oob_is_err=False).then_inc(sent, 16)

            for k in range(2):
                pool.wait_ge(e_out[k], 16 * (NX // 2))

            def f_body(i):
                step.round(i, 1)
                if not first(i):
                    for k in range(4):
                        pool.wait_ge(og_in[k], i * 32)
                step(pool.tensor_copy(rt_st[:, :, 0:4], gidx[:, :, ds(i * 4, 4)]))
                for k in range(4):
                    if not first(i):
                        hold(pool, fin_made, i * 4 + (k - 3), pool_passed)
                    for j in range(2):
                        pool.indirect_dma_start(
                            ring[:, 2 * k + j, :], None, o_d,
                            bass.IndirectOffsetOnAxis(rt_st[:, j, k:k + 1], 0)).then_inc(og_in[k], 16)
            rounds(pool, NT // 4, f_body)
            step.end(NT // 4)

        @block.scalar
        def _(act):
            act.wait_ge(const_made, NCONST)
            act.wait_ge(var_made, 1)
            act.activation(sA[:, :], l2s[:, :], ACT.Sqrt, bias=eps[:, 0:1], scale=1.0).then_inc(sd_made, 1)
            act.activation(sB[:, :], l2s[:, :], ACT.Sqrt, bias=eps[:, 1:2], scale=float(D)).then_inc(sd_made, 1)
            for m in range(DC):
                act.wait_ge(wt_tr, m + 1)
                act.copy(wT[:, m, :], bank[m][:, :]).then_inc(wt_made, 1)

            def a1_body(i):
                for s in range(2):
                    n = i * 2 + s
                    act.wait_ge(xn_turned, n + 1)
                    if not first(i):
                        act.wait_ge(h_summed, i * 2 + (s - 1))
                    act.copy(xT[:, s, :], bank[4][:, :]).then_inc(xT_made, 1)
                    act.wait_ge(h_summed, n + 1)
                    if not first(i):
                        act.wait_ge(h_out[s], i * 16)
                    act.copy(h_sb[:, s, :], bank[5 + s][:, :]).then_inc(h_made, 1)
                    act.wait_ge(h_made, n + 1)
                    act.dma_start(H_t[n], h_sb[:, s, :]).then_inc(h_out[s], 16)
            rounds(act, NT // 2, a1_body)

            act.wait_ge(gram_done, NT)
            for m in range(DC):
                act.copy(G[:, m, :], bank[m][:, :]).then_inc(m_act, 1)
            for m in range(DC):
                act.wait_ge(m_pe, m + 1)
                act.copy(wvT[:, m, :], bank[4 + m][:, :]).then_inc(m_act, 1)
            for m in range(DC):
                act.wait_ge(m_pe, 4 + m + 1)
                act.copy(Tk[:, m, :], bank[m][:, :]).then_inc(m_act, 1)
            act.wait_ge(small_in, 16 * 4)
            act.activation(tcol[:, :], tcol[:, :], ACT.Exp).then_inc(m_act, 1)
            act.wait_ge(m_dve, 9)
            act.activation(qs[:, :], qs[:, :], ACT.Sqrt).then_inc(m_act, 1)
            act.wait_ge(m_dve, 10)
            act.activation(kinv, kinv, ACT.Sqrt).then_inc(m_act, 1)
            act.wait_ge(m_dve, 11)
            act.activation(sim, sim, ACT.Exp).then_inc(m_act, 1)
            for m in range(DC):
                act.wait_ge(m_pe, 18 + m)
                act.copy(Bm[:, m, :], bank[m][:, :]).then_inc(m_act, 1)
            for m in range(DC):
                act.wait_ge(m_pe, 22 + m)
                act.copy(Msb[:, m, :], bank[4 + m][:, :]).then_inc(m_act, 1)

            def a2_body(i):
                for s in range(2):
                    act.wait_ge(yn_turned, i * 2 + (s + 1))
                    if not first(i):
                        act.wait_ge(mix_summed, i * 2 + (s - 1))
                    act.copy(xT[:, s, :], bank[s][:, :]).then_inc(yT_made, 1)
            rounds(act, NT // 2, a2_body)

            act.wait_ge(recs_in, 16)

            def idx_body(i):
                for h in range(2):
                    if not first(i):
                        for k in range(4):
                            hold(act, row_in[h * 4 + k], i * 16, act_passed)
                    act.copy(idx_st[:, h, :], recs_i[:, ds(i * 8 + h * 4, 4), 0]).then_inc(idx_made, 1)
            rounds(act, ET // 8, idx_body)

            act.wait_ge(b1_turned, 1)
            act.copy(b1T[:, :, :].rearrange("p c e -> p (c e)"), bank[7][:, 0:DC * NX]).then_inc(b1T_made, 1)

            def root(q):
                act.wait_ge(var2_made, q + 1)
                act.activation(sA[:, 0:TQ], sB[:, 0:TQ], ACT.Sqrt, bias=eps[:, 0:1], scale=1.0).then_inc(sd2_made, 1)

            def d_body(q, last=False):
                def normed(k):
                    t = q * TQ + k
                    if k == 0:
                        hold(act, norm2_made, q + 1, act_passed)
                    if k % (TQ // 2) == 0:
                        hold(act, x1_out[k // (TQ // 2)], q * 16 + 16, act_passed)
                    row = acc[:, ds(t, 1), :].rearrange("p a d -> p (a d)")
                    act.activation(row, row, ACT.Identity, bias=nb2[:, ds(t, 1)],
                                   scale=rstd2[:, ds(t, 1)]).then_inc(xs_made, 1)

                def logits_out(g):
                    act.wait_ge(gated, q * NG + (g + 1))
                    if not (first(q) and g < 2):
                        act.wait_ge(turned_back, q * NG + (g - 1))
                    act.copy(lt[:, g % 2, :], bank[4][0:NX, :]).then_inc(lt_made, 1)

                for k in range(TG):
                    normed(k)
                for k in range(TQ):
                    g, c = k // TG, k % TG
                    if k + TG < TQ:
                        normed(k + TG)
                    act.wait_ge(xs_turned, q * TQ + (k + 1))
                    if c == 0 and not (first(q) and g < 2):
                        act.wait_ge(gated, q * NG + (g - 1))
                    act.copy(xT4[g % 2][:, :, c * P:(c + 1) * P], v3(bank[c][:, :], DC)).then_inc(xsT_made, 1)
                    if c == 1 and g > 0:
                        logits_out(g - 1)
                    if k == TQ - TG - 1 and not last:
                        root(q + 1)
                logits_out(NG - 1)
                act.wait_ge(turned_back, q * NG + NG)
                act.copy(L[:, ds(q * TQ, TQ), :], v3(bank[7][:, :], TQ)).then_inc(L_made, 1)

            root(0)
            d_body(0)
            with act.Fori(1, NQ - 1) as q:
                d_body(q)
            d_body(NQ - 1, last=True)
            act.wait_ge(lsub_made, 1)
            act.activation(L, L, ACT.Exp).then_inc(exp_made, 1)
            act.activation(share[:, 1, :], share[:, 1, :], ACT.Exp).then_inc(exp_made, 1)

            def e_rows(i, s):
                for c in range(CT):
                    act.wait_ge(e_turned, i * 2 * CT + (s * CT + c + 1))
                    if c == 0 and not (first(i) and s == 0):
                        act.wait_ge(e_up, i * 16 + s * 8)
                    act.copy(bTh[:, :, c * P:(c + 1) * P],
                             v3(bank[(s * CT + c) % 2][:, :], DC)).then_inc(e_bT, 1)

            def e_body(i):
                for s in range(2):
                    e_rows(i, s)
                    for g in range(8):
                        hc, hf = g // 2, g % 2
                        half = slice(hf * HN, (hf + 1) * HN)
                        bias = b1T[:, hc, ds(i * 2 + s, 1)]
                        act.wait_ge(e_up, i * 16 + (s * 8 + g + 1))
                        if g == 0 and not (first(i) and s == 0):
                            act.wait_ge(e_down, i * 2 * CT + s * CT)
                        if not (first(i) and s == 0 and g < 4):
                            act.wait_ge(e_hs, i * 16 + (s * 8 + g - 3))
                        act.sem_inc(act_passed, 1)
                        act.activation(h_st[:, g % 4, :], bank[2 + g % 4][:, 0:HN], ACT.Relu, bias=bias, scale=1.0)
                        act.activation(hTh[:, hc, half], bank[2 + g % 4][:, 0:HN], ACT.Relu, bias=bias,
                                       scale=1.0).then_inc(e_h, 1)
            rounds(act, NX // 2, e_body)

            def f_body(i):
                for k in range(4):
                    t = i * 4 + k
                    hold(act, xr_in[k], i * 16 + 16, act_passed)
                    if not first(i):
                        hold(act, fin_out[k], i * 16, act_passed)
                    act.activation(fin[:, k, :], xr[:, k, :], ACT.Identity, bias=cb[:, ds(t, 1)],
                                   scale=ca[:, ds(t, 1)]).then_inc(x1b_made, 1)
            rounds(act, NT // 4, f_body)

        @block.vector
        def _(dve):
            step = Chain(dve, dve_step)
            dve.wait_ge(const_made, NCONST)

            def moments(step, stat, mean, var, a, b):
                step(dve.tensor_tensor(a, stat[:, :, 1], stat[:, :, 4], ALU.subtract))
                step(dve.tensor_tensor(mean, stat[:, :, 1], stat[:, :, 4], ALU.add))
                step(dve.tensor_scalar(mean, mean, 0.5, None, ALU.mult))
                step(dve.tensor_tensor(a, a, a, ALU.mult))
                step(dve.tensor_scalar(a, a, 0.25, None, ALU.mult))
                step(dve.tensor_tensor(b, stat[:, :, 2], stat[:, :, 5], ALU.add))
                step(dve.scalar_tensor_tensor(out=var, in0=b, scalar=1.0 / D, in1=a, op0=ALU.mult, op1=ALU.add))

            dve.wait_ge(edges_in, 48)
            sh = P.bit_length() - 1
            step(dve.tensor_scalar(tmp_i, src_i, sh, None, ALU.logical_shift_right))
            step(dve.tensor_copy(win_bf, tmp_i))
            step(dve.tensor_scalar(tmp_i, src_i, P - 1, None, ALU.bitwise_and))
            step(dve.tensor_copy(srcl_f, tmp_i))

            io = iota_b[:, None, :].to_broadcast([P, KC, NT])

            def oh_body(i):
                for c in range(HG):
                    g = i * HG + c
                    dve.tensor_tensor(oh_all[:, ds(g * 512, 512)].rearrange("p (k w) -> p k w", k=KC),
                                      win_bf[:, ds(g * KC, KC)][:, :, None].to_broadcast([P, KC, NT]), io,
                                      ALU.is_equal).then_inc(oh_built, 1)
            rounds(dve, NB, oh_body)
            dve.wait_ge(totals_made, 1)
            step(dve.tensor_copy(tot_sb.rearrange("p k w -> p (k w)"), bank[0][:, :]))
            step(dve.memset(init_sb[:, 0, :], 0.0))
            for m in range(KC - 1):
                step(dve.tensor_tensor(init_sb[:, m + 1, :], init_sb[:, m, :], tot_sb[:, m, :], ALU.add))
            step(dve.tensor_tensor(wtot[:, :], init_sb[:, KC - 1, :], tot_sb[:, KC - 1, :], ALU.add))
            step(dve.tensor_scalar(wtot[:, :], wtot[:, :], float(P - 1), None, ALU.add))
            step(dve.tensor_copy(nt_i[:, :], wtot[:, :]))
            step(dve.tensor_scalar(nt_i[:, :], nt_i[:, :], sh, None, ALU.logical_shift_right))
            step(dve.tensor_copy(wtot[:, :], nt_i[:, :]))
            step(dve.memset(sA[:, :], 0.0))
            step(dve.tensor_tensor_scan(ends[:, :], wtot[:, :], sA[:, :], 0.0, ALU.add, ALU.add))
            step(dve.tensor_tensor(sA[:, :], ends[:, :], wtot[:, :], ALU.subtract))
            step(dve.tensor_scalar(sA[:, :], sA[:, :], float(P), None, ALU.mult))
            dve.tensor_tensor(init_sb, init_sb, sA[:, None, :].to_broadcast([P, KC, NT]),
                              ALU.add).then_inc(init_made, 1)

            def rank_group(n, c):
                g = n * HG + c
                dve.wait_ge(ranked, g + 1)
                dve.tensor_tensor(prod[:, c % 2, :], bank[7][:, :], oh_all[:, ds(g * 512, 512)],
                                  ALU.mult).then_inc(rank_read, 1)
                dve.wait_ge(rank_read, g + 1)
                step(dve.tensor_reduce(rk_f[:, c * KC:(c + 1) * KC],
                                       prod[:, c % 2, :].rearrange("p (k w) -> p k w", k=KC), AX, ALU.add))

            def addresses(n):
                step(dve.tensor_copy(rk_i[:, 0:HC], rk_f[:, :]))
                step(dve.tensor_scalar(rk_i[:, HC:2 * HC], rk_i[:, 0:HC], sh, None, ALU.logical_shift_right))
                step(dve.tensor_scalar(rk_i[:, 0:HC], rk_i[:, 0:HC], P - 1, None, ALU.bitwise_and))
                step(dve.scalar_tensor_tensor(out=addr_all[:, ds(n * HC, HC)], in0=rk_i[:, 0:HC], scalar=float(ET),
                                              in1=rk_i[:, HC:2 * HC], op0=ALU.mult, op1=ALU.add))
                dve.sem_inc(addr_made, 1)

            for n in range(EARLY):
                for c in range(HG):
                    rank_group(n, c)
                addresses(n)

            def s_body(i):
                for k in range(8):
                    dve.wait_ge(xs_in[k], i * 16 + 16)
                    dve.bn_stats(stat1[:, ds(i * 8 + k, 1), :].rearrange("p a s -> p (a s)"),
                                 ring[:, k, :]).then_inc(stat_read, 1)
            rounds(dve, NT // 8, s_body)
            dve.wait_ge(stat_read, NT)
            moments(step, stat1, mean1[:, :], l2s[:, :], sA[:, :], sB[:, :])
            dve.sem_inc(var_made, 1)
            dve.wait_ge(sd_made, 2)
            step(dve.reciprocal(rstd1[:, :], sA[:, :]))
            step(dve.tensor_tensor(sB[:, :], sB[:, :], rstd1[:, :], ALU.mult))
            step(dve.tensor_scalar(sB[:, :], sB[:, :], L2_EPS, None, ALU.max))
            step(dve.reciprocal(l2s[:, :], sB[:, :]))
            step(dve.tensor_scalar(l2s[:, :], l2s[:, :], float(D) ** 0.5, None, ALU.mult))
            step(dve.tensor_tensor(xhs[:, :], l2s[:, :], rstd1[:, :], ALU.mult))

            def a1_body(i, ranks=True):
                if ranks:
                    step.round(i, HG + 4)
                for s in range(2):
                    n = i * 2 + s
                    dve.wait_ge(a1_in[s], i * 16 + 16)
                    if not first(i):
                        dve.wait_ge(xn_turned, i * 2 + (s - 1))
                    dve.tensor_scalar(xn[:, s, :], xt[:, s, :], mean1[:, ds(n, 1)], rstd1[:, ds(n, 1)],
                                      ALU.subtract, ALU.mult).then_inc(xn_made, 1)
                    if not first(i):
                        dve.wait_ge(gram_done, i * 2 + (s - 1))
                    dve.tensor_scalar(xh[:, s, :], xt[:, s, :], mean1[:, ds(n, 1)], xhs[:, ds(n, 1)],
                                      ALU.subtract, ALU.mult).then_inc(xh_made, 1)
                    if ranks:
                        rank_group(i + EARLY, 2 * s)
                        rank_group(i + EARLY, 2 * s + 1)
                if ranks:
                    addresses(i + EARLY)
            rounds(dve, NB - EARLY, a1_body)
            step.end(NB - EARLY)
            for i in range(NB - EARLY, NT // 2):
                a1_body(i, ranks=False)

            dve.wait_ge(qkv_in, 32)
            dve.wait_ge(small_in, 16 * 4)
            for m in range(DC):
                dve.tensor_scalar(wqkv[:, m, :], wqkv[:, m, :], gcol[:, m:m + 1], None,
                                  ALU.mult).then_inc(qkv_scaled, 1)
            dve.wait_ge(qkv_scaled, DC)
            for m in range(DC):
                dve.wait_ge(m_act, 9 + m)
                dve.tensor_tensor(prk[:, m, :], bank[m][:, :], wqkv[:, m, D:2 * D], ALU.mult).then_inc(m_dve, 1)
            for m in range(DC):
                dve.wait_ge(m_pe, 8 + m + 1)
                dve.tensor_tensor(prq[:, m, :], bank[4 + m][:, :], wqkv[:, m, 0:D], ALU.mult).then_inc(m_dve, 1)
            step(dve.memset(Abd, 0.0))
            dve.wait_ge(m_pe, 13)
            dve.tensor_scalar(qs[:, :], bank[4][:, 0:DC], 0.0, None, ALU.max).then_inc(m_dve, 1)
            dve.tensor_scalar(kinv, bank[5][:, :], 0.0, None, ALU.max).then_inc(m_dve, 1)
            dve.wait_ge(m_act, 14)
            step(dve.tensor_scalar(qs[:, :], qs[:, :], L2_EPS, None, ALU.max))
            step(dve.reciprocal(qs[:, :], qs[:, :]))
            step(dve.tensor_tensor(qs[:, :], qs[:, :], tcol[:, :], ALU.mult))
            step(dve.tensor_scalar(qs[:, :], qs[:, :], SCALE, None, ALU.mult))
            dve.wait_ge(m_act, 15)
            step(dve.tensor_scalar(kinv, kinv, L2_EPS, None, ALU.max))
            step(dve.reciprocal(kinv, kinv))
            dve.wait_ge(m_pe, 17)
            for m in range(DC):
                for lo in (0, DH):
                    r = slice(lo, lo + DH)
                    step(dve.tensor_tensor(sim[r, m, :], bank[m][r, lo:lo + DH],
                                           kinv[r, m * P + lo:m * P + lo + DH], ALU.mult))
                step(dve.tensor_scalar(sim[:, m, :], sim[:, m, :], qs[:, m:m + 1], None, ALU.mult))
            step(dve.tensor_reduce(mx[:, :], sim, AX, ALU.max))
            dve.tensor_tensor(sim, sim, mx[:, :, None].to_broadcast([P, DC, DH]),
                              ALU.subtract).then_inc(m_dve, 1)
            dve.wait_ge(m_act, 16)
            step(dve.tensor_reduce(mx[:, :], sim, AX, ALU.add))
            step(dve.reciprocal(mx[:, :], mx[:, :]))
            for m in range(DC):
                for lo in (0, DH):
                    r = slice(lo, lo + DH)
                    dve.tensor_scalar(Abd[r, m, lo:lo + DH], sim[r, m, :], mx[r, m:m + 1], None,
                                      ALU.mult).then_inc(m_dve, 1)

            def a2_body(i):
                for s in range(2):
                    n = i * 2 + s
                    dve.wait_ge(a2_in[s], i * 16 + 16)
                    if not first(i):
                        dve.wait_ge(yn_turned, i * 2 + (s - 1))
                    dve.tensor_scalar(xn[:, s, :], xt[:, s, :], mean1[:, ds(n, 1)], rstd1[:, ds(n, 1)],
                                      ALU.subtract, ALU.mult).then_inc(yn_made, 1)
                for s in range(2):
                    n = i * 2 + s
                    dve.wait_ge(mix_summed, n + 1)
                    dve.scalar_tensor_tensor(
                        out=acc[:, ds(n, 1), :].rearrange("p a d -> p (a d)"), in0=bank[2 + s][:, :],
                        scalar=l2s[:, ds(n, 1)], in1=xt[:, s, :], op0=ALU.mult, op1=ALU.add).then_inc(acc_set, 1)
            rounds(dve, NT // 2, a2_body)
            dve.wait_ge(acc_set, NT)

            dve.wait_ge(iota_t, 1)
            dve.wait_ge(ecol_made, 1)
            step(dve.tensor_copy(ecol[:, :], bank[0][0:NT, 0:1]))
            dve.tensor_scalar(maskT[0:NT, :], iotaT[0:NT, :], ecol[:, 0:1], None, ALU.is_ge).then_inc(mask_made, 1)
            dve.wait_ge(wt_summed, 1)
            for c0 in range(0, ET, BANK):
                n = min(BANK, ET - c0)
                step(dve.tensor_scalar(wt_i[:, c0:c0 + n], bank[1 + c0 // BANK][0:1, 0:n], float(NT - 1), float(D),
                                       ALU.min, ALU.mult))
            dve.wait_ge(recs_in, 16)

            def onehot(i, s):
                t = i * 8 + s
                if not first(i):
                    dve.wait_ge(msg_summed, i * 8 + (s - 7))
                dve.tensor_scalar(oh[:, s, :], iota_f[:, :], recs[:, ds(t, 1), 1], recs[:, ds(t, 1), 2],
                                  ALU.is_equal, ALU.mult).then_inc(oh_made, 1)

            win_reg = [dve.alloc_register(f"window{k}") for k in range(8)]

            def windows(t, n):
                dve.load(win_reg[:n], wt_i[0:1, ds(t, n)])
                return [dve.snap(r, min_val=0, max_val=(NT - 1) * D) for r in win_reg[:n]]

            def add(off, i, s, back=0):
                t = i * 8 + (s - back)
                dve.wait_ge(msg_summed, t + 1)
                if not (isinstance(t, int) and t == 0):
                    dve.wait_ge(acc_added, t)
                dve.tensor_tensor(arena[:, ds(off, D)], arena[:, ds(off, D)], bank[s][:, :],
                                  ALU.add).then_inc(acc_added, 1)

            def c_body(i):
                offs = windows(i * 8 - (0 if first(i) else 4), 4 if first(i) else 8)
                for k in range(4):
                    onehot(i, k)
                    if not first(i):
                        add(offs[k], i, 4 + k, 8)
                for k in range(4):
                    onehot(i, 4 + k)
                    add(offs[k - 4], i, k)
            rounds(dve, ET // 8, c_body)
            for k, off in enumerate(windows(ET - 4, 4)):
                add(off, ET // 8, 4 + k, 8)
            dve.wait_ge(acc_added, ET)

            step_n = Chain(dve, norm_step)
            step_r = Chain(dve, route_step)

            def norm_body(q):
                step_n.round(q, 9)
                at = ds(q * TQ, TQ)
                for k in range(TQ):
                    dve.bn_stats(stat2[:, k, :], acc[:, ds(q * TQ + k, 1), :].rearrange("p a d -> p (a d)")
                                 ).then_inc(stat_read, 1)
                dve.wait_ge(stat_read, q * TQ + (NT + TQ))
                moments(step_n, stat2, mean2[:, at], sB[:, 0:TQ], sA[:, 0:TQ], nb2[:, at])
                dve.sem_inc(var2_made, 1)
                dve.wait_ge(sd2_made, q + 1)
                step_n(dve.reciprocal(rstd2[:, at], sA[:, 0:TQ]))
                step_n(dve.scalar_tensor_tensor(out=nb2[:, at], in0=mean2[:, at], scalar=-1.0, in1=rstd2[:, at],
                                                op0=ALU.mult, op1=ALU.mult))
                dve.sem_inc(norm2_made, 1)

            def over_e(v):
                return v[:, :, None].to_broadcast([P, v.shape[1], NX])

            def route_body(q):
                step = step_r
                step.round(q, 40)
                at = ds(q * TQ, TQ)
                revb = rev[:, None, :].to_broadcast([P, TQ, NX])
                slot, rank = small
                dve.wait_ge(L_made, q + 1)
                for j, l_ in enumerate((L[:, at, :], Lx)):
                    step(dve.tensor_reduce(tops[:, j, at], l_, AX, ALU.max))
                    step(dve.tensor_tensor(eq, l_, over_e(tops[:, j, at]), ALU.is_equal))
                    step(dve.tensor_tensor(eq, eq, revb, ALU.mult))
                    step(dve.tensor_reduce(slot[:, j, :], eq, AX, ALU.max))
                    step(dve.tensor_tensor(v3(OHA[:, j, :], TQ), revb, over_e(slot[:, j, :]), ALU.is_equal))
                    if j == 0:
                        step(dve.scalar_tensor_tensor(out=Lx, in0=v3(OHA[:, 0, :], TQ), scalar=-3e38, in1=l_,
                                                      op0=ALU.mult, op1=ALU.add))
                dve.sem_inc(oha_made, 1)
                step(dve.tensor_scalar(slot, slot, -1.0, float(NX), ALU.mult, ALU.add))
                dve.wait_ge(pfx_made, q + 1)
                if first(q):
                    step(dve.memset(Cx[:, 0, :], 0.0))
                else:
                    step(dve.tensor_copy(Cx[:, 0, :], Cx[:, TQ, :]))
                for k in range(TQ):
                    step(dve.tensor_tensor(Cx[:, k + 1, :], Cx[:, k, :], bank[6][:, k * NX:(k + 1) * NX], ALU.add))
                step(dve.tensor_tensor(Pfx, v3(bank[5][:, :], TQ), Cx[:, 0:TQ, :], ALU.add))
                for j in range(2):
                    step(dve.tensor_tensor(eq, v3(OHA[:, j, :], TQ), Pfx, ALU.mult))
                    step(dve.tensor_reduce(rank[:, j, :], eq, AX, ALU.add))
                step(dve.scalar_tensor_tensor(out=slot, in0=slot, scalar=float(CAP), in1=rank, op0=ALU.mult,
                                              op1=ALU.add))
                step(dve.tensor_scalar(wts[:, :, at], rank, float(CAP), None, ALU.is_lt))
                step(dve.scalar_tensor_tensor(out=slot, in0=wts[:, :, at], scalar=-FAR, in1=slot, op0=ALU.mult,
                                              op1=ALU.add))
                step(dve.tensor_scalar(slot, slot, FAR, None, ALU.add))
                step(dve.tensor_copy(sidx[:, :, at], slot))
                step(dve.tensor_scalar(gidx[:, :, at], slot, float(SLOTS - 1), None, ALU.min))
                dve.sem_inc(route_made, 1)

            lagged(dve, NQ, norm_body, route_body)
            step_n.end(NQ)
            step_r.end(NQ)

            dve.wait_ge(L_made, NQ)
            step(dve.tensor_tensor(share[:, 1, :], tops[:, 1, :], tops[:, 0, :], ALU.subtract))
            step(dve.tensor_tensor(L, L, over_e(tops[:, 0, :]), ALU.subtract))
            dve.sem_inc(lsub_made, 1)
            dve.wait_ge(exp_made, 2)
            step(dve.tensor_reduce(tmp2[:, 0, :], L, AX, ALU.add))
            step(dve.reciprocal(share[:, 0, :], tmp2[:, 0, :]))
            step(dve.tensor_tensor(share[:, 1, :], share[:, 1, :], share[:, 0, :], ALU.mult))
            step(dve.tensor_tensor(tmp2[:, 0, :], share[:, 0, :], share[:, 1, :], ALU.add))
            step(dve.tensor_scalar(tmp2[:, 0, :], tmp2[:, 0, :], 1e-9, None, ALU.max))
            step(dve.reciprocal(tmp2[:, 1, :], tmp2[:, 0, :]))
            step(dve.tensor_tensor(share, share, tmp2[:, 1, :][:, None, :].to_broadcast([P, 2, NT]), ALU.mult))
            step(dve.tensor_tensor(wts, wts, share, ALU.mult))
            step(dve.tensor_tensor(tmp2[:, 0, :], wts[:, 0, :], wts[:, 1, :], ALU.add))
            step(dve.tensor_scalar(tmp2[:, 0, :], tmp2[:, 0, :], 1e-12, None, ALU.is_le))
            step(dve.tensor_tensor(tmp2[:, 1, :], tmp2[:, 0, :], rstd2[:, :], ALU.mult))
            step(dve.tensor_scalar(ca[:, :], tmp2[:, 1, :], 1.0, None, ALU.add))
            step(dve.tensor_tensor(cb[:, :], tmp2[:, 0, :], nb2[:, :], ALU.mult))

            def bias_add(i, s, c, back=0):
                w = (s - back) % 2
                n = i * 2 * CT + ((s - back) * CT + c)
                dve.wait_ge(e_down, n + 1)
                if c == 0:
                    dve.wait_ge(b2_in[w], i * 16 + (16 if s >= back else 0))
                    if s >= back and not first(i):
                        dve.wait_ge(e_out[w], i * 16)
                    if s < back and not (isinstance(i, int) and i < 2):
                        dve.wait_ge(e_out[w], i * 16 - 16)
                dve.tensor_tensor(osb[w][:, c, :], bank[6 + (w * CT + c) % 2][:, :], b2s[w],
                                  ALU.add).then_inc(e_o, 1)

            def low_rows(i, s, c):
                n = i * 2 * CT + (s * CT + c)
                dve.wait_ge(e_bT, n + 1)
                at = slice(c * P, (c + 1) * P)
                dve.tensor_tensor(bTl[:, :, at], v3(bank[(s * CT + c) % 2][:, :], DC), bTh[:, :, at].bitcast(f32),
                                  ALU.subtract).then_inc(e_bTl, 1)

            def split(wh, wl, wf, high, low, n, k):
                dve.tensor_copy(wh[:, k, :], wf[:, k, :]).then_inc(high, 1)
                dve.wait_ge(high, n + 1)
                dve.tensor_tensor(wl[:, k, :], wf[:, k, :], wh[:, k, :].bitcast(f32),
                                  ALU.subtract).then_inc(low, 1)

            def low_h(i, s, g):
                dve.wait_ge(e_h, i * 16 + (s * 8 + g + 1))
                hc, half = g // 2, slice((g % 2) * HN, (g % 2 + 1) * HN)
                dve.tensor_tensor(hTl[:, hc, half], h_st[:, g % 4, :], hTh[:, hc, half].bitcast(f32),
                                  ALU.subtract).then_inc(e_hs, 1)

            def e_body(i):
                for s in range(2):
                    low_rows(i, s, 0)
                    low_rows(i, s, 1)
                    for c in range(CT):
                        if not (first(i) and s == 0):
                            bias_add(i, s, c, 1)
                        if c + 2 < CT:
                            low_rows(i, s, c + 2)
                        if c < DC:
                            if c == 0:
                                dve.wait_ge(w1_in, i * 32 + (s + 1) * 16)
                            split(w1h[s], w1l[s], w1f, w1_high, w1_split, i * 2 * DC + (s * DC + c), c)
                    for g in range(8):
                        low_h(i, s, g)
                        if g < DC:
                            if g == 0:
                                dve.wait_ge(w2_in, i * 32 + (s + 1) * 16)
                            split(w2h[s], w2l[s], w2f, w2_high, w2_split, i * 2 * DC + (s * DC + g), g)

            e_body(0)
            e_body(1)
            with dve.Fori(2, NX // 2) as i:
                e_body(i)
            for c in range(CT):
                bias_add(NX // 2, 0, c, 1)

            def f_body(i):
                step.round(i, 4)
                for k in range(4):
                    t = i * 4 + k
                    dve.wait_ge(x1b_made, t + 1)
                    dve.wait_ge(og_in[k], i * 32 + 32)
                    step(dve.scalar_tensor_tensor(out=fin[:, k, :], in0=ring[:, 2 * k, :],
                                                  scalar=wts[:, 0, ds(t, 1)], in1=fin[:, k, :],
                                                  op0=ALU.mult, op1=ALU.add))
                    dve.scalar_tensor_tensor(out=fin[:, k, :], in0=ring[:, 2 * k + 1, :],
                                             scalar=wts[:, 1, ds(t, 1)], in1=fin[:, k, :],
                                             op0=ALU.mult, op1=ALU.add).then_inc(fin_made, 1)
            rounds(dve, NT // 4, f_body)
            step.end(NT // 4)

        @block.tensor
        def _(pe):
            def mm(o_, l_, r_, start, stop, **kw):
                return nc.tensor.matmul(o_, l_, r_, start=start, stop=stop, **kw)

            def turn(o_, in_):
                return nc.tensor.transpose(o_, in_, ident[:, :])

            pe.wait_ge(const_made, NCONST)
            mm(bank[0][:, 0:P], zero_b[:, :], zero_b[:, :], True, False, skip_group_check=True)

            def tot_body(i):
                for c in range(HG):
                    g = i * HG + c
                    pe.wait_ge(oh_built, g + 1)
                    mm(bank[0][:, :], ones_b[:, :], oh_all[:, ds(g * 512, 512)], False, False,
                       skip_group_check=True)
            rounds(pe, NB, tot_body)
            mm(bank[0][:, 0:P], zero_b[:, :], zero_b[:, :], False, True,
               skip_group_check=True).then_inc(totals_made, 1)
            pe.wait_ge(init_made, 1)
            mm(bank[7][:, :], ident[:, :], init_sb.rearrange("p k w -> p (k w)"), True, False,
               skip_group_check=True)

            def rank_on(n, c):
                g = n * HG + c
                mm(bank[7][:, :], before[:, :], oh_all[:, ds(g * 512, 512)], False, True,
                   skip_group_check=True).then_inc(ranked, 1)

            def rank_off(n, c):
                g = n * HG + c
                pe.wait_ge(rank_read, g + 1)
                mm(bank[7][:, :], notbefore[:, :], oh_all[:, ds(g * 512, 512)], False, True,
                   skip_group_check=True)

            for n in range(EARLY):
                for c in range(HG):
                    rank_on(n, c)
                    rank_off(n, c)

            pe.wait_ge(gw_in, 16)
            for m in range(DC):
                for k in range(DC):
                    last = turn(bank[m][:, k * P:(k + 1) * P], gwr[:, k, m * P:(m + 1) * P])
                last.then_inc(wt_tr, 1)
            pe.wait_ge(wt_made, DC)

            for m in range(DC):
                mm(bank[m][:, 0:P], zero_b[:, :], zero_b[:, :], True, False, skip_group_check=True)

            def a1_body(i, ranks=True):
                r = i + EARLY
                for s in range(2):
                    n = i * 2 + s
                    pe.wait_ge(xn_made, n + 1)
                    if not (first(i) and s == 0):
                        pe.wait_ge(xT_made, n)
                    for m in range(DC):
                        last = turn(bank[4][:, m * P:(m + 1) * P], xn[:, s, m * P:(m + 1) * P])
                    last.then_inc(xn_turned, 1)
                    if ranks:
                        rank_on(r, 2 * s)
                    pe.wait_ge(xh_made, n + 1)
                    for m in range(DC):
                        last = mm(bank[m][:, :], xh[:, s, m * P:(m + 1) * P], xh[:, s, :], False, False,
                                  skip_group_check=True)
                    last.then_inc(gram_done, 1)
                    if ranks:
                        rank_off(r, 2 * s)
                        rank_on(r, 2 * s + 1)
                    pe.wait_ge(xT_made, n + 1)
                    if not first(i):
                        pe.wait_ge(h_made, i * 2 + (s - 1))
                    for m in range(DC):
                        last = mm(bank[5 + s][:, :], xT[:, s, m * P:(m + 1) * P], wT[:, m, :], m == 0, m == DC - 1)
                    last.then_inc(h_summed, 1)
                    if ranks:
                        rank_off(r, 2 * s + 1)
            rounds(pe, NB - EARLY, a1_body)
            for i in range(NB - EARLY, NT // 2):
                a1_body(i, ranks=False)

            pe.wait_ge(qkv_scaled, DC)
            pe.wait_ge(h_made, NT)
            for m in range(DC):
                for k in range(DC):
                    last = turn(bank[4 + m][:, k * P:(k + 1) * P],
                                wqkv[:, k, 2 * D + m * P:2 * D + (m + 1) * P])
                last.then_inc(m_pe, 1)
            pe.wait_ge(m_act, 4)
            for m in range(DC):
                for k in range(DC):
                    last = mm(bank[m][:, :], G[:, k, m * P:(m + 1) * P], wqkv[:, k, D:2 * D], k == 0, k == DC - 1)
                last.then_inc(m_pe, 1)
            pe.wait_ge(m_act, 8)
            for m in range(DC):
                for k in range(DC):
                    last = mm(bank[4 + m][:, :], G[:, k, m * P:(m + 1) * P], wqkv[:, k, 0:D], k == 0, k == DC - 1)
                last.then_inc(m_pe, 1)
            pe.wait_ge(m_dve, 8)
            for m in range(DC):
                for k in range(DC):
                    mm(bank[4][:, m:m + 1], prq[:, k, m * P:(m + 1) * P], ones_f[:, 0:1], k == 0, k == DC - 1)
            for k in range(DC):
                last = mm(bank[5][:, :], ones_f[:, :], prk[:, k, :], k == 0, k == DC - 1)
            last.then_inc(m_pe, 1)
            pe.wait_ge(m_act, 12)
            for m in range(DC):
                for k in range(DC):
                    last = mm(bank[m][:, 0:P], wqkv[:, k, m * P:(m + 1) * P], Tk[:, k, m * P:(m + 1) * P],
                              k == 0, k == DC - 1)
                last.then_inc(m_pe, 1)
            pe.wait_ge(m_dve, 19)
            for m in range(DC):
                mm(bank[m][:, :], Abd[:, m, :], wout[:, m, :], True, True).then_inc(m_pe, 1)
            pe.wait_ge(m_act, 20)
            for m in range(DC):
                for k in range(DC):
                    last = mm(bank[4 + m][:, :], wvT[:, k, m * P:(m + 1) * P], Bm[:, k, :], k == 0, k == DC - 1)
                last.then_inc(m_pe, 1)
            pe.wait_ge(m_act, 24)

            def a2_body(i):
                for s in range(2):
                    n = i * 2 + s
                    pe.wait_ge(yn_made, n + 1)
                    if not first(i):
                        pe.wait_ge(yT_made, i * 2 + (s - 1))
                    for m in range(DC):
                        last = turn(bank[s][:, m * P:(m + 1) * P], xn[:, s, m * P:(m + 1) * P])
                    last.then_inc(yn_turned, 1)
                for s in range(2):
                    n = i * 2 + s
                    pe.wait_ge(yT_made, n + 1)
                    if not first(i):
                        pe.wait_ge(acc_set, i * 2 + (s - 1))
                    for m in range(DC):
                        last = mm(bank[2 + s][:, :], xT[:, s, m * P:(m + 1) * P], Msb[:, m, :], m == 0, m == DC - 1)
                    last.then_inc(mix_summed, 1)
            rounds(pe, NT // 2, a2_body)

            pe.wait_ge(acc_set, NT)
            pe.wait_ge(yT_made, NT)
            mm(bank[0][0:NT, 0:1], ends[0:1, :], ones_f[0:1, 0:1], True, True).then_inc(ecol_made, 1)
            pe.wait_ge(mask_made, 1)
            for c0 in range(0, ET, BANK):
                n = min(BANK, ET - c0)
                last = mm(bank[1 + c0 // BANK][0:1, 0:n], ones_f[0:NT, 0:1], maskT[0:NT, c0:c0 + n], True, True)
            last.then_inc(wt_summed, 1)

            def c_body(i):
                for s in range(8):
                    t = i * 8 + s
                    pe.wait_ge(oh_made, t + 1)
                    pe.wait_ge(row_in[s], i * 16 + 16)
                    if not first(i):
                        pe.wait_ge(acc_added, i * 8 + (s - 7))
                    mm(bank[s][:, :], oh[:, s, :], ring[:, s, :], True, True).then_inc(msg_summed, 1)
            rounds(pe, ET // 8, c_body)
            pe.wait_ge(acc_added, ET)

            pe.wait_ge(b1_in, 16)
            pe.wait_ge(small_in, 16 * 4)
            for m in range(DC):
                last = nc.tensor.transpose(bank[7][:, m * NX:(m + 1) * NX], b1_sb[:, m * P:(m + 1) * P],
                                           ident[0:NX, 0:NX])
            last.then_inc(b1_turned, 1)

            def count(q):
                pe.wait_ge(oha_made, q + 1)
                if not first(q):
                    pe.wait_ge(route_made, q)
                for j in range(2):
                    mm(bank[5][:, :], before[:, :], OHA[:, j, :], j == 0, j == 1)
                for j in range(2):
                    last = mm(bank[6][:, :], ones_b[:, :], OHA[:, j, :], j == 0, j == 1)
                last.then_inc(pfx_made, 1)

            def gate_body(q):
                def turn_tile(k):
                    t = q * TQ + k
                    pe.wait_ge(xs_made, t + 1)
                    if not (first(q) and k < TG):
                        pe.wait_ge(xsT_made, t - (TG - 1))
                    for m in range(DC):
                        last = turn(bank[k % TG][:, m * P:(m + 1) * P], acc[:, t, m * P:(m + 1) * P])
                    last.then_inc(xs_turned, 1)

                def gate(g):
                    pe.wait_ge(xsT_made, q * TQ + (g + 1) * TG)
                    if not (first(q) and g == 0):
                        pe.wait_ge(lt_made, q * NG + g)
                    for m in range(DC):
                        last = mm(bank[4][0:NX, :], wg_sb[:, m, :], xT4[g % 2][:, m, :], m == 0, m == DC - 1)
                    last.then_inc(gated, 1)

                def back(g):
                    pe.wait_ge(lt_made, q * NG + (g + 1))
                    if g == 0 and not first(q):
                        pe.wait_ge(L_made, q)
                    for c in range(TG):
                        k = g * TG + c
                        last = nc.tensor.transpose(bank[7][:, k * NX:(k + 1) * NX], lt[:, g % 2, c * P:(c + 1) * P],
                                                   ident[0:NX, 0:NX])
                    last.then_inc(turned_back, 1)

                for g in range(NG):
                    for c in range(TG):
                        turn_tile(g * TG + c)
                        if c == 1 and g > 0:
                            gate(g - 1)
                        if c == 1 and g == 1 and not first(q):
                            count(q - 1)
                    if g > 0:
                        back(g - 1)
                gate(NG - 1)
                back(NG - 1)

            for q in range(NQ):
                gate_body(q)
            count(NQ - 1)
            pe.wait_ge(route_made, NQ)
            pe.wait_ge(b1T_made, 1)

            def product(o_, parts):
                n = len(parts)
                for k, (fh, fl, gh, gl) in enumerate(parts):
                    mm(o_, fh, gh, k == 0, False)
                    mm(o_, fh, gl, False, False)
                    last = mm(o_, fl, gh, False, k == n - 1)
                return last

            def turn_rows(i, s, c):
                n = i * 2 * CT + (s * CT + c)
                if c == 0:
                    pe.wait_ge(bin_in[s], i * 16 + 16)
                if not (isinstance(n, int) and n < 2):
                    pe.wait_ge(e_bTl, n - 1)
                for k in range(DC):
                    last = turn(bank[(s * CT + c) % 2][:, k * P:(k + 1) * P], bin_[s][:, c, k * P:(k + 1) * P])
                last.then_inc(e_turned, 1)

            def down(i, s, c):
                w = s % 2
                if c == 0:
                    pe.wait_ge(w2_split, i * 2 * DC + (s + 1) * DC)
                    pe.wait_ge(e_hs, i * 16 + ((s + 1) * 8 - 1))
                if (c + 1) * P > HN:
                    pe.wait_ge(e_hs, i * 16 + (s + 1) * 8)
                n = i * 2 * CT + (s * CT + c)
                if not (isinstance(n, int) and n < 2):
                    pe.wait_ge(e_o, n - 1)
                at = slice(c * P, (c + 1) * P)
                product(bank[6 + (w * CT + c) % 2][:, :],
                        [(hTh[:, k, at], hTl[:, k, at], w2h[w][:, k, :], w2l[w][:, k, :])
                         for k in range(DC)]).then_inc(e_down, 1)

            def e_body(i):
                for s in range(2):
                    turn_rows(i, s, 0)
                    turn_rows(i, s, 1)
                    for c in range(CT):
                        if not (first(i) and s == 0):
                            down(i, s - 1, c)
                        if c + 2 < CT:
                            turn_rows(i, s, c + 2)
                    pe.wait_ge(w1_split, i * 2 * DC + (s + 1) * DC)
                    pe.wait_ge(e_bTl, i * 2 * CT + (s + 1) * CT)
                    for g in range(8):
                        hc, hf = g // 2, g % 2
                        n = i * 16 + (s * 8 + g)
                        if not (isinstance(n, int) and n < 4):
                            pe.wait_ge(e_h, n - 3)
                        half = slice(hf * HN, (hf + 1) * HN)
                        cols = slice(hc * P, (hc + 1) * P)
                        product(bank[2 + g % 4][:, 0:HN],
                                [(w1h[s][:, k, cols], w1l[s][:, k, cols], bTh[:, k, half],
                                  bTl[:, k, half]) for k in range(DC)]).then_inc(e_up, 1)
            rounds(pe, NX // 2, e_body)
            for c in range(CT):
                down(NX // 2, -1, c)


_INS = ['x', 'src', 'dst', 'edge_weight', 'L0_gnn_weight', 'L0_mix_gamma', 'L0_mix_w_qkv', 'L0_mix_temperature',
        'L0_mix_w_out', 'L0_ffn_Wg', 'L0_ffn_W1', 'L0_ffn_b1', 'L0_ffn_W2', 'L0_ffn_b2']


def kernel(**inputs):
    import numpy as _np
    import concourse.bacc as _bacc
    from concourse import mybir as _mybir
    from concourse.bass_utils import run_bass_kernel_spmd as _run

    nc = _bacc.Bacc("TRN2", target_bir_lowering=False, num_devices=1)
    arrays, args = {}, []
    for name in _INS:
        a = _np.ascontiguousarray(inputs[name])
        arrays[f"in_{name}"] = a
        args.append(nc.dram_tensor(f"in_{name}", a.shape, _mybir.dt.from_np(a.dtype), kind="ExternalInput").ap())
    shape = tuple(inputs['x'].shape)
    args.append(nc.dram_tensor("out_rows", shape, _mybir.dt.float32, kind="ExternalOutput").ap())
    build(nc, *args)
    r = _run(nc, [arrays], core_ids=[0])
    return r.results[0]["out_rows"]
```

```python
import concourse.bass as bass
from concourse import mybir
from contextlib import ExitStack
import math

P = 128
BANK = 512
D = 512
DC = D // P


class Chain:

    def __init__(self, eng, sem, passed=None):
        self.eng, self.sem, self.base, self.k, self.i, self.per = eng, sem, 0, 0, 0, 0
        self.passed = passed

    def at(self):
        return self.i * self.per + (self.base + self.k)

    def __call__(self, ins):
        ins.then_inc(self.sem, 1)
        self.k += 1
        self.eng.wait_ge(self.sem, self.at())
        if self.passed is not None and not isinstance(self.at(), int):
            self.eng.sem_inc(self.passed, 1)

    def round(self, i, per):
        if isinstance(i, int) and i == 0:
            self.base, self.k = self.base + self.k, 0
        else:
            assert self.k == per, (self.k, per)
        self.i, self.per, self.k = i, per, 0

    def end(self, n):
        assert self.k == self.per, (self.k, self.per)
        self.base, self.k, self.i, self.per = self.base + n * self.per, 0, 0, 0


def hold(eng, sem, value, passed):
    eng.wait_ge(sem, value)
    eng.sem_inc(passed, 1)


def rounds(eng, n, body):
    body(0)
    with eng.Fori(1, n) as i:
        body(i)


def first(i):
    return isinstance(i, int) and i == 0


def build(nc, x, src, dst, edge_w, gnn_w, gamma, w_qkv, temp, w_out, Wg, W1, b1, W2, b2, out):
    f32, bf16, i32, u32 = mybir.dt.float32, mybir.dt.bfloat16, mybir.dt.int32, mybir.dt.uint32
    f32r = mybir.dt.float32r
    ALU, ACT, AX = mybir.AluOpType, mybir.ActivationFunctionType, mybir.AxisListType.X
    ds = bass.ds

    N = x.shape[0]
    NT = N // P
    E = src.shape[0]
    EC = E // P
    ET = EC + NT
    KC = 8
    HG = 4
    HC = HG * KC
    NB = EC // HC
    LO = 8
    PAIRS = EC // (2 * KC)
    EARLY = 3
    HEADS, DH, SCALE = 8, 64, 8.0
    LN_EPS, L2_EPS = 1e-5, 1e-12
    NX = Wg.shape[1]
    CAP = int(math.ceil(1.25 * 2 * N / NX))
    CT = CAP // P
    HN = CAP // 2
    SLOTS = NX * CAP
    TQ = 8
    TG = BANK // P
    NG = TQ // TG
    NQ = NT // TQ
    NORM = (0, 1, 4, 6, 8)
    FIRST = 4 * DC
    FAR = 65536.0

    H_d = nc.dram_tensor("h_rows", (N, D), f32, kind="Internal").ap()
    rec_d = nc.dram_tensor("edge_records", (P * ET, 4), f32, kind="Internal").ap()
    x1_d = nc.dram_tensor("x1_rows", (N, D), f32, kind="Internal").ap()
    zr = -(-SLOTS // (P * (NB - EARLY)))
    buf_all = nc.dram_tensor("expert_in", (P * zr * (NB - EARLY), D), f32, kind="Internal").ap()
    buf_d = buf_all[0:SLOTS, :]
    o_d = nc.dram_tensor("expert_out", (SLOTS, D), f32, kind="Internal").ap()

    ctx = ExitStack()
    with ctx:
        def sb(name, shape, dt):
            return ctx.enter_context(nc.sbuf_tensor(name, shape, dt))

        def sem(name):
            return ctx.enter_context(nc.semaphore(name))

        work = sb("work", [P, 14336], f32)
        with nc.sbuf_tensor("arena", [P, NT * D], f32) as arena, nc.sbuf_tensor("ring", [P, 8, D], f32) as ring:
            pass
        sets = ctx.enter_context(ExitStack())

        def late(name, shape, dt):
            return sets.enter_context(nc.sbuf_tensor(name, shape, dt))

        w1h, w1l, w2h, w2l = (late(name, [P, DC, D], f32r) for name in ("w1_high", "w1_low", "w2_high", "w2_low"))
        bTh, bTl, hTh, hTl = (late(name, [P, DC, CAP], f32r)
                              for name in ("rows_high", "rows_low", "hidden_high", "hidden_low"))
        NPRE = NX // 2
        x1_pre = late("x1_pre", [P, NPRE, D], f32)
        bin_, osb = ([late(f"{name}_{k}", [P, CT, D], f32) for k in range(2)] for name in ("rows_in", "rows_out"))

        def cut(t, at, n):
            return t[:, at:at + n]

        def v3(t, a):
            return t.rearrange("p (a b) -> p a b", a=a)

        acc = v3(arena[:, :], NT)
        oh_all = arena[:, :].bitcast(bf16)
        src_i = cut(work, 0, EC).bitcast(i32)
        srcl_f = cut(work, 0, EC)
        dst_i = cut(work, EC, EC).bitcast(i32)
        w_f = cut(work, 2 * EC, EC)
        tmp_i = cut(work, 3 * EC, EC).bitcast(i32)
        addr_all = cut(work, 3 * EC, EC).bitcast(u32)
        win_bf = cut(work, 4 * EC, EC // 2).bitcast(bf16)
        o_rec = 4 * EC + EC // 2
        recs_flat = cut(work, o_rec, 4 * ET)
        recs = v3(recs_flat, ET)
        recs_i = v3(recs_flat.bitcast(u32), ET)
        o_wT = o_rec + 4 * ET
        wT = v3(cut(work, o_wT, 2048), DC)
        o_M = o_wT + 2048
        Msb = v3(cut(work, o_M, 2048), DC)
        o_h = o_M + 2048
        h_sb = v3(cut(work, o_h, 1024), 2)
        assert o_h + 1024 <= 14336
        tot_sb = v3(cut(work, o_M, 512), KC)
        init_sb = v3(cut(work, o_wT, 512), KC)
        prod = v3(cut(work, o_M, 1024), 2)
        zrow = cut(work, o_M + 1024, D)
        gwr = v3(cut(work, o_rec, 2048), DC)
        stat1 = cut(work, o_h, NT * 6).rearrange("p (t s) -> p t s", s=6)
        dig = oh_all[:, 3 * NT * EC // 4:]
        ohd = [dig[:, k * LO * EC:(k + 1) * LO * EC] for k in range(2)]
        assert 2 * LO * EC <= NT * EC // 4 and LO * LO == NT
        hi_bf, lo_bf = (cut(work, o_h + k * (EC // 2), EC // 2).bitcast(bf16) for k in range(2))
        sel_a = v3(cut(work, o_wT, LO * P), LO)
        same = cut(work, o_wT + LO * P, P)
        same_g = cut(work, o_wT + LO * P + P, P)
        cnt = cut(work, o_wT + LO * P + 2 * P, P)
        k_col, g_col, a_col = (cut(work, o_wT + LO * P + (3 + k) * P, P) for k in range(3))
        xt, xn, xh, xT = (ring[:, 2 * k:2 * k + 2, :] for k in range(4))
        xa = [t_[:, k, :] for t_ in (xt, xh) for k in range(2)]
        o = 0
        wqkv = v3(cut(arena, o, 6144), DC); o += 6144
        wout = v3(cut(arena, o, 2048), DC); o += 2048
        G = v3(cut(arena, o, 2048), DC); o += 2048
        Tk = v3(cut(arena, o, 2048), DC); o += 2048
        prk = v3(cut(arena, o, 2048), DC); o += 2048
        prq = v3(cut(arena, o, 2048), DC); o += 2048
        wvT = v3(cut(arena, o, 2048), DC); o += 2048
        Bm = v3(cut(arena, o, 2048), DC); o += 2048
        kinv = cut(arena, o, 512); o += 512
        sim = v3(cut(arena, o, 256), DC); o += 256
        Abd = v3(cut(arena, o, 512), DC); o += 512
        oh = v3(cut(work, o_wT, 1024), 8)
        iotaT = cut(work, 0, ET)
        maskT = cut(work, ET, ET)
        wt_i = cut(work, 2 * ET, ET)[0:1, :].bitcast(i32)
        o = 8192
        L = v3(cut(work, o, NT * NX), NT); o += NT * NX
        Lx, eq = (v3(cut(work, o + k * TQ * NX, TQ * NX), TQ) for k in range(2)); o += 2 * TQ * NX
        Pfx = Lx
        OHA = v3(cut(work, o, TQ * NX).bitcast(bf16), 2); o += TQ * NX
        assert o <= 12288
        lt = v3(cut(work, 5120, 2 * TG * P), 2)[0:NX, :, :]
        Cx = v3(cut(work, 13568, (TQ + 1) * NX), TQ + 1)
        stat2 = cut(work, 6400, NT * 6).rearrange("p (t s) -> p t s", s=6)
        wts, sidx, gidx = (v3(cut(work, 12288 + k * 2 * NT, 2 * NT), 2) for k in range(3))
        sidx, gidx = sidx.bitcast(u32), gidx.bitcast(u32)
        small = [v3(cut(work, 12672 + k * 2 * TQ, 2 * TQ), 2) for k in range(2)]
        tops, share, tmp2 = (v3(cut(work, 12736 + k * 2 * NT, 2 * NT), 2) for k in range(3))
        xT4 = [ring[:, 4 * k:4 * k + 4, :] for k in range(2)]
        w1f, w2f = (v3(cut(work, k * 2048, 2048), DC) for k in range(2))
        b2s = [cut(work, 4096 + k * D, D) for k in range(2)]
        h_st = v3(cut(work, 5120, 4 * HN), 4)
        xr = v3(cut(work, 6400, 2048), 4)
        fin = v3(cut(work, 8448, 2048), 4)
        b1_sb = cut(work, o_h, D)[0:NX, :]

        ident = sb("ident", [P, P], f32)
        ones_f = sb("ones_f", [P, P], f32)
        iota_f = sb("iota_f", [P, P], f32)
        before = sb("before", [P, P], bf16)
        notbefore = sb("notbefore", [P, P], bf16)
        ones_b = sb("ones_b", [P, P], bf16)
        zero_b = sb("zero_b", [P, P], bf16)
        iota_b = sb("iota_b", [P, NT], bf16)
        eps = sb("eps", [P, 2], f32)
        mean1 = sb("mean1", [P, NT], f32)
        rstd1 = sb("rstd1", [P, NT], f32)
        l2s = sb("l2s", [P, NT], f32)
        xhs = sb("xhs", [P, NT], f32)
        sA = sb("sA", [P, NT], f32)
        sB = sb("sB", [P, NT], f32)
        addr_st = sb("addr_st", [P, 2, HC], u32)
        rec_st = sb("rec_st", [P, 2, HC, 4], f32)
        idx_st = sb("idx_st", [P, 2, 4], u32)
        ends = sb("ends", [P, NT], f32)
        wtot = sb("wtot", [P, NT], f32)
        nt_i = sb("nt_i", [P, NT], i32)
        ecol = sb("ecol", [NT, 1], f32)
        gcol = sb("gcol", [P, DC], f32)
        tcol = sb("tcol", [P, DC], f32)
        qs = sb("qs", [P, DC], f32)
        mx = sb("mx", [P, DC], f32)
        wg_sb = sb("wg_sb", [P, DC, NX], f32)
        b1T = sb("b1T", [P, DC, NX], f32)
        rt_st = sb("rt_st", [P, 2, 4], u32)
        p_i = sb("p_i", [P, 4], i32)
        p_f = sb("p_f", [P, 4], f32)
        rk_f = sb("rk_f", [P, HC], f32)
        rk_i = sb("rk_i", [P, 2 * HC], i32)
        rev = cut(work, 14208, NX)
        mean2, rstd2, nb2, ca, cb = mean1, rstd1, l2s, xhs, ends

        bank = [ctx.enter_context(nc.psum_tensor(f"bank{k}", [P, BANK], f32)) for k in range(8)]

        const_made = sem("const_made")
        fill_made = sem("fill_made")
        pool_step = sem("pool_step")
        dve_step = sem("dve_step")
        route_step = sem("route_step")
        pool_passed = sem("pool_passed")
        dve_passed = sem("dve_passed")
        act_passed = sem("act_passed")
        edges_in = sem("edges_in")
        rec_filled = sem("rec_filled")
        buf_filled = sem("buf_filled")
        xs_in = [sem(f"xs_in{k}") for k in range(8)]
        stat_read = sem("stat_read")
        var_made = sem("var_made")
        sd_made = sem("sd_made")
        oh_built = sem("oh_built")
        digits_made = sem("digits_made")
        pairs_summed = sem("pairs_summed")
        cnt_made = sem("cnt_made")
        totals_made = sem("totals_made")
        init_made = sem("init_made")
        ecol_made = sem("ecol_made")
        ranked = sem("ranked")
        rank_read = sem("rank_read")
        addr_made = sem("addr_made")
        scat = [sem(f"scat{k}") for k in range(2)]
        gw_in = sem("gw_in")
        qkv_in = sem("qkv_in")
        wt_tr = sem("wt_tr")
        wt_made = sem("wt_made")
        a1_in = [sem(f"a1_in{k}") for k in range(2)]
        xn_made = sem("xn_made")
        xh_made = sem("xh_made")
        xn_turned = sem("xn_turned")
        xT_made = sem("xT_made")
        gram_done = sem("gram_done")
        h_summed = sem("h_summed")
        h_made = sem("h_made")
        h_out = [sem(f"h_out{k}") for k in range(2)]
        qkv_scaled = sem("qkv_scaled")
        m_pe = sem("m_pe")
        m_act = sem("m_act")
        m_dve = sem("m_dve")
        a2_in = [sem(f"a2_in{k}") for k in range(4)]
        yn_made = sem("yn_made")
        yn_turned = sem("yn_turned")
        yT_made = sem("yT_made")
        mix_summed = sem("mix_summed")
        acc_set = sem("acc_set")
        recs_in = sem("recs_in")
        idx_made = sem("idx_made")
        iota_t = sem("iota_t")
        mask_made = sem("mask_made")
        wt_summed = sem("wt_summed")
        row_in = [sem(f"row_in{k}") for k in range(8)]
        oh_made = sem("oh_made")
        msg_summed = sem("msg_summed")
        acc_added = sem("acc_added")
        x1_out = [sem(f"x1_out{k}") for k in range(2)]
        var2_made = sem("var2_made")
        sd2_made = sem("sd2_made")
        xs_made = sem("xs_made")
        xs_turned = sem("xs_turned")
        xsT_made = sem("xsT_made")
        gated = sem("gated")
        L_made = sem("L_made")
        small_in = sem("small_in")
        b1_in = sem("b1_in")
        b1_turned = sem("b1_turned")
        b1T_made = sem("b1T_made")
        lsub_made = sem("lsub_made")
        x1b_made = sem("x1b_made")
        exp_made = sem("exp_made")
        oha_made = sem("oha_made")
        pfx_made = sem("pfx_made")
        route_made = sem("route_made")
        sent_first = sem("sent_first")
        sent = sem("sent")
        pre_in = sem("pre_in")
        norm2_made = sem("norm2_made")
        lt_made = sem("lt_made")
        turned_back = sem("turned_back")
        bin_in = [sem(f"bin_in{k}") for k in range(2)]
        w1_in = sem("w1_in")
        w2_in = sem("w2_in")
        b2_in = [sem(f"b2_in{k}") for k in range(2)]
        e_turned = sem("e_turned")
        e_bT = sem("e_bT")
        e_up = sem("e_up")
        e_h = sem("e_h")
        e_down = sem("e_down")
        e_o = sem("e_o")
        e_bTl = sem("e_bTl")
        e_hs = sem("e_hs")
        w1_high = sem("w1_high")
        w1_split = sem("w1_split")
        w2_high = sem("w2_high")
        w2_split = sem("w2_split")
        e_out = [sem(f"e_out{k}") for k in range(2)]
        og_in = [sem(f"og_in{k}") for k in range(4)]
        xr_in = [sem(f"xr_in{k}") for k in range(4)]
        fin_made = sem("fin_made")
        fin_out = [sem(f"fin_out{k}") for k in range(4)]

        x_t = x.rearrange("(t p) d -> t p d", p=P)
        ZR = -(-SLOTS // (P * (NB - EARLY)))
        buf_z = buf_all.rearrange("(k p r) d -> k p r d", p=P, r=ZR)
        H_t = H_d.rearrange("(t p) d -> t p d", p=P)
        x1_pt = x1_d.rearrange("(t p) d -> p t d", p=P)
        x1_t = x1_d.rearrange("(t p) d -> t p d", p=P)
        out_t = out.rearrange("(t p) d -> t p d", p=P)
        buf_e = buf_d.rearrange("(e c p) d -> e p c d", p=P, c=CT)
        o_e = o_d.rearrange("(e c p) d -> e p c d", p=P, c=CT)
        w1_e = W1.rearrange("e (c p) h -> e p c h", p=P)
        w2_e = W2.rearrange("e (c p) h -> e p c h", p=P)

        NCONST = 14
        block = ctx.enter_context(nc.Block())

        @block.sync
        def _(sp):
            for t_, s_ in ((src_i, src), (dst_i, dst), (w_f, edge_w)):
                sp.dma_start(t_, s_.rearrange("(p c) -> p c", p=P)).then_inc(edges_in, 16)

            sp.wait_ge(fill_made, 3)
            sp.dma_start(rec_d.rearrange("(q t) c -> q (t c)", q=P), recs_flat).then_inc(rec_filled, 16)

            def s_body(i):
                for k in range(8):
                    if not first(i):
                        sp.wait_ge(stat_read, i * 8 + (k - 7))
                    sp.dma_start(ring[:, k, :], x_t[i * 8 + k]).then_inc(xs_in[k], 16)
            rounds(sp, NT // 8, s_body)
            sp.wait_ge(rec_filled, 16)
            sp.dma_start(gwr, gnn_w.rearrange("(c p) f -> p c f", p=P)).then_inc(gw_in, 16)
            sp.wait_ge(stat_read, NT)

            def a1_body(i):
                for s in range(2):
                    if not first(i):
                        sp.wait_ge(xh_made, i * 2 + (s - 1))
                    sp.dma_start(xt[:, s, :], x_t[i * 2 + s]).then_inc(a1_in[s], 16)
                if not (isinstance(i, int) and i >= NB - EARLY):
                    sp.dma_start(buf_z[i], zrow[:, None, :].to_broadcast([P, ZR, D])).then_inc(buf_filled, 16)
                if first(i):
                    sp.dma_start(wg_sb[:, :, :], Wg.rearrange("(c p) e -> p c e", p=P)).then_inc(small_in, 16)
                    with nc.allow_non_contiguous_dma(reason="small"):
                        sp.dma_start(gcol[:, :], gamma.rearrange("(c p) -> p c", p=P)).then_inc(small_in, 16)
                        t2 = temp.rearrange("(c two) a b -> two c (a b)", two=2)
                        for hh in range(2):
                            tv = t2[hh].rearrange("c b -> b c")
                            sp.dma_start(tcol[hh * 64:hh * 64 + 64, :],
                                         tv.to_broadcast([64, DC])).then_inc(small_in, 16)
            rounds(sp, NB - EARLY, a1_body)
            sp.wait_ge(rank_read, HG * NB)
            sp.dma_start(wqkv, w_qkv.rearrange("(c p) f -> p c f", p=P)).then_inc(qkv_in, 16)
            sp.dma_start(wout, w_out.rearrange("(c p) f -> p c f", p=P)).then_inc(qkv_in, 16)
            for i in range(NB - EARLY, NT // 2):
                a1_body(i)

            sp.wait_ge(xh_made, NT)

            sp.wait_ge(gram_done, NT)

            def a2_body(i):
                for s in range(4):
                    if not first(i):
                        sp.wait_ge(acc_set, i * 4 + (s - 3))
                    sp.dma_start(xa[s], x_t[i * 4 + s]).then_inc(a2_in[s], 16)
            rounds(sp, NT // 4, a2_body)

            for k in range(2):
                sp.wait_ge(scat[k], 16 * HC * (NB // 2))
            sp.dma_start(recs_flat, rec_d.rearrange("(q t) c -> q (t c)", q=P)).then_inc(recs_in, 16)

            for k in range(2):
                sp.wait_ge(h_out[k], 16 * (NT // 2))
            sp.dma_start(b1_sb, b1[:, :]).then_inc(b1_in, 16)

            sp.wait_ge(acc_added, ET)
            HQ = TQ // 2
            for q in range(NQ):
                for h in range(2):
                    if q > 0:
                        sp.wait_ge(x1_out[h], q * 16)
                    t = q * TQ + h * HQ
                    sp.dma_start(x1_pt[:, t:t + HQ, :], acc[:, t:t + HQ, :]).then_inc(x1_out[h], 16)

            sp.dma_start(w1f, w1_e[0]).then_inc(w1_in, 16)
            sp.dma_start(w2f, w2_e[0]).then_inc(w2_in, 16)
            sp.dma_start(b2s[0], b2[0:1, :].to_broadcast([P, D])).then_inc(b2_in[0], 16)
            sp.wait_ge(sent_first, 32 * FIRST)
            sp.wait_ge(sent, 32 * (NT - FIRST))
            for h in range(2):
                sp.wait_ge(x1_out[h], 16 * NQ)

            def e_body(i):
                for s in range(2):
                    e = i * 2 + s
                    if not first(i):
                        sp.wait_ge(e_turned, i * 2 * CT + (s - 1) * CT)
                    sp.dma_start(bin_[s][:, :, :], buf_e[e]).then_inc(bin_in[s], 16)
                    if not (first(i) and s == 0):
                        sp.wait_ge(w1_split, i * 2 * DC + s * DC)
                        sp.dma_start(w1f, w1_e[e]).then_inc(w1_in, 16)
                        sp.wait_ge(w2_split, i * 2 * DC + s * DC)
                        sp.dma_start(w2f, w2_e[e]).then_inc(w2_in, 16)
                        if not first(i):
                            sp.wait_ge(e_o, i * 2 * CT + (s - 1) * CT)
                        sp.dma_start(b2s[s], b2[ds(e, 1), :].to_broadcast([P, D])).then_inc(b2_in[s], 16)
                    if not (first(i) and s == 0):
                        sp.wait_ge(e_o, i * 2 * CT + s * CT)
                        sp.dma_start(o_e[i * 2 + (s - 1)], osb[1 - s][:, :, :]).then_inc(e_out[1 - s], 16)
                    if s == 1:
                        sp.dma_start(x1_pre[:, ds(i, 1), :], x1_pt[:, ds(i, 1), :]).then_inc(pre_in, 16)
            rounds(sp, NX // 2, e_body)
            sp.wait_ge(e_o, NX * CT)
            sp.dma_start(o_e[NX - 1], osb[1][:, :, :]).then_inc(e_out[1], 16)

            def x1_load(i, k):
                sp.dma_start(xr[:, k, :], x1_t[i * 4 + k]).then_inc(xr_in[k], 16)

            def f_body(i):
                for k in range(4):
                    sp.wait_ge(fin_made, i * 4 + (k + 1))
                    sp.dma_start(out_t[i * 4 + k], fin[:, k, :]).then_inc(fin_out[k], 16)
            for k in range(4):
                x1_load(NPRE // 4, k)
            with sp.Fori(0, NPRE // 4) as i:
                f_body(i)
            with sp.Fori(NPRE // 4, NT // 4 - 1) as i:
                f_body(i)
                for k in range(4):
                    x1_load(i + 1, k)
            f_body(NT // 4 - 1)
            for k in range(4):
                sp.wait_ge(fin_out[k], 16 * (NT // 4))

        @block.gpsimd
        def _(pool):
            step = Chain(pool, pool_step, pool_passed)
            step(pool.memset(ident[:, :], 0.0))
            step(pool.memset(ones_b[:, :], 1.0))
            pool.affine_select(out=ident[:, :], in_=ident[:, :], compare_op=ALU.not_equal, fill=1.0, base=0,
                               pattern=[[-1, P]], channel_multiplier=1).then_inc(const_made, 1)
            pool.affine_select(out=before[:, :], in_=ones_b[:, :], compare_op=ALU.is_gt, fill=0.0, base=0,
                               pattern=[[1, P]], channel_multiplier=-1).then_inc(const_made, 1)
            pool.affine_select(out=notbefore[:, :], in_=ones_b[:, :], compare_op=ALU.is_ge, fill=0.0, base=0,
                               pattern=[[-1, P]], channel_multiplier=1).then_inc(const_made, 1)
            pool.memset(ones_f[:, :], 1.0).then_inc(const_made, 1)
            pool.memset(zero_b[:, :], 0.0).then_inc(const_made, 1)
            pool.memset(eps[:, 0:1], LN_EPS).then_inc(const_made, 1)
            pool.memset(eps[:, 1:2], 0.0).then_inc(const_made, 1)
            pool.iota(iota_b[:, :], [[1, NT]], base=0, channel_multiplier=0,
                      allow_small_or_imprecise_dtypes=True).then_inc(const_made, 1)
            pool.iota(iota_f[:, :], [[1, P]], base=0, channel_multiplier=0,
                      allow_small_or_imprecise_dtypes=True).then_inc(const_made, 1)
            pool.iota(k_col, [[0, 2 * LO], [1, KC]], base=0, channel_multiplier=0,
                      allow_small_or_imprecise_dtypes=True).then_inc(const_made, 1)
            pool.iota(g_col, [[1, 2], [0, LO * KC]], base=0, channel_multiplier=0,
                      allow_small_or_imprecise_dtypes=True).then_inc(const_made, 1)
            pool.iota(p_i[:, 0:1], [[0, 1]], base=0, channel_multiplier=1).then_inc(const_made, 1)
            pool.memset(rec_st[:, :, :, :], 0.0).then_inc(const_made, 1)
            pool.memset(b1T[:, :, :], 0.0).then_inc(const_made, 1)
            pool.memset(recs_flat, 0.0).then_inc(fill_made, 1)
            pool.wait_ge(fill_made, 1)
            pool.memset(recs[:, :, 1:2], -1.0).then_inc(fill_made, 1)
            pool.memset(zrow, 0.0).then_inc(fill_made, 1)
            pool.iota(rev[:, :], [[-1, NX]], base=NX, channel_multiplier=0,
                      allow_small_or_imprecise_dtypes=True).then_inc(fill_made, 1)

            pool.wait_ge(rec_filled, 16)

            def b_body(i):
                step.round(i, 8)
                for h in range(2):
                    if not first(i):
                        pool.wait_ge(scat[h], i * (16 * HC))
                    pool.wait_ge(addr_made, i * 2 + (h + 1))
                    c0 = i * (2 * HC) + h * HC
                    step(pool.tensor_copy(addr_st[:, h, :], addr_all[:, ds(c0, HC)]))
                    step(pool.tensor_copy(rec_st[:, h, :, 0].bitcast(i32), dst_i[:, ds(c0, HC)]))
                    step(pool.tensor_copy(rec_st[:, h, :, 1], srcl_f[:, ds(c0, HC)]))
                    step(pool.tensor_copy(rec_st[:, h, :, 2], w_f[:, ds(c0, HC)]))
                    for c in range(HC):
                        pool.indirect_dma_start(
                            rec_d, bass.IndirectOffsetOnAxis(addr_st[:, h, c:c + 1], 0),
                            rec_st[:, h, c, :], None).then_inc(scat[h], 16)
            rounds(pool, NB // 2, b_body)
            step.end(NB // 2)

            for k in range(2):
                pool.wait_ge(scat[k], 16 * HC * (NB // 2))
            pool.iota(iotaT, [[1, ET]], base=0, channel_multiplier=0,
                      allow_small_or_imprecise_dtypes=True).then_inc(iota_t, 1)
            for k in range(2):
                pool.wait_ge(h_out[k], 16 * (NT // 2))
            pool.wait_ge(acc_set, NT)

            def c_body(i):
                for h in range(2):
                    hold(pool, idx_made, i * 2 + (h + 1), pool_passed)
                    for k in range(4):
                        s = h * 4 + k
                        if not first(i):
                            hold(pool, msg_summed, i * 8 + (s - 7), pool_passed)
                        pool.indirect_dma_start(
                            ring[:, s, :], None, H_d,
                            bass.IndirectOffsetOnAxis(idx_st[:, h, k:k + 1], 0)).then_inc(row_in[s], 16)
            rounds(pool, ET // 8, c_body)

            pool.wait_ge(buf_filled, 16 * (NB - EARLY))

            for t in range(NT):
                if t % TQ == 0:
                    pool.wait_ge(route_made, t // TQ + 1)
                for j in range(2):
                    pool.indirect_dma_start(
                        buf_d, bass.IndirectOffsetOnAxis(sidx[:, j, t:t + 1], 0), acc[:, t, :], None,
                        bounds_check=SLOTS - 1,
                        oob_is_err=False).then_inc(sent_first if t < FIRST else sent, 16)

            for k in range(2):
                pool.wait_ge(e_out[k], 16 * (NX // 2))

            def f_body(i):
                step.round(i, 1)
                if not first(i):
                    for k in range(4):
                        pool.wait_ge(og_in[k], i * 32)
                step(pool.tensor_copy(rt_st[:, :, 0:4], gidx[:, :, ds(i * 4, 4)]))
                for k in range(4):
                    if not first(i):
                        hold(pool, fin_made, i * 4 + (k - 3), pool_passed)
                    for j in range(2):
                        pool.indirect_dma_start(
                            ring[:, 2 * k + j, :], None, o_d,
                            bass.IndirectOffsetOnAxis(rt_st[:, j, k:k + 1], 0)).then_inc(og_in[k], 16)
            rounds(pool, NT // 4, f_body)
            step.end(NT // 4)

        @block.scalar
        def _(act):
            act.wait_ge(const_made, NCONST)
            act.wait_ge(var_made, 1)
            act.activation(sA[:, :], l2s[:, :], ACT.Sqrt, bias=eps[:, 0:1], scale=1.0).then_inc(sd_made, 1)
            act.activation(sB[:, :], l2s[:, :], ACT.Sqrt, bias=eps[:, 1:2], scale=float(D)).then_inc(sd_made, 1)
            for m in range(DC):
                act.wait_ge(wt_tr, m + 1)
                act.copy(wT[:, m, :], bank[m][:, :]).then_inc(wt_made, 1)

            def a1_body(i):
                for s in range(2):
                    n = i * 2 + s
                    act.wait_ge(xn_turned, n + 1)
                    if not first(i):
                        act.wait_ge(h_summed, i * 2 + (s - 1))
                    act.copy(xT[:, s, :], bank[4][:, :]).then_inc(xT_made, 1)
                    act.wait_ge(h_summed, n + 1)
                    if not first(i):
                        act.wait_ge(h_out[s], i * 16)
                    act.copy(h_sb[:, s, :], bank[5 + s][:, :]).then_inc(h_made, 1)
                    act.wait_ge(h_made, n + 1)
                    act.dma_start(H_t[n], h_sb[:, s, :]).then_inc(h_out[s], 16)
            rounds(act, NT // 2, a1_body)

            act.wait_ge(gram_done, NT)
            for m in range(DC):
                act.copy(G[:, m, :], bank[m][:, :]).then_inc(m_act, 1)
            for m in range(DC):
                act.wait_ge(m_pe, m + 1)
                act.copy(wvT[:, m, :], bank[4 + m][:, :]).then_inc(m_act, 1)
            for m in range(DC):
                act.wait_ge(m_pe, 4 + m + 1)
                act.copy(Tk[:, m, :], bank[m][:, :]).then_inc(m_act, 1)
            act.wait_ge(small_in, 16 * 4)
            act.activation(tcol[:, :], tcol[:, :], ACT.Exp).then_inc(m_act, 1)
            act.wait_ge(m_dve, 9)
            act.activation(qs[:, :], qs[:, :], ACT.Sqrt).then_inc(m_act, 1)
            act.wait_ge(m_dve, 10)
            act.activation(kinv, kinv, ACT.Sqrt).then_inc(m_act, 1)
            act.wait_ge(m_dve, 11)
            act.activation(sim, sim, ACT.Exp).then_inc(m_act, 1)
            for m in range(DC):
                act.wait_ge(m_pe, 18 + m)
                act.copy(Bm[:, m, :], bank[m][:, :]).then_inc(m_act, 1)
            for m in range(DC):
                act.wait_ge(m_pe, 22 + m)
                act.copy(Msb[:, m, :], bank[4 + m][:, :]).then_inc(m_act, 1)

            def a2_body(i):
                for s in range(2):
                    act.wait_ge(yn_turned, i * 2 + (s + 1))
                    if not first(i):
                        act.wait_ge(mix_summed, i * 2 + (s - 1))
                    act.copy(xT[:, s, :], bank[s][:, :]).then_inc(yT_made, 1)
            rounds(act, NT // 2, a2_body)

            act.wait_ge(recs_in, 16)

            def idx_body(i):
                for h in range(2):
                    if not first(i):
                        for k in range(4):
                            hold(act, row_in[h * 4 + k], i * 16, act_passed)
                    act.copy(idx_st[:, h, :], recs_i[:, ds(i * 8 + h * 4, 4), 0]).then_inc(idx_made, 1)
            rounds(act, ET // 8, idx_body)

            act.wait_ge(b1_turned, 1)
            act.copy(b1T[:, :, :].rearrange("p c e -> p (c e)"), bank[7][:, 0:DC * NX]).then_inc(b1T_made, 1)

            def root(n, lo, hi):
                act.wait_ge(var2_made, n)
                act.activation(sA[:, lo:hi], sB[:, lo:hi], ACT.Sqrt, bias=eps[:, 0:1], scale=1.0).then_inc(sd2_made, 1)

            def d_body(q):
                def normed(k):
                    t = q * TQ + k
                    if k % (TQ // 2) == 0:
                        hold(act, x1_out[k // (TQ // 2)], q * 16 + 16, act_passed)
                    row = acc[:, ds(t, 1), :].rearrange("p a d -> p (a d)")
                    act.activation(row, row, ACT.Identity, bias=nb2[:, ds(t, 1)],
                                   scale=rstd2[:, ds(t, 1)]).then_inc(xs_made, 1)

                def logits_out(g):
                    act.wait_ge(gated, q * NG + (g + 1))
                    if not (first(q) and g < 2):
                        act.wait_ge(turned_back, q * NG + (g - 1))
                    act.copy(lt[:, g % 2, :], bank[4][0:NX, :]).then_inc(lt_made, 1)

                for k in range(TG):
                    normed(k)
                for k in range(TQ):
                    g, c = k // TG, k % TG
                    if k + TG < TQ:
                        normed(k + TG)
                    act.wait_ge(xs_turned, q * TQ + (k + 1))
                    if c == 0 and not (first(q) and g < 2):
                        act.wait_ge(gated, q * NG + (g - 1))
                    act.copy(xT4[g % 2][:, :, c * P:(c + 1) * P], v3(bank[c][:, :], DC)).then_inc(xsT_made, 1)
                    if c == 1 and g > 0:
                        logits_out(g - 1)
                logits_out(NG - 1)
                act.wait_ge(turned_back, q * NG + NG)
                act.copy(L[:, ds(q * TQ, TQ), :], v3(bank[7][:, 0:TQ * NX], TQ)).then_inc(L_made, 1)

            root(1, 0, TQ)
            act.wait_ge(norm2_made, 1)
            d_body(0)
            root(2, TQ, NORM[2] * TQ)
            act.wait_ge(norm2_made, 2)
            with act.Fori(1, NORM[2] - 1) as q:
                d_body(q)
            root(3, NORM[2] * TQ, NORM[3] * TQ)
            d_body(NORM[2] - 1)
            root(4, NORM[3] * TQ, NT)
            act.wait_ge(norm2_made, 4)
            with act.Fori(NORM[2], NQ) as q:
                d_body(q)
            act.wait_ge(lsub_made, 1)
            act.activation(L, L, ACT.Exp).then_inc(exp_made, 1)
            act.activation(share[:, 1, :], share[:, 1, :], ACT.Exp).then_inc(exp_made, 1)

            def e_rows(i, s):
                for c in range(CT):
                    act.wait_ge(e_turned, i * 2 * CT + (s * CT + c + 1))
                    if c == 0 and not (first(i) and s == 0):
                        act.wait_ge(e_up, i * 16 + s * 8)
                    act.copy(bTh[:, :, c * P:(c + 1) * P],
                             v3(bank[(s * CT + c) % 2][:, :], DC)).then_inc(e_bT, 1)

            def e_body(i):
                for s in range(2):
                    e_rows(i, s)
                    for g in range(8):
                        hc, hf = g // 2, g % 2
                        half = slice(hf * HN, (hf + 1) * HN)
                        bias = b1T[:, hc, ds(i * 2 + s, 1)]
                        act.wait_ge(e_up, i * 16 + (s * 8 + g + 1))
                        if g == 0 and not (first(i) and s == 0):
                            act.wait_ge(e_down, i * 2 * CT + s * CT)
                        if not (first(i) and s == 0 and g < 4):
                            act.wait_ge(e_hs, i * 16 + (s * 8 + g - 3))
                        act.sem_inc(act_passed, 1)
                        act.activation(h_st[:, g % 4, :], bank[2 + g % 4][:, 0:HN], ACT.Relu, bias=bias, scale=1.0)
                        act.activation(hTh[:, hc, half], bank[2 + g % 4][:, 0:HN], ACT.Relu, bias=bias,
                                       scale=1.0).then_inc(e_h, 1)
            rounds(act, NX // 2, e_body)

            act.wait_ge(pre_in, 16 * NPRE)

            def f_body(i, pre=False):
                for k in range(4):
                    t = i * 4 + k
                    if not pre:
                        hold(act, xr_in[k], i * 16 + (16 - 4 * NPRE), act_passed)
                    if not first(i):
                        hold(act, fin_out[k], i * 16, act_passed)
                    row = x1_pre[:, ds(t, 1), :].rearrange("p a d -> p (a d)") if pre else xr[:, k, :]
                    act.activation(fin[:, k, :], row, ACT.Identity, bias=cb[:, ds(t, 1)],
                                   scale=ca[:, ds(t, 1)]).then_inc(x1b_made, 1)
            f_body(0, pre=True)
            with act.Fori(1, NPRE // 4) as i:
                f_body(i, pre=True)
            with act.Fori(NPRE // 4, NT // 4) as i:
                f_body(i)

        @block.vector
        def _(dve):
            step = Chain(dve, dve_step)
            dve.wait_ge(const_made, NCONST)

            def moments(step, stat, mean, var, a, b):
                step(dve.tensor_tensor(a, stat[:, :, 1], stat[:, :, 4], ALU.subtract))
                step(dve.tensor_tensor(mean, stat[:, :, 1], stat[:, :, 4], ALU.add))
                step(dve.tensor_scalar(mean, mean, 0.5, None, ALU.mult))
                step(dve.tensor_tensor(a, a, a, ALU.mult))
                step(dve.tensor_scalar(a, a, 0.25, None, ALU.mult))
                step(dve.tensor_tensor(b, stat[:, :, 2], stat[:, :, 5], ALU.add))
                step(dve.scalar_tensor_tensor(out=var, in0=b, scalar=1.0 / D, in1=a, op0=ALU.mult, op1=ALU.add))

            dve.wait_ge(edges_in, 48)
            sh = P.bit_length() - 1
            lo_sh = LO.bit_length() - 1
            step(dve.tensor_scalar(tmp_i, src_i, sh, None, ALU.logical_shift_right))
            step(dve.tensor_copy(win_bf, tmp_i))
            step(dve.tensor_scalar(tmp_i, tmp_i, LO - 1, None, ALU.bitwise_and))
            step(dve.tensor_copy(lo_bf, tmp_i))
            step(dve.tensor_scalar(tmp_i, src_i, sh + lo_sh, None, ALU.logical_shift_right))
            step(dve.tensor_copy(hi_bf, tmp_i))
            step(dve.tensor_scalar(tmp_i, src_i, P - 1, None, ALU.bitwise_and))
            step(dve.tensor_copy(srcl_f, tmp_i))

            digit = [v3(d, 2 * PAIRS) for d in (hi_bf, lo_bf)]

            def digit_body(i):
                for d in range(2):
                    dve.tensor_tensor(ohd[d][:, ds(i * 512, 512)].rearrange("p (g a k) -> p g a k", g=8, a=LO),
                                      digit[d][:, ds(i * 8, 8), :][:, :, None, :].to_broadcast([P, 8, LO, KC]),
                                      iota_b[:, 0:LO][:, None, :, None].to_broadcast([P, 8, LO, KC]),
                                      ALU.is_equal).then_inc(digits_made, 1)
            rounds(dve, PAIRS // 4, digit_body)

            kb = KC.bit_length() - 1
            step(dve.tensor_scalar(p_i[:, 1:2], p_i[:, 0:1], KC - 1, None, ALU.bitwise_and))
            step(dve.tensor_scalar(p_i[:, 2:3], p_i[:, 0:1], kb, None, ALU.logical_shift_right))
            step(dve.tensor_scalar(p_i[:, 2:3], p_i[:, 2:3], LO - 1, None, ALU.bitwise_and))
            step(dve.tensor_scalar(p_i[:, 3:4], p_i[:, 0:1], kb + lo_sh, None, ALU.logical_shift_right))
            step(dve.tensor_copy(p_f[:, :], p_i[:, :]))
            step(dve.tensor_scalar(same_g, g_col, p_f[:, 3:4], None, ALU.is_equal))
            step(dve.tensor_scalar(same, k_col, p_f[:, 1:2], None, ALU.is_equal))
            step(dve.tensor_tensor(same, same, same_g, ALU.mult))
            step(dve.tensor_scalar(a_col[:, 0:LO], iota_f[:, 0:LO], p_f[:, 2:3], None, ALU.is_equal))
            step(dve.tensor_copy(sel_a, a_col[:, 0:LO][:, :, None].to_broadcast([P, LO, P])))
            dve.wait_ge(pairs_summed, 1)
            step(dve.tensor_tensor(cnt, bank[1][:, 0:P], same, ALU.mult))
            dve.tensor_tensor(cnt[:, 0:LO * KC], cnt[:, 0:LO * KC], cnt[:, LO * KC:], ALU.add).then_inc(cnt_made, 1)

            def window_onehots(n):
                for c in range(HG):
                    g = n * HG + c
                    dve.tensor_tensor(oh_all[:, ds(g * 512, 512)].rearrange("p (k w) -> p k w", k=KC),
                                      win_bf[:, ds(g * KC, KC)][:, :, None].to_broadcast([P, KC, NT]),
                                      iota_b[:, None, :].to_broadcast([P, KC, NT]),
                                      ALU.is_equal).then_inc(oh_built, 1)
            for n in range(EARLY):
                window_onehots(n)
            dve.wait_ge(totals_made, 1)
            step(dve.tensor_copy(tot_sb, bank[0][:, :].rearrange("p (w k) -> p k w", k=KC)))
            step(dve.memset(init_sb[:, 0, :], 0.0))
            for m in range(KC - 1):
                step(dve.tensor_tensor(init_sb[:, m + 1, :], init_sb[:, m, :], tot_sb[:, m, :], ALU.add))
            step(dve.tensor_tensor(wtot[:, :], init_sb[:, KC - 1, :], tot_sb[:, KC - 1, :], ALU.add))
            step(dve.tensor_scalar(wtot[:, :], wtot[:, :], float(P - 1), None, ALU.add))
            step(dve.tensor_copy(nt_i[:, :], wtot[:, :]))
            step(dve.tensor_scalar(nt_i[:, :], nt_i[:, :], sh, None, ALU.logical_shift_right))
            step(dve.tensor_copy(wtot[:, :], nt_i[:, :]))
            step(dve.memset(sA[:, :], 0.0))
            step(dve.tensor_tensor_scan(ends[:, :], wtot[:, :], sA[:, :], 0.0, ALU.add, ALU.add))
            step(dve.tensor_tensor(sA[:, :], ends[:, :], wtot[:, :], ALU.subtract))
            step(dve.tensor_scalar(sA[:, :], sA[:, :], float(P), None, ALU.mult))
            dve.tensor_tensor(init_sb, init_sb, sA[:, None, :].to_broadcast([P, KC, NT]),
                              ALU.add).then_inc(init_made, 1)

            def rank_group(n, c):
                g = n * HG + c
                dve.wait_ge(ranked, g + 1)
                dve.tensor_tensor(prod[:, c % 2, :], bank[7][:, :], oh_all[:, ds(g * 512, 512)],
                                  ALU.mult).then_inc(rank_read, 1)
                dve.wait_ge(rank_read, g + 1)
                step(dve.tensor_reduce(rk_f[:, c * KC:(c + 1) * KC],
                                       prod[:, c % 2, :].rearrange("p (k w) -> p k w", k=KC), AX, ALU.add))

            def addresses(n):
                step(dve.tensor_copy(rk_i[:, 0:HC], rk_f[:, :]))
                step(dve.tensor_scalar(rk_i[:, HC:2 * HC], rk_i[:, 0:HC], sh, None, ALU.logical_shift_right))
                step(dve.tensor_scalar(rk_i[:, 0:HC], rk_i[:, 0:HC], P - 1, None, ALU.bitwise_and))
                step(dve.scalar_tensor_tensor(out=addr_all[:, ds(n * HC, HC)], in0=rk_i[:, 0:HC], scalar=float(ET),
                                              in1=rk_i[:, HC:2 * HC], op0=ALU.mult, op1=ALU.add))
                dve.sem_inc(addr_made, 1)

            for n in range(EARLY):
                for c in range(HG):
                    rank_group(n, c)
                addresses(n)

            def s_body(i):
                for k in range(8):
                    dve.wait_ge(xs_in[k], i * 16 + 16)
                    dve.bn_stats(stat1[:, ds(i * 8 + k, 1), :].rearrange("p a s -> p (a s)"),
                                 ring[:, k, :]).then_inc(stat_read, 1)
            rounds(dve, NT // 8, s_body)
            dve.wait_ge(stat_read, NT)
            moments(step, stat1, mean1[:, :], l2s[:, :], sA[:, :], sB[:, :])
            dve.sem_inc(var_made, 1)
            dve.wait_ge(sd_made, 2)
            step(dve.reciprocal(rstd1[:, :], sA[:, :]))
            step(dve.tensor_tensor(sB[:, :], sB[:, :], rstd1[:, :], ALU.mult))
            step(dve.tensor_scalar(sB[:, :], sB[:, :], L2_EPS, None, ALU.max))
            step(dve.reciprocal(l2s[:, :], sB[:, :]))
            step(dve.tensor_scalar(l2s[:, :], l2s[:, :], float(D) ** 0.5, None, ALU.mult))
            step(dve.tensor_tensor(xhs[:, :], l2s[:, :], rstd1[:, :], ALU.mult))

            def a1_body(i, ranks=True):
                if ranks:
                    step.round(i, HG + 4)
                    window_onehots(i + EARLY)
                for s in range(2):
                    n = i * 2 + s
                    dve.wait_ge(a1_in[s], i * 16 + 16)
                    if not first(i):
                        dve.wait_ge(xn_turned, i * 2 + (s - 1))
                    dve.tensor_scalar(xn[:, s, :], xt[:, s, :], mean1[:, ds(n, 1)], rstd1[:, ds(n, 1)],
                                      ALU.subtract, ALU.mult).then_inc(xn_made, 1)
                    if not first(i):
                        dve.wait_ge(gram_done, i * 2 + (s - 1))
                    dve.tensor_scalar(xh[:, s, :], xt[:, s, :], mean1[:, ds(n, 1)], xhs[:, ds(n, 1)],
                                      ALU.subtract, ALU.mult).then_inc(xh_made, 1)
                    if ranks:
                        rank_group(i + EARLY, 2 * s)
                        rank_group(i + EARLY, 2 * s + 1)
                if ranks:
                    addresses(i + EARLY)
            rounds(dve, NB - EARLY, a1_body)
            step.end(NB - EARLY)
            for i in range(NB - EARLY, NT // 2):
                a1_body(i, ranks=False)

            dve.wait_ge(qkv_in, 32)
            dve.wait_ge(small_in, 16 * 4)
            for m in range(DC):
                dve.tensor_scalar(wqkv[:, m, :], wqkv[:, m, :], gcol[:, m:m + 1], None,
                                  ALU.mult).then_inc(qkv_scaled, 1)
            dve.wait_ge(qkv_scaled, DC)
            for m in range(DC):
                dve.wait_ge(m_act, 9 + m)
                dve.tensor_tensor(prk[:, m, :], bank[m][:, :], wqkv[:, m, D:2 * D], ALU.mult).then_inc(m_dve, 1)
            for m in range(DC):
                dve.wait_ge(m_pe, 8 + m + 1)
                dve.tensor_tensor(prq[:, m, :], bank[4 + m][:, :], wqkv[:, m, 0:D], ALU.mult).then_inc(m_dve, 1)
            step(dve.memset(Abd, 0.0))
            dve.wait_ge(m_pe, 13)
            dve.tensor_scalar(qs[:, :], bank[4][:, 0:DC], 0.0, None, ALU.max).then_inc(m_dve, 1)
            dve.tensor_scalar(kinv, bank[5][:, :], 0.0, None, ALU.max).then_inc(m_dve, 1)
            dve.wait_ge(m_act, 14)
            step(dve.tensor_scalar(qs[:, :], qs[:, :], L2_EPS, None, ALU.max))
            step(dve.reciprocal(qs[:, :], qs[:, :]))
            step(dve.tensor_tensor(qs[:, :], qs[:, :], tcol[:, :], ALU.mult))
            step(dve.tensor_scalar(qs[:, :], qs[:, :], SCALE, None, ALU.mult))
            dve.wait_ge(m_act, 15)
            step(dve.tensor_scalar(kinv, kinv, L2_EPS, None, ALU.max))
            step(dve.reciprocal(kinv, kinv))
            dve.wait_ge(m_pe, 17)
            for m in range(DC):
                for lo in (0, DH):
                    r = slice(lo, lo + DH)
                    step(dve.tensor_tensor(sim[r, m, :], bank[m][r, lo:lo + DH],
                                           kinv[r, m * P + lo:m * P + lo + DH], ALU.mult))
                step(dve.tensor_scalar(sim[:, m, :], sim[:, m, :], qs[:, m:m + 1], None, ALU.mult))
            step(dve.tensor_reduce(mx[:, :], sim, AX, ALU.max))
            dve.tensor_tensor(sim, sim, mx[:, :, None].to_broadcast([P, DC, DH]),
                              ALU.subtract).then_inc(m_dve, 1)
            dve.wait_ge(m_act, 16)
            step(dve.tensor_reduce(mx[:, :], sim, AX, ALU.add))
            step(dve.reciprocal(mx[:, :], mx[:, :]))
            for m in range(DC):
                for lo in (0, DH):
                    r = slice(lo, lo + DH)
                    dve.tensor_scalar(Abd[r, m, lo:lo + DH], sim[r, m, :], mx[r, m:m + 1], None,
                                      ALU.mult).then_inc(m_dve, 1)

            def acc_tile(i, s):
                n = i * 4 + (s - 2)
                dve.wait_ge(mix_summed, n + 1)
                dve.scalar_tensor_tensor(
                    out=acc[:, ds(n, 1), :].rearrange("p a d -> p (a d)"), in0=bank[2 + s % 2][:, :],
                    scalar=l2s[:, ds(n, 1)], in1=xa[(s - 2) % 4], op0=ALU.mult, op1=ALU.add).then_inc(acc_set, 1)

            def a2_body(i):
                for s in range(4):
                    n = i * 4 + s
                    dve.wait_ge(a2_in[s], i * 16 + 16)
                    if not (first(i) and s < 2):
                        dve.wait_ge(yn_turned, i * 4 + (s - 1))
                    dve.tensor_scalar(xn[:, s % 2, :], xa[s], mean1[:, ds(n, 1)], rstd1[:, ds(n, 1)],
                                      ALU.subtract, ALU.mult).then_inc(yn_made, 1)
                    if not (first(i) and s < 2):
                        acc_tile(i, s)
            rounds(dve, NT // 4, a2_body)
            for s in range(2):
                acc_tile(NT // 4, s)
            dve.wait_ge(acc_set, NT)

            dve.wait_ge(iota_t, 1)
            dve.wait_ge(ecol_made, 1)
            step(dve.tensor_copy(ecol[:, :], bank[0][0:NT, 0:1]))
            dve.tensor_scalar(maskT[0:NT, :], iotaT[0:NT, :], ecol[:, 0:1], None, ALU.is_ge).then_inc(mask_made, 1)
            dve.wait_ge(wt_summed, 1)
            for c0 in range(0, ET, BANK):
                n = min(BANK, ET - c0)
                step(dve.tensor_scalar(wt_i[:, c0:c0 + n], bank[1 + c0 // BANK][0:1, 0:n], float(NT - 1), float(D),
                                       ALU.min, ALU.mult))
            dve.wait_ge(recs_in, 16)

            def onehot(i, s):
                t = i * 8 + s
                if not first(i):
                    dve.wait_ge(msg_summed, i * 8 + (s - 7))
                dve.tensor_scalar(oh[:, s, :], iota_f[:, :], recs[:, ds(t, 1), 1], recs[:, ds(t, 1), 2],
                                  ALU.is_equal, ALU.mult).then_inc(oh_made, 1)

            win_reg = [dve.alloc_register(f"window{k}") for k in range(8)]

            def windows(t, n):
                dve.load(win_reg[:n], wt_i[0:1, ds(t, n)])
                return [dve.snap(r, min_val=0, max_val=(NT - 1) * D) for r in win_reg[:n]]

            def add(off, i, s, back=0):
                t = i * 8 + (s - back)
                dve.wait_ge(msg_summed, t + 1)
                if not (isinstance(t, int) and t == 0):
                    dve.wait_ge(acc_added, t)
                dve.tensor_tensor(arena[:, ds(off, D)], arena[:, ds(off, D)], bank[s][:, :],
                                  ALU.add).then_inc(acc_added, 1)

            def c_body(i):
                offs = windows(i * 8 - (0 if first(i) else 4), 4 if first(i) else 8)
                for k in range(4):
                    onehot(i, k)
                    if not first(i):
                        add(offs[k], i, 4 + k, 8)
                for k in range(4):
                    onehot(i, 4 + k)
                    add(offs[k - 4], i, k)
            rounds(dve, ET // 8, c_body)
            for k, off in enumerate(windows(ET - 4, 4)):
                add(off, ET // 8, 4 + k, 8)
            dve.wait_ge(acc_added, ET)

            step_r = Chain(dve, route_step)

            def norm_stats(lo, hi):
                at = slice(lo, hi)

                def stats(t):
                    dve.bn_stats(stat2[:, ds(t, 1), :].rearrange("p a s -> p (a s)"),
                                 acc[:, ds(t, 1), :].rearrange("p a d -> p (a d)")).then_inc(stat_read, 1)
                with dve.Fori(lo // 8, hi // 8) as i:
                    for k in range(8):
                        stats(i * 8 + k)
                dve.wait_ge(stat_read, NT + hi)
                moments(step, stat2[:, at, :], mean2[:, at], sB[:, at], sA[:, at], nb2[:, at])
                dve.sem_inc(var2_made, 1)

            def norm_factors(lo, hi, n):
                at = slice(lo, hi)
                dve.wait_ge(sd2_made, n)
                step(dve.reciprocal(rstd2[:, at], sA[:, at]))
                step(dve.scalar_tensor_tensor(out=nb2[:, at], in0=mean2[:, at], scalar=-1.0, in1=rstd2[:, at],
                                              op0=ALU.mult, op1=ALU.mult))
                dve.sem_inc(norm2_made, 1)

            parts = [(NORM[k] * TQ, NORM[k + 1] * TQ) for k in range(4)]
            for k in range(2):
                norm_stats(*parts[k])
                norm_factors(*parts[k], k + 1)

            def over_e(v):
                return v[:, :, None].to_broadcast([P, v.shape[1], NX])

            def route_body(q):
                step = step_r
                step.round(q, 24 + TQ)
                at = ds(q * TQ, TQ)
                revb = rev[:, None, :].to_broadcast([P, TQ, NX])
                slot, rank = small
                dve.wait_ge(L_made, q + 1)
                for j, l_ in enumerate((L[:, at, :], Lx)):
                    step(dve.tensor_reduce(tops[:, j, at], l_, AX, ALU.max))
                    step(dve.tensor_tensor(eq, l_, over_e(tops[:, j, at]), ALU.is_equal))
                    step(dve.tensor_tensor(eq, eq, revb, ALU.mult))
                    step(dve.tensor_reduce(slot[:, j, :], eq, AX, ALU.max))
                    step(dve.tensor_tensor(v3(OHA[:, j, :], TQ), revb, over_e(slot[:, j, :]), ALU.is_equal))
                    if j == 0:
                        step(dve.scalar_tensor_tensor(out=Lx, in0=v3(OHA[:, 0, :], TQ), scalar=-3e38, in1=l_,
                                                      op0=ALU.mult, op1=ALU.add))
                dve.sem_inc(oha_made, 1)
                step(dve.tensor_scalar(slot, slot, -1.0, float(NX), ALU.mult, ALU.add))
                dve.wait_ge(pfx_made, q + 1)
                if first(q):
                    step(dve.memset(Cx[:, 0, :], 0.0))
                else:
                    step(dve.tensor_copy(Cx[:, 0, :], Cx[:, TQ, :]))
                for k in range(TQ):
                    step(dve.tensor_tensor(Cx[:, k + 1, :], Cx[:, k, :], bank[6][:, k * NX:(k + 1) * NX], ALU.add))
                step(dve.tensor_tensor(Pfx, v3(bank[5][:, 0:TQ * NX], TQ), Cx[:, 0:TQ, :], ALU.add))
                for j in range(2):
                    step(dve.tensor_tensor(eq, v3(OHA[:, j, :], TQ), Pfx, ALU.mult))
                    step(dve.tensor_reduce(rank[:, j, :], eq, AX, ALU.add))
                step(dve.scalar_tensor_tensor(out=slot, in0=slot, scalar=float(CAP), in1=rank, op0=ALU.mult,
                                              op1=ALU.add))
                step(dve.tensor_scalar(wts[:, :, at], rank, float(CAP), None, ALU.is_lt))
                step(dve.scalar_tensor_tensor(out=slot, in0=wts[:, :, at], scalar=-FAR, in1=slot, op0=ALU.mult,
                                              op1=ALU.add))
                step(dve.tensor_scalar(slot, slot, FAR, None, ALU.add))
                step(dve.tensor_copy(sidx[:, :, at], slot))
                step(dve.tensor_scalar(gidx[:, :, at], slot, float(SLOTS - 1), None, ALU.min))
                dve.sem_inc(route_made, 1)

            for q in range(2):
                route_body(q)
                norm_stats(*parts[q + 2])
            for q in range(2):
                norm_factors(*parts[q + 2], q + 3)
                route_body(q + 2)
            with dve.Fori(4, NQ) as q:
                route_body(q)
            step_r.end(NQ)

            dve.wait_ge(L_made, NQ)
            step(dve.tensor_tensor(share[:, 1, :], tops[:, 1, :], tops[:, 0, :], ALU.subtract))
            step(dve.tensor_tensor(L, L, over_e(tops[:, 0, :]), ALU.subtract))
            dve.sem_inc(lsub_made, 1)
            dve.wait_ge(exp_made, 2)
            step(dve.tensor_reduce(tmp2[:, 0, :], L, AX, ALU.add))
            step(dve.reciprocal(share[:, 0, :], tmp2[:, 0, :]))
            step(dve.tensor_tensor(share[:, 1, :], share[:, 1, :], share[:, 0, :], ALU.mult))
            step(dve.tensor_tensor(tmp2[:, 0, :], share[:, 0, :], share[:, 1, :], ALU.add))
            step(dve.tensor_scalar(tmp2[:, 0, :], tmp2[:, 0, :], 1e-9, None, ALU.max))
            step(dve.reciprocal(tmp2[:, 1, :], tmp2[:, 0, :]))
            step(dve.tensor_tensor(share, share, tmp2[:, 1, :][:, None, :].to_broadcast([P, 2, NT]), ALU.mult))
            step(dve.tensor_tensor(wts, wts, share, ALU.mult))
            step(dve.tensor_tensor(tmp2[:, 0, :], wts[:, 0, :], wts[:, 1, :], ALU.add))
            step(dve.tensor_scalar(tmp2[:, 0, :], tmp2[:, 0, :], 1e-12, None, ALU.is_le))
            step(dve.tensor_tensor(tmp2[:, 1, :], tmp2[:, 0, :], rstd2[:, :], ALU.mult))
            step(dve.tensor_scalar(ca[:, :], tmp2[:, 1, :], 1.0, None, ALU.add))
            step(dve.tensor_tensor(cb[:, :], tmp2[:, 0, :], nb2[:, :], ALU.mult))

            def bias_add(i, s, c, back=0):
                w = (s - back) % 2
                n = i * 2 * CT + ((s - back) * CT + c)
                dve.wait_ge(e_down, n + 1)
                if c == 0:
                    dve.wait_ge(b2_in[w], i * 16 + (16 if s >= back else 0))
                    if s >= back and not first(i):
                        dve.wait_ge(e_out[w], i * 16)
                    if s < back and not (isinstance(i, int) and i < 2):
                        dve.wait_ge(e_out[w], i * 16 - 16)
                dve.tensor_tensor(osb[w][:, c, :], bank[6 + (w * CT + c) % 2][:, :], b2s[w],
                                  ALU.add).then_inc(e_o, 1)

            def low_rows(i, s, c):
                n = i * 2 * CT + (s * CT + c)
                dve.wait_ge(e_bT, n + 1)
                at = slice(c * P, (c + 1) * P)
                dve.tensor_tensor(bTl[:, :, at], v3(bank[(s * CT + c) % 2][:, :], DC), bTh[:, :, at].bitcast(f32),
                                  ALU.subtract).then_inc(e_bTl, 1)

            def split(wh, wl, wf, high, low, n, k):
                dve.tensor_copy(wh[:, k, :], wf[:, k, :]).then_inc(high, 1)
                dve.wait_ge(high, n + 1)
                dve.tensor_tensor(wl[:, k, :], wf[:, k, :], wh[:, k, :].bitcast(f32),
                                  ALU.subtract).then_inc(low, 1)

            def low_h(i, s, g):
                dve.wait_ge(e_h, i * 16 + (s * 8 + g + 1))
                hc, half = g // 2, slice((g % 2) * HN, (g % 2 + 1) * HN)
                dve.tensor_tensor(hTl[:, hc, half], h_st[:, g % 4, :], hTh[:, hc, half].bitcast(f32),
                                  ALU.subtract).then_inc(e_hs, 1)

            def e_body(i):
                for s in range(2):
                    low_rows(i, s, 0)
                    low_rows(i, s, 1)
                    for c in range(CT):
                        if not (first(i) and s == 0):
                            bias_add(i, s, c, 1)
                        if c + 2 < CT:
                            low_rows(i, s, c + 2)
                        if c < DC and not (first(i) and s == 0):
                            if c == 0:
                                dve.wait_ge(w1_in, i * 32 + (s + 1) * 16)
                            split(w1h, w1l, w1f, w1_high, w1_split, i * 2 * DC + (s * DC + c), c)
                    for g in range(8):
                        low_h(i, s, g)
                        if g < DC and not (first(i) and s == 0):
                            if g == 0:
                                dve.wait_ge(w2_in, i * 32 + (s + 1) * 16)
                            split(w2h, w2l, w2f, w2_high, w2_split, i * 2 * DC + (s * DC + g), g)

            dve.wait_ge(sent_first, 32 * FIRST)
            dve.wait_ge(w1_in, 16)
            for k in range(DC):
                split(w1h, w1l, w1f, w1_high, w1_split, k, k)
            dve.wait_ge(w2_in, 16)
            for k in range(DC):
                split(w2h, w2l, w2f, w2_high, w2_split, k, k)
            e_body(0)
            e_body(1)
            with dve.Fori(2, NX // 2) as i:
                e_body(i)
            for c in range(CT):
                bias_add(NX // 2, 0, c, 1)

            def f_body(i):
                step.round(i, 4)
                for k in range(4):
                    t = i * 4 + k
                    dve.wait_ge(x1b_made, t + 1)
                    dve.wait_ge(og_in[k], i * 32 + 32)
                    step(dve.scalar_tensor_tensor(out=fin[:, k, :], in0=ring[:, 2 * k, :],
                                                  scalar=wts[:, 0, ds(t, 1)], in1=fin[:, k, :],
                                                  op0=ALU.mult, op1=ALU.add))
                    dve.scalar_tensor_tensor(out=fin[:, k, :], in0=ring[:, 2 * k + 1, :],
                                             scalar=wts[:, 1, ds(t, 1)], in1=fin[:, k, :],
                                             op0=ALU.mult, op1=ALU.add).then_inc(fin_made, 1)
            rounds(dve, NT // 4, f_body)
            step.end(NT // 4)

        @block.tensor
        def _(pe):
            def mm(o_, l_, r_, start, stop, **kw):
                return nc.tensor.matmul(o_, l_, r_, start=start, stop=stop, **kw)

            def turn(o_, in_):
                return nc.tensor.transpose(o_, in_, ident[:, :])

            pe.wait_ge(const_made, NCONST)
            mm(bank[1][:, 0:P], zero_b[:, :], zero_b[:, :], True, False, skip_group_check=True)

            def pair_body(i):
                for h in range(2):
                    pe.wait_ge(digits_made, i * 4 + 2 * (h + 1))
                    for c in range(4):
                        at = ds((i * 8 + h * 4 + c) * 2 * LO * KC, 2 * LO * KC)
                        mm(bank[1][:, 0:P], ohd[0][:, at], ohd[1][:, at], False, False, skip_group_check=True)
            rounds(pe, PAIRS // 8, pair_body)
            mm(bank[1][:, 0:P], zero_b[:, :], zero_b[:, :], False, True,
               skip_group_check=True).then_inc(pairs_summed, 1)
            pe.wait_ge(cnt_made, 1)
            for a in range(LO):
                last = mm(bank[0][:, a * LO * KC:(a + 1) * LO * KC], sel_a[:, a, :], cnt[:, 0:LO * KC], True, True)
            last.then_inc(totals_made, 1)
            pe.wait_ge(init_made, 1)
            mm(bank[7][:, :], ident[:, :], init_sb.rearrange("p k w -> p (k w)"), True, False,
               skip_group_check=True)

            def rank_on(n, c):
                g = n * HG + c
                pe.wait_ge(oh_built, g + 1)
                mm(bank[7][:, :], before[:, :], oh_all[:, ds(g * 512, 512)], False, True,
                   skip_group_check=True).then_inc(ranked, 1)

            def rank_off(n, c):
                g = n * HG + c
                pe.wait_ge(rank_read, g + 1)
                mm(bank[7][:, :], notbefore[:, :], oh_all[:, ds(g * 512, 512)], False, True,
                   skip_group_check=True)

            for n in range(EARLY):
                for c in range(HG):
                    rank_on(n, c)
                    rank_off(n, c)

            pe.wait_ge(gw_in, 16)
            for m in range(DC):
                for k in range(DC):
                    last = turn(bank[m][:, k * P:(k + 1) * P], gwr[:, k, m * P:(m + 1) * P])
                last.then_inc(wt_tr, 1)
            pe.wait_ge(wt_made, DC)

            for m in range(DC):
                mm(bank[m][:, 0:P], zero_b[:, :], zero_b[:, :], True, False, skip_group_check=True)

            def a1_body(i, ranks=True):
                r = i + EARLY
                for s in range(2):
                    n = i * 2 + s
                    pe.wait_ge(xn_made, n + 1)
                    if not (first(i) and s == 0):
                        pe.wait_ge(xT_made, n)
                    for m in range(DC):
                        last = turn(bank[4][:, m * P:(m + 1) * P], xn[:, s, m * P:(m + 1) * P])
                    last.then_inc(xn_turned, 1)
                    if ranks:
                        rank_on(r, 2 * s)
                    pe.wait_ge(xh_made, n + 1)
                    for m in range(DC):
                        last = mm(bank[m][:, :], xh[:, s, m * P:(m + 1) * P], xh[:, s, :], False, False,
                                  skip_group_check=True)
                    last.then_inc(gram_done, 1)
                    if ranks:
                        rank_off(r, 2 * s)
                        rank_on(r, 2 * s + 1)
                    pe.wait_ge(xT_made, n + 1)
                    if not first(i):
                        pe.wait_ge(h_made, i * 2 + (s - 1))
                    for m in range(DC):
                        last = mm(bank[5 + s][:, :], xT[:, s, m * P:(m + 1) * P], wT[:, m, :], m == 0, m == DC - 1)
                    last.then_inc(h_summed, 1)
                    if ranks:
                        rank_off(r, 2 * s + 1)
            rounds(pe, NB - EARLY, a1_body)
            for i in range(NB - EARLY, NT // 2):
                a1_body(i, ranks=False)

            pe.wait_ge(qkv_scaled, DC)
            pe.wait_ge(h_made, NT)
            for m in range(DC):
                for k in range(DC):
                    last = turn(bank[4 + m][:, k * P:(k + 1) * P],
                                wqkv[:, k, 2 * D + m * P:2 * D + (m + 1) * P])
                last.then_inc(m_pe, 1)
            pe.wait_ge(m_act, 4)
            for m in range(DC):
                for k in range(DC):
                    last = mm(bank[m][:, :], G[:, k, m * P:(m + 1) * P], wqkv[:, k, D:2 * D], k == 0, k == DC - 1)
                last.then_inc(m_pe, 1)
            pe.wait_ge(m_act, 8)
            for m in range(DC):
                for k in range(DC):
                    last = mm(bank[4 + m][:, :], G[:, k, m * P:(m + 1) * P], wqkv[:, k, 0:D], k == 0, k == DC - 1)
                last.then_inc(m_pe, 1)
            pe.wait_ge(m_dve, 8)
            for m in range(DC):
                for k in range(DC):
                    mm(bank[4][:, m:m + 1], prq[:, k, m * P:(m + 1) * P], ones_f[:, 0:1], k == 0, k == DC - 1)
            for k in range(DC):
                last = mm(bank[5][:, :], ones_f[:, :], prk[:, k, :], k == 0, k == DC - 1)
            last.then_inc(m_pe, 1)
            pe.wait_ge(m_act, 12)
            for m in range(DC):
                for k in range(DC):
                    last = mm(bank[m][:, 0:P], wqkv[:, k, m * P:(m + 1) * P], Tk[:, k, m * P:(m + 1) * P],
                              k == 0, k == DC - 1)
                last.then_inc(m_pe, 1)
            pe.wait_ge(m_dve, 19)
            for m in range(DC):
                mm(bank[m][:, :], Abd[:, m, :], wout[:, m, :], True, True).then_inc(m_pe, 1)
            pe.wait_ge(m_act, 20)
            for m in range(DC):
                for k in range(DC):
                    last = mm(bank[4 + m][:, :], wvT[:, k, m * P:(m + 1) * P], Bm[:, k, :], k == 0, k == DC - 1)
                last.then_inc(m_pe, 1)
            pe.wait_ge(m_act, 24)

            def mix(i, s):
                k = (s - 1) % 2
                pe.wait_ge(yT_made, i * 4 + s)
                if not (first(i) and s < 3):
                    pe.wait_ge(acc_set, i * 4 + (s - 2))
                for m in range(DC):
                    last = mm(bank[2 + k][:, :], xT[:, k, m * P:(m + 1) * P], Msb[:, m, :], m == 0, m == DC - 1)
                last.then_inc(mix_summed, 1)

            def a2_body(i):
                for s in range(4):
                    n = i * 4 + s
                    pe.wait_ge(yn_made, n + 1)
                    if not (first(i) and s < 2):
                        pe.wait_ge(yT_made, i * 4 + (s - 1))
                    for m in range(DC):
                        last = turn(bank[s % 2][:, m * P:(m + 1) * P], xn[:, s % 2, m * P:(m + 1) * P])
                    last.then_inc(yn_turned, 1)
                    if not (first(i) and s == 0):
                        mix(i, s)
            rounds(pe, NT // 4, a2_body)
            mix(NT // 4, 0)

            pe.wait_ge(acc_set, NT)
            pe.wait_ge(yT_made, NT)
            mm(bank[0][0:NT, 0:1], ends[0:1, :], ones_f[0:1, 0:1], True, True).then_inc(ecol_made, 1)
            pe.wait_ge(mask_made, 1)
            for c0 in range(0, ET, BANK):
                n = min(BANK, ET - c0)
                last = mm(bank[1 + c0 // BANK][0:1, 0:n], ones_f[0:NT, 0:1], maskT[0:NT, c0:c0 + n], True, True)
            last.then_inc(wt_summed, 1)

            def c_body(i):
                for s in range(8):
                    t = i * 8 + s
                    pe.wait_ge(oh_made, t + 1)
                    pe.wait_ge(row_in[s], i * 16 + 16)
                    if not first(i):
                        pe.wait_ge(acc_added, i * 8 + (s - 7))
                    mm(bank[s][:, :], oh[:, s, :], ring[:, s, :], True, True).then_inc(msg_summed, 1)
            rounds(pe, ET // 8, c_body)
            pe.wait_ge(acc_added, ET)

            pe.wait_ge(b1_in, 16)
            pe.wait_ge(small_in, 16 * 4)
            for m in range(DC):
                last = nc.tensor.transpose(bank[7][:, m * NX:(m + 1) * NX], b1_sb[:, m * P:(m + 1) * P],
                                           ident[0:NX, 0:NX])
            last.then_inc(b1_turned, 1)

            def count(q):
                pe.wait_ge(oha_made, q + 1)
                if not first(q):
                    pe.wait_ge(route_made, q)
                for j in range(2):
                    mm(bank[5][:, 0:TQ * NX], before[:, :], OHA[:, j, :], j == 0, j == 1)
                for j in range(2):
                    last = mm(bank[6][:, 0:TQ * NX], ones_b[:, :], OHA[:, j, :], j == 0, j == 1)
                last.then_inc(pfx_made, 1)

            def gate_body(q):
                def turn_tile(k):
                    t = q * TQ + k
                    pe.wait_ge(xs_made, t + 1)
                    if not (first(q) and k < TG):
                        pe.wait_ge(xsT_made, t - (TG - 1))
                    for m in range(DC):
                        last = turn(bank[k % TG][:, m * P:(m + 1) * P], acc[:, t, m * P:(m + 1) * P])
                    last.then_inc(xs_turned, 1)

                def gate(g):
                    pe.wait_ge(xsT_made, q * TQ + (g + 1) * TG)
                    if not (first(q) and g == 0):
                        pe.wait_ge(lt_made, q * NG + g)
                    for m in range(DC):
                        last = mm(bank[4][0:NX, :], wg_sb[:, m, :], xT4[g % 2][:, m, :], m == 0, m == DC - 1)
                    last.then_inc(gated, 1)

                def back(g):
                    pe.wait_ge(lt_made, q * NG + (g + 1))
                    if g == 0 and not first(q):
                        pe.wait_ge(L_made, q)
                    for c in range(TG):
                        k = g * TG + c
                        last = nc.tensor.transpose(bank[7][:, k * NX:(k + 1) * NX], lt[:, g % 2, c * P:(c + 1) * P],
                                                   ident[0:NX, 0:NX])
                    last.then_inc(turned_back, 1)

                for g in range(NG):
                    for c in range(TG):
                        turn_tile(g * TG + c)
                        if c == 0 and g == 1 and not first(q):
                            count(q - 1)
                        if c == 1 and g > 0:
                            gate(g - 1)
                    if g > 0:
                        back(g - 1)
                gate(NG - 1)
                back(NG - 1)

            for q in range(NQ):
                gate_body(q)
            count(NQ - 1)
            pe.wait_ge(route_made, NQ)
            pe.wait_ge(b1T_made, 1)

            def product(o_, parts):
                n = len(parts)
                for k, (fh, fl, gh, gl) in enumerate(parts):
                    mm(o_, fh, gh, k == 0, False)
                    mm(o_, fh, gl, False, False)
                    last = mm(o_, fl, gh, False, k == n - 1)
                return last

            def turn_rows(i, s, c):
                n = i * 2 * CT + (s * CT + c)
                if c == 0:
                    pe.wait_ge(bin_in[s], i * 16 + 16)
                if not (isinstance(n, int) and n < 2):
                    pe.wait_ge(e_bTl, n - 1)
                for k in range(DC):
                    last = turn(bank[(s * CT + c) % 2][:, k * P:(k + 1) * P], bin_[s][:, c, k * P:(k + 1) * P])
                last.then_inc(e_turned, 1)

            def down(i, s, c):
                w = s % 2
                if c == 0:
                    pe.wait_ge(w2_split, i * 2 * DC + (s + 1) * DC)
                    pe.wait_ge(e_hs, i * 16 + ((s + 1) * 8 - 1))
                if (c + 1) * P > HN:
                    pe.wait_ge(e_hs, i * 16 + (s + 1) * 8)
                n = i * 2 * CT + (s * CT + c)
                if not (isinstance(n, int) and n < 2):
                    pe.wait_ge(e_o, n - 1)
                at = slice(c * P, (c + 1) * P)
                product(bank[6 + (w * CT + c) % 2][:, :],
                        [(hTh[:, k, at], hTl[:, k, at], w2h[:, k, :], w2l[:, k, :])
                         for k in range(DC)]).then_inc(e_down, 1)

            def e_body(i):
                for s in range(2):
                    turn_rows(i, s, 0)
                    turn_rows(i, s, 1)
                    for c in range(CT):
                        if not (first(i) and s == 0):
                            down(i, s - 1, c)
                        if c + 2 < CT:
                            turn_rows(i, s, c + 2)
                    pe.wait_ge(w1_split, i * 2 * DC + (s + 1) * DC)
                    pe.wait_ge(e_bTl, i * 2 * CT + (s + 1) * CT)
                    for g in range(8):
                        hc, hf = g // 2, g % 2
                        n = i * 16 + (s * 8 + g)
                        if not (isinstance(n, int) and n < 4):
                            pe.wait_ge(e_h, n - 3)
                        half = slice(hf * HN, (hf + 1) * HN)
                        cols = slice(hc * P, (hc + 1) * P)
                        product(bank[2 + g % 4][:, 0:HN],
                                [(w1h[:, k, cols], w1l[:, k, cols], bTh[:, k, half],
                                  bTl[:, k, half]) for k in range(DC)]).then_inc(e_up, 1)
            rounds(pe, NX // 2, e_body)
            for c in range(CT):
                down(NX // 2, -1, c)


_INS = ['x', 'src', 'dst', 'edge_weight', 'L0_gnn_weight', 'L0_mix_gamma', 'L0_mix_w_qkv', 'L0_mix_temperature',
        'L0_mix_w_out', 'L0_ffn_Wg', 'L0_ffn_W1', 'L0_ffn_b1', 'L0_ffn_W2', 'L0_ffn_b2']


def kernel(**inputs):
    import numpy as _np
    import concourse.bacc as _bacc
    from concourse import mybir as _mybir
    from concourse.bass_utils import run_bass_kernel_spmd as _run

    nc = _bacc.Bacc("TRN2", target_bir_lowering=False, num_devices=1)
    arrays, args = {}, []
    for name in _INS:
        a = _np.ascontiguousarray(inputs[name])
        arrays[f"in_{name}"] = a
        args.append(nc.dram_tensor(f"in_{name}", a.shape, _mybir.dt.from_np(a.dtype), kind="ExternalInput").ap())
    shape = tuple(inputs['x'].shape)
    args.append(nc.dram_tensor("out_rows", shape, _mybir.dt.float32, kind="ExternalOutput").ap())
    build(nc, *args)
    r = _run(nc, [arrays], core_ids=[0])
    return r.results[0]["out_rows"]
```
